# Optimizing a Trainium2 kernel written in Bass

```python
import numpy as np
import jax
import jax.numpy as jnp

def _softmax(x, axis=-1):
    return jax.nn.softmax(x, axis=axis)

def _gelu(x):
    return jax.nn.gelu(x, approximate=True)

def _silu(x):
    return jax.nn.silu(x)

def _sigmoid(x):
    return jax.nn.sigmoid(x)

def _layernorm(x, axis=-1, eps=1e-05):
    m = jnp.mean(x, axis=axis, keepdims=True)
    v = jnp.var(x, axis=axis, keepdims=True)
    return (x - m) / jnp.sqrt(v + eps)

def _scatter_add(tgt, idx, src, axis=0):
    return tgt.at[idx].add(src)

def _segment_sum(src, seg, n):
    return jax.ops.segment_sum(src, seg, n)
kernel_name = 'mk_adaln_d2_jaxref_r8_cc6af1'

def setup_inputs(seed: int=0):
    np.random.seed(seed)
    _w = jnp.asarray

    def _L0_attn_setup():
        import jax, jax.numpy as jnp
        import numpy as np
        D_MODEL = 128
        N_HEADS = 8
        N_KV_HEADS = 4
        HEAD_DIM = D_MODEL // N_HEADS
        N_REP = N_HEADS // N_KV_HEADS
        WINDOW = 128
        SINKS = 4
        ROPE_BASE = 10000.0
        SCALE = 1.0 / np.sqrt(HEAD_DIM)

        def _trigram_dirs():
            t = np.array([[s0, s1, s2] for s0 in (1.0, -1.0) for s1 in (1.0, -1.0) for s2 in (1.0, -1.0)], dtype=np.float32)
            t = t / np.linalg.norm(t, axis=1, keepdims=True)
            return jnp.asarray(t[:N_HEADS])

        def _rope_tables(T):
            inv_freq = 1.0 / ROPE_BASE ** (jnp.arange(0, HEAD_DIM, 2, dtype=jnp.float32) / HEAD_DIM)
            freqs = jnp.arange(T, dtype=jnp.float32)[:, None] * inv_freq[None, :]
            return (jnp.cos(freqs), jnp.sin(freqs))

        def _apply_rope(t, cos, sin):
            t1, t2 = jnp.split(t, 2, axis=-1)
            c = cos[None, None, :, :]
            s = sin[None, None, :, :]
            return jnp.concatenate([t1 * c - t2 * s, t2 * c + t1 * s], axis=-1)
        key = jax.random.key(seed)
        ks = jax.random.split(key, 6)
        B, T = (2, 256)
        std = 0.02
        x = jax.random.normal(ks[0], (B, T, D_MODEL), jnp.float32)
        Wq = jax.random.normal(ks[1], (D_MODEL, N_HEADS * HEAD_DIM), jnp.float32) * std
        Wk = jax.random.normal(ks[2], (D_MODEL, N_KV_HEADS * HEAD_DIM), jnp.float32) * std
        Wv = jax.random.normal(ks[3], (D_MODEL, N_KV_HEADS * HEAD_DIM), jnp.float32) * std
        Wo = jax.random.normal(ks[4], (D_MODEL, D_MODEL), jnp.float32) * std
        head_scales = jax.random.normal(ks[5], (N_HEADS,), jnp.float32) * 0.1
        head_dirs = _trigram_dirs()
        return {'x': x, 'Wq': Wq, 'Wk': Wk, 'Wv': Wv, 'Wo': Wo, 'head_scales': head_scales, 'head_dirs': head_dirs}
    _L0_attn_in = _L0_attn_setup()

    def _L0_ffn_setup():
        import jax, jax.numpy as jnp
        import numpy as np
        B, S, D = (2, 256, 128)
        H, HKV = (16, 4)
        HD = D // H
        F, E, K = (256, 8, 2)
        THETA = 10000.0
        EPS = 1e-05

        def _rmsnorm(x, w):
            return x * jax.lax.rsqrt(jnp.mean(x * x, axis=-1, keepdims=True) + EPS) * w

        def _rope_cos_sin(seq_len, head_dim, theta):
            inv_freq = 1.0 / theta ** (jnp.arange(0, head_dim, 2, dtype=jnp.float32) / head_dim)
            freqs = jnp.arange(seq_len, dtype=jnp.float32)[:, None] * inv_freq
            return (jnp.cos(freqs), jnp.sin(freqs))

        def _apply_rope(x, cos, sin):
            x1, x2 = jnp.split(x, 2, axis=-1)
            c = cos[None, :, None, :]
            s = sin[None, :, None, :]
            return jnp.concatenate([x1 * c - x2 * s, x2 * c + x1 * s], axis=-1)
        key = jax.random.key(seed)
        ks = jax.random.split(key, 12)
        s = 0.02
        return {'hidden_states': jax.random.normal(ks[0], (B, S, D), jnp.float32), 'ln1_w': 1.0 + 0.1 * jax.random.normal(ks[1], (D,), jnp.float32), 'ln2_w': 1.0 + 0.1 * jax.random.normal(ks[2], (D,), jnp.float32), 'Wq': s * jax.random.normal(ks[3], (D, H * HD), jnp.float32), 'Wk': s * jax.random.normal(ks[4], (D, HKV * HD), jnp.float32), 'Wv': s * jax.random.normal(ks[5], (D, HKV * HD), jnp.float32), 'Wo': s * jax.random.normal(ks[6], (H * HD, D), jnp.float32), 'Wr': s * jax.random.normal(ks[7], (D, E), jnp.float32), 'Wg': s * jax.random.normal(ks[8], (E, D, F), jnp.float32), 'Wu': s * jax.random.normal(ks[9], (E, D, F), jnp.float32), 'Wd': s * jax.random.normal(ks[10], (E, F, D), jnp.float32)}
    _L0_ffn_in = _L0_ffn_setup()
    _L0_c = _w((lambda *s: np.random.randn(*s).astype(np.float32) * 0.05)(16, 128))
    _L0_wmod = _w((lambda *s: np.random.randn(*s).astype(np.float32) * 0.05)(128, 6 * 128) * 128 ** (-0.5))

    def _L1_attn_setup():
        import jax, jax.numpy as jnp
        import numpy as np
        H_DIM = 128
        N_HEADS = 16
        HEAD_DIM = H_DIM // N_HEADS
        MAX_POS = 256
        BASE = 10000.0
        SCALING_FACTOR = 1.0

        def rotate_half(x):
            return jnp.concatenate([-x[..., 1::2], x[..., ::2]], axis=-1)

        def rope_cos_sin(seq_len, dtype):
            base = BASE
            if seq_len > MAX_POS:
                base = BASE * (SCALING_FACTOR * seq_len / MAX_POS - (SCALING_FACTOR - 1.0)) ** (HEAD_DIM / (HEAD_DIM - 2))
            inv_freq = 1.0 / base ** (jnp.arange(0, HEAD_DIM, 2, dtype=jnp.float32) / HEAD_DIM)
            t = jnp.arange(seq_len, dtype=jnp.float32)
            freqs = jnp.einsum('i,j->ij', t, inv_freq)
            emb = jnp.concatenate([freqs, freqs], axis=-1)
            return (emb.astype(dtype), jnp.cos(emb).astype(dtype), jnp.sin(emb).astype(dtype))
        key = jax.random.key(seed)
        ks = jax.random.split(key, 5)
        B, S = (1, 512)
        scale_w = 0.02
        return {'hidden_states': jax.random.normal(ks[0], (B, S, H_DIM), dtype=jnp.float32), 'Wq': jax.random.normal(ks[1], (H_DIM, H_DIM), dtype=jnp.float32) * scale_w, 'Wk': jax.random.normal(ks[2], (H_DIM, H_DIM), dtype=jnp.float32) * scale_w, 'Wv': jax.random.normal(ks[3], (H_DIM, H_DIM), dtype=jnp.float32) * scale_w, 'Wo': jax.random.normal(ks[4], (H_DIM, H_DIM), dtype=jnp.float32) * scale_w}
    _L1_attn_in = _L1_attn_setup()

    def _L1_ffn_setup():
        import math
        import jax, jax.numpy as jnp
        import numpy as np
        B, S, D, F, E = (8, 256, 128, 512, 8)
        CAPACITY_FACTOR = 1.0
        key = jax.random.key(seed)
        k1, k2, k3, k4 = jax.random.split(key, 4)
        x = jax.random.normal(k1, (B, S, D), dtype=jnp.float32)
        Wr = jax.random.normal(k2, (D, E), dtype=jnp.float32) * (1.0 / math.sqrt(D))
        W1 = jax.random.normal(k3, (E, D, F), dtype=jnp.float32) * (1.0 / math.sqrt(D))
        W2 = jax.random.normal(k4, (E, F, D), dtype=jnp.float32) * (1.0 / math.sqrt(F))
        return {'x': x, 'Wr': Wr, 'W1': W1, 'W2': W2}
    _L1_ffn_in = _L1_ffn_setup()
    _L1_c = _w((lambda *s: np.random.randn(*s).astype(np.float32) * 0.05)(16, 128))
    _L1_wmod = _w((lambda *s: np.random.randn(*s).astype(np.float32) * 0.05)(128, 6 * 128) * 128 ** (-0.5))
    _d = {'L0_attn_x': _L0_attn_in['x'], 'L0_attn_Wq': _L0_attn_in['Wq'], 'L0_attn_Wk': _L0_attn_in['Wk'], 'L0_attn_Wv': _L0_attn_in['Wv'], 'L0_attn_Wo': _L0_attn_in['Wo'], 'L0_attn_head_scales': _L0_attn_in['head_scales'], 'L0_attn_head_dirs': _L0_attn_in['head_dirs'], 'L0_ffn_ln1_w': _L0_ffn_in['ln1_w'], 'L0_ffn_ln2_w': _L0_ffn_in['ln2_w'], 'L0_ffn_Wq': _L0_ffn_in['Wq'], 'L0_ffn_Wk': _L0_ffn_in['Wk'], 'L0_ffn_Wv': _L0_ffn_in['Wv'], 'L0_ffn_Wo': _L0_ffn_in['Wo'], 'L0_ffn_Wr': _L0_ffn_in['Wr'], 'L0_ffn_Wg': _L0_ffn_in['Wg'], 'L0_ffn_Wu': _L0_ffn_in['Wu'], 'L0_ffn_Wd': _L0_ffn_in['Wd'], 'L0_c': _L0_c, 'L0_wmod': _L0_wmod, 'L1_attn_Wq': _L1_attn_in['Wq'], 'L1_attn_Wk': _L1_attn_in['Wk'], 'L1_attn_Wv': _L1_attn_in['Wv'], 'L1_attn_Wo': _L1_attn_in['Wo'], 'L1_ffn_Wr': _L1_ffn_in['Wr'], 'L1_ffn_W1': _L1_ffn_in['W1'], 'L1_ffn_W2': _L1_ffn_in['W2'], 'L1_c': _L1_c, 'L1_wmod': _L1_wmod}
    _x0 = _d['L0_attn_x']
    _d['L0_attn_x'] = jax.random.normal(jax.random.fold_in(jax.random.key(seed), 1), (16, 256, 128), dtype=_x0.dtype)
    del _x0
    return _d

def reference(L0_attn_x, L0_attn_Wq, L0_attn_Wk, L0_attn_Wv, L0_attn_Wo, L0_attn_head_scales, L0_attn_head_dirs, L0_ffn_ln1_w, L0_ffn_ln2_w, L0_ffn_Wq, L0_ffn_Wk, L0_ffn_Wv, L0_ffn_Wo, L0_ffn_Wr, L0_ffn_Wg, L0_ffn_Wu, L0_ffn_Wd, L0_c, L0_wmod, L1_attn_Wq, L1_attn_Wk, L1_attn_Wv, L1_attn_Wo, L1_ffn_Wr, L1_ffn_W1, L1_ffn_W2, L1_c, L1_wmod):

    def _L0_attn_ref(x, Wq, Wk, Wv, Wo, head_scales, head_dirs):
        import jax, jax.numpy as jnp
        import numpy as np
        D_MODEL = 128
        N_HEADS = 8
        N_KV_HEADS = 4
        HEAD_DIM = D_MODEL // N_HEADS
        N_REP = N_HEADS // N_KV_HEADS
        WINDOW = 128
        SINKS = 4
        ROPE_BASE = 10000.0
        SCALE = 1.0 / np.sqrt(HEAD_DIM)

        def _trigram_dirs():
            t = np.array([[s0, s1, s2] for s0 in (1.0, -1.0) for s1 in (1.0, -1.0) for s2 in (1.0, -1.0)], dtype=np.float32)
            t = t / np.linalg.norm(t, axis=1, keepdims=True)
            return jnp.asarray(t[:N_HEADS])

        def _rope_tables(T):
            inv_freq = 1.0 / ROPE_BASE ** (jnp.arange(0, HEAD_DIM, 2, dtype=jnp.float32) / HEAD_DIM)
            freqs = jnp.arange(T, dtype=jnp.float32)[:, None] * inv_freq[None, :]
            return (jnp.cos(freqs), jnp.sin(freqs))

        def _apply_rope(t, cos, sin):
            t1, t2 = jnp.split(t, 2, axis=-1)
            c = cos[None, None, :, :]
            s = sin[None, None, :, :]
            return jnp.concatenate([t1 * c - t2 * s, t2 * c + t1 * s], axis=-1)
        B, T, C = x.shape
        q = (x @ Wq).reshape(B, T, N_HEADS, HEAD_DIM).transpose(0, 2, 1, 3)
        k = (x @ Wk).reshape(B, T, N_KV_HEADS, HEAD_DIM).transpose(0, 2, 1, 3)
        v = (x @ Wv).reshape(B, T, N_KV_HEADS, HEAD_DIM).transpose(0, 2, 1, 3)
        cos, sin = _rope_tables(T)
        q = _apply_rope(q, cos, sin)
        k = _apply_rope(k, cos, sin)
        k = jnp.repeat(k, N_REP, axis=1)
        v = jnp.repeat(v, N_REP, axis=1)
        scores = jnp.einsum('bhtd,bhsd->bhts', q, k) * SCALE
        qp = jnp.einsum('bhtd,hd->bht', q[..., :3], head_dirs)
        kp = jnp.einsum('bhsd,hd->bhs', k[..., :3], head_dirs)
        scores = scores + head_scales[None, :, None, None] * (qp[..., :, None] * kp[..., None, :])
        i = jnp.arange(T)[:, None]
        j = jnp.arange(T)[None, :]
        allowed = (j <= i) & ((j < SINKS) | (j >= i - WINDOW + 1))
        scores = jnp.where(allowed[None, None, :, :], scores, -jnp.inf)
        attn = jax.nn.softmax(scores, axis=-1)
        out = jnp.einsum('bhts,bhsd->bhtd', attn, v)
        out = out.transpose(0, 2, 1, 3).reshape(B, T, C)
        return out @ Wo

    def _L0_ffn_ref(hidden_states, ln1_w, ln2_w, Wq, Wk, Wv, Wo, Wr, Wg, Wu, Wd):
        import jax, jax.numpy as jnp
        import numpy as np
        B, S, D = (2, 256, 128)
        H, HKV = (16, 4)
        HD = D // H
        F, E, K = (256, 8, 2)
        THETA = 10000.0
        EPS = 1e-05

        def _rmsnorm(x, w):
            return x * jax.lax.rsqrt(jnp.mean(x * x, axis=-1, keepdims=True) + EPS) * w

        def _rope_cos_sin(seq_len, head_dim, theta):
            inv_freq = 1.0 / theta ** (jnp.arange(0, head_dim, 2, dtype=jnp.float32) / head_dim)
            freqs = jnp.arange(seq_len, dtype=jnp.float32)[:, None] * inv_freq
            return (jnp.cos(freqs), jnp.sin(freqs))

        def _apply_rope(x, cos, sin):
            x1, x2 = jnp.split(x, 2, axis=-1)
            c = cos[None, :, None, :]
            s = sin[None, :, None, :]
            return jnp.concatenate([x1 * c - x2 * s, x2 * c + x1 * s], axis=-1)
        b, s, d = hidden_states.shape
        residual = hidden_states
        h = _rmsnorm(hidden_states, ln1_w)
        q = (h @ Wq).reshape(b, s, H, HD)
        k = (h @ Wk).reshape(b, s, HKV, HD)
        v = (h @ Wv).reshape(b, s, HKV, HD)
        cos, sin = _rope_cos_sin(s, HD, THETA)
        q = _apply_rope(q, cos, sin)
        k = _apply_rope(k, cos, sin)
        rep = H // HKV
        k = jnp.repeat(k, rep, axis=2)
        v = jnp.repeat(v, rep, axis=2)
        scores = jnp.einsum('bqhd,bkhd->bhqk', q, k) / np.sqrt(HD).astype(np.float32)
        causal = jnp.tril(jnp.ones((s, s), dtype=bool))
        scores = jnp.where(causal[None, None], scores, jnp.finfo(scores.dtype).min)
        attn = jax.nn.softmax(scores, axis=-1)
        ctx = jnp.einsum('bhqk,bkhd->bqhd', attn, v).reshape(b, s, H * HD)
        attn_out = ctx @ Wo
        h = jnp.clip(residual + attn_out, -100.0, 100.0)
        residual = h
        hn = _rmsnorm(h, ln2_w)
        flat = hn.reshape(b * s, d)
        logits = flat @ Wr
        probs = jax.nn.softmax(logits, axis=-1)
        topv, topi = jax.lax.top_k(probs, K)
        topv = topv / jnp.sum(topv, axis=-1, keepdims=True)
        w = jnp.sum(jax.nn.one_hot(topi, E, dtype=flat.dtype) * topv[..., None], axis=1)
        g = jnp.einsum('td,edf->etf', flat, Wg)
        u = jnp.einsum('td,edf->etf', flat, Wu)
        a = jax.nn.silu(g) * u
        o = jnp.einsum('etf,efd->etd', a, Wd)
        moe_out = jnp.einsum('te,etd->td', w, o).reshape(b, s, d)
        out = jnp.clip(residual + moe_out, -100.0, 100.0)
        return out

    def _L1_attn_ref(hidden_states, Wq, Wk, Wv, Wo):
        import jax, jax.numpy as jnp
        import numpy as np
        H_DIM = 128
        N_HEADS = 16
        HEAD_DIM = H_DIM // N_HEADS
        MAX_POS = 256
        BASE = 10000.0
        SCALING_FACTOR = 1.0

        def rotate_half(x):
            return jnp.concatenate([-x[..., 1::2], x[..., ::2]], axis=-1)

        def rope_cos_sin(seq_len, dtype):
            base = BASE
            if seq_len > MAX_POS:
                base = BASE * (SCALING_FACTOR * seq_len / MAX_POS - (SCALING_FACTOR - 1.0)) ** (HEAD_DIM / (HEAD_DIM - 2))
            inv_freq = 1.0 / base ** (jnp.arange(0, HEAD_DIM, 2, dtype=jnp.float32) / HEAD_DIM)
            t = jnp.arange(seq_len, dtype=jnp.float32)
            freqs = jnp.einsum('i,j->ij', t, inv_freq)
            emb = jnp.concatenate([freqs, freqs], axis=-1)
            return (emb.astype(dtype), jnp.cos(emb).astype(dtype), jnp.sin(emb).astype(dtype))
        B, S, H = hidden_states.shape

        def proj(x, W):
            y = jnp.einsum('bsh,oh->bso', x, W)
            return y.reshape(B, S, N_HEADS, HEAD_DIM).transpose(0, 2, 1, 3)
        q = proj(hidden_states, Wq)
        k = proj(hidden_states, Wk)
        v = proj(hidden_states, Wv)
        _, cos, sin = rope_cos_sin(S, hidden_states.dtype)
        cos = cos[None, None, :, :]
        sin = sin[None, None, :, :]
        q = q * cos + rotate_half(q) * sin
        k = k * cos + rotate_half(k) * sin
        scale = HEAD_DIM ** (-0.5)
        attn = jnp.einsum('bhsd,bhtd->bhst', q, k) / scale
        attn = jax.nn.softmax(attn, axis=-1)
        out = jnp.einsum('bhst,bhtd->bhsd', attn, v)
        out = out.transpose(0, 2, 1, 3).reshape(B, S, H)
        return jnp.einsum('bsh,oh->bso', out, Wo)

    def _L1_ffn_ref(x, Wr, W1, W2):
        import math
        import jax, jax.numpy as jnp
        import numpy as np
        B, S, D, F, E = (8, 256, 128, 512, 8)
        CAPACITY_FACTOR = 1.0
        b, s, d = x.shape
        t = b * s
        cap = max(math.ceil(t * CAPACITY_FACTOR / E), 1)
        xf = x.reshape(t, d)
        probs = jax.nn.softmax(xf.astype(jnp.float32) @ Wr, axis=-1)
        eidx = jnp.argmax(probs, axis=-1)
        p_tok = jnp.take_along_axis(probs, eidx[:, None], axis=1)[:, 0]
        onehot = jax.nn.one_hot(eidx, E, dtype=jnp.int32)
        rank_all = jnp.cumsum(onehot, axis=0) - onehot
        rank = jnp.take_along_axis(rank_all, eidx[:, None], axis=1)[:, 0]
        keep = rank < cap
        slot = jnp.where(keep, rank, cap)
        dispatch = jnp.zeros((E, cap + 1), dtype=jnp.int32).at[eidx, slot].set(jnp.arange(t, dtype=jnp.int32))
        valid = jnp.zeros((E, cap + 1), dtype=bool).at[eidx, slot].set(keep)
        dispatch = dispatch[:, :cap]
        valid = valid[:, :cap]
        xe = xf[dispatch]
        h = jnp.maximum(jnp.einsum('ecd,edf->ecf', xe, W1), 0.0)
        ye = jnp.einsum('ecf,efd->ecd', h, W2)
        pe = p_tok[dispatch]
        ye = ye * (pe * valid.astype(ye.dtype))[:, :, None]
        y = jnp.zeros((t, d), dtype=x.dtype).at[dispatch.reshape(-1)].add(ye.reshape(E * cap, d).astype(x.dtype))
        return y.reshape(b, s, d)
    x = L0_attn_x
    mod = (_silu(L0_c) @ L0_wmod).reshape(L0_c.shape[0], 6, 1, -1)
    sa, ca, ga, sb, cb, gb = (mod[:, 0], mod[:, 1], mod[:, 2], mod[:, 3], mod[:, 4], mod[:, 5])
    ga = (2 * (ga >= 0) - 1) * jnp.maximum(jnp.abs(ga), 0.25)
    gb = (2 * (gb >= 0) - 1) * jnp.maximum(jnp.abs(gb), 0.25)
    h = _layernorm(x, axis=-1) * (1 + ca) + sa
    x = x + ga * _L0_attn_ref(h, L0_attn_Wq, L0_attn_Wk, L0_attn_Wv, L0_attn_Wo, L0_attn_head_scales, L0_attn_head_dirs)
    h = _layernorm(x, axis=-1) * (1 + cb) + sb
    x = x + gb * _L0_ffn_ref(h, L0_ffn_ln1_w, L0_ffn_ln2_w, L0_ffn_Wq, L0_ffn_Wk, L0_ffn_Wv, L0_ffn_Wo, L0_ffn_Wr, L0_ffn_Wg, L0_ffn_Wu, L0_ffn_Wd)
    mod = (_silu(L1_c) @ L1_wmod).reshape(L1_c.shape[0], 6, 1, -1)
    sa, ca, ga, sb, cb, gb = (mod[:, 0], mod[:, 1], mod[:, 2], mod[:, 3], mod[:, 4], mod[:, 5])
    ga = (2 * (ga >= 0) - 1) * jnp.maximum(jnp.abs(ga), 0.25)
    gb = (2 * (gb >= 0) - 1) * jnp.maximum(jnp.abs(gb), 0.25)
    h = _layernorm(x, axis=-1) * (1 + ca) + sa
    x = x + ga * _L1_attn_ref(h, L1_attn_Wq, L1_attn_Wk, L1_attn_Wv, L1_attn_Wo)
    h = _layernorm(x, axis=-1) * (1 + cb) + sb
    x = x + gb * _L1_ffn_ref(h, L1_ffn_Wr, L1_ffn_W1, L1_ffn_W2)
    return x

_drawn_inputs = setup_inputs


def setup_inputs(seed=0):
    import zlib

    import numpy as np

    out = dict(_drawn_inputs(seed))
    spreads = {}
    factors = {'L0_attn_Wq': 8.0,
     'L0_attn_Wk': 8.0,
     'L0_attn_Wv': 8.0,
     'L0_attn_Wo': 8.0,
     'L0_attn_head_scales': 8.0,
     'L0_attn_head_dirs': 8.0,
     'L0_ffn_ln1_w': 8.0,
     'L0_ffn_ln2_w': 8.0,
     'L0_ffn_Wq': 8.0,
     'L0_ffn_Wk': 8.0,
     'L0_ffn_Wv': 8.0,
     'L0_ffn_Wo': 8.0,
     'L0_ffn_Wr': 8.0,
     'L0_ffn_Wg': 8.0,
     'L0_ffn_Wu': 8.0,
     'L0_ffn_Wd': 8.0,
     'L1_attn_Wq': 8.0,
     'L1_attn_Wk': 8.0,
     'L1_attn_Wv': 8.0,
     'L1_attn_Wo': 8.0,
     'L1_ffn_Wr': 8.0,
     'L1_ffn_W1': 8.0,
     'L1_ffn_W2': 8.0}
    for name, (base, spread) in spreads.items():
        noise = np.random.default_rng([zlib.crc32(name.encode()), seed]).standard_normal(out[name].shape)
        drawn = base * np.exp(spread * noise) if base else spread * noise
        out[name] = jnp.asarray(drawn.astype(out[name].dtype))
    for name, factor in factors.items():
        out[name] = (out[name] * factor).astype(out[name].dtype)
    return out
```

```python
from contextlib import ExitStack

import numpy as np

import concourse.bass as bass
from concourse import mybir

ALU = mybir.AluOpType
ACT = mybir.ActivationFunctionType
F32 = mybir.dt.float32
F32R = mybir.dt.float32r
BF16 = mybir.dt.bfloat16
I32 = mybir.dt.int32
AX_X = mybir.AxisListType.X

P = 128
D = 128
S = 256
NB = 16
BLK = S // P
TOKENS = NB * S
LN_EPS = 1e-5
MASKED = -1e30
CLIP = 100.0
RSQRT_D = float(D) ** -0.5

E0, F0 = 8, 256
E1, F1 = 8, 512
CAP = TOKENS // E1

RING = 4


class Attn:

    def __init__(self, index, layer, mod, heads, kv, causal, window, scale):
        self.index = index
        self.layer = layer
        self.mod = mod
        self.heads = heads
        self.hd = D // heads
        self.kv = kv
        self.causal = causal
        self.window = window
        self.scale = scale
        self.strip = 32 if self.hd == 8 else 64
        self.per_group = P // self.strip
        self.krows = 3 * self.hd
        self.pairs = heads // 2
        self.first = NB * index

    def q_cols(self):
        return 384 if self.causal else 512


CFGS = [
    Attn(0, 0, 0, 8, 4, True, True, 1.0),
    Attn(1, 0, 3 * D, 16, 4, True, False, float(1.0 / np.sqrt(np.float32(8.0)))),
    Attn(2, 1, 0, 16, 16, False, False, float(np.sqrt(8.0))),
]
GROUPS = 4
HEADS_BEFORE = [0, NB * 8, NB * 24]
PAIRS_BEFORE = [0, NB * 4, NB * 12]


def rope_tables():
    out = []
    for hd in (16, 8):
        inv = (1.0 / np.float32(10000.0) ** (np.arange(0, hd, 2, dtype=np.float32) / np.float32(hd))).astype(np.float32)
        f = (np.arange(S, dtype=np.float32)[:, None] * inv[None, :]).astype(np.float32)
        c, s = np.cos(f).T, np.sin(f).T
        out.append(np.tile(np.concatenate([c, c]), (D // hd, 1)))
        out.append(np.tile(np.concatenate([-s, s]), (D // hd, 1)))
    return np.stack(out, 1).astype(np.float32)


def square_constants():
    a = np.arange(P)
    row, col = a[:, None], a[None, :]
    causal = np.where(col > row, MASKED, 0.0)
    window = np.where((col < 4) | (col >= row + 1), 0.0, MASKED)
    return np.stack([np.eye(P), causal, window, causal.T, window.T, row < col, np.ones((P, P))], 1).astype(np.float32)


def select_constants():
    out = np.zeros((P, 3, 4, GROUPS, P), np.float32)
    for c in CFGS:
        for g in range(GROUPS):
            for j in range(c.per_group):
                head = g * c.per_group + j
                kv = head // (c.heads // c.kv)
                for d in range(c.hd):
                    for slot, (qp, kp) in enumerate(((0, 0), (0, 1), (1, 0))):
                        row = j * c.strip + slot * c.hd + d
                        out[head * c.hd + d, c.index, qp, g, row] = 1.0
                        out[kv * c.hd + d, c.index, 2 + kp, g, row] = 1.0
    return out


def max_select_constant():
    out = np.zeros((P, 16, P), np.float32)
    for h in range(16):
        out[h, h, :] = -1.0
        out[32 + h, h, :] = -1.0
    return out


def expert_constants():
    out = np.zeros((P, 6, 8), np.float32)
    out[:, 0] = 8 - np.arange(8)
    out[:, 1] = CAP * np.arange(8)
    out[:, 2:] = (TOKENS + P * np.arange(NB * BLK)[None, :] + np.arange(P)[:, None]).reshape(P, 4, 8)
    return out


def adaln_two_layers(nc, a, out):
    with ExitStack() as ctx:
        def sb(name, shape, dt=F32):
            return ctx.enter_context(nc.sbuf_tensor(name, shape, dt))

        def psum(name, shape, dt=F32):
            return ctx.enter_context(nc.psum_tensor(name, shape, dt))

        def sem(name):
            return ctx.enter_context(nc.semaphore(name))

        ps_max = psum("ps_max", [P, 2, 512])
        ps_exp = psum("ps_exp", [P, 2, 2, 512])
        ps_out = psum("ps_out", [P, 512])
        ps_work = psum("ps_work", [P, 512])

        x_all = sb("x_all", [P, NB * BLK, D])
        res_all = sb("res_all", [P, NB * BLK, D])
        squares = sb("squares", [P, 7, P])
        ident = squares[:, 0, :]
        ident_bf = sb("ident_bf", [P, P], BF16)
        masks = sb("masks", [P, 4, P], BF16)
        upper_ones = sb("upper_ones", [P, 2, P], BF16)
        rope = sb("rope", [P, 4, S])
        select = sb("select", [P, 4, GROUPS, P], F32R)
        max_select = sb("max_select", [P, 16, P], F32R)
        expert_c = sb("expert_c", [P, 6, 8])
        half_neg = sb("half_neg", [P, 2])
        eps = sb("eps", [P, 2])
        one = sb("one", [P, 1])
        ln_w = sb("ln_w", [P, 2])
        silu_c = sb("silu_c", [P, 2, NB])
        c_rows = sb("c_rows", [NB, 2, D])
        wmod = sb("wmod", [P, 2, 6 * D])
        wq = sb("wq", [P, 3, 2, D])
        wk = sb("wk", [P, 3, 2, D])
        wv = sb("wv", [P, 3, D])
        wo = sb("wo", [P, 3, D])
        dirs = sb("dirs", [8, 4])
        dir_rows = sb("dir_rows", [8, 2, D])
        dir_mix = sb("dir_mix", [P, D])
        wr = sb("wr", [P, 2, 8])
        wgu = sb("wgu", [P, 2, E0, F0])
        wg, wu = wgu[:, 0], wgu[:, 1]
        wd = sb("wd", [P, E0, F0 // P, D])

        c_bcast = sb("c_bcast", [P, 2, P])
        mod = sb("mod", [P, RING, 3, D])
        gate_tmp = sb("gate_tmp", [P, 2, D])
        stats6 = sb("stats6", [P, 2, BLK, 6])
        mean_var = sb("mean_var", [P, 2, BLK, 2])
        var_eps = sb("var_eps", [P, 2, BLK])
        rstd = sb("rstd", [P, 2, BLK])
        h_tok = sb("h_tok", [P, RING, BLK, D])
        sq_junk = sb("sq_junk", [P, BLK, D])
        ssq = sb("ssq", [P, 2, BLK])
        ssq_eps = sb("ssq_eps", [P, 2, BLK])
        rrms = sb("rrms", [P, 2, BLK])
        hn_tok = sb("hn_tok", [P, 2, BLK, D])
        h_t = sb("h_t", [P, 2, S])
        rope_ab = sb("rope_ab", [P, 2, 2, S])
        rope_a, rope_b = rope_ab[:, 0], rope_ab[:, 1]
        roped = sb("roped", [P, 2, S])
        split = sb("split", [P, 2, 2, S], F32R)
        q_st = sb("q_st", [P, RING, GROUPS, S], F32R)
        k_st = sb("k_st", [P, RING, GROUPS, S], F32R)
        v_tok = [sb(f"v_tok{c.index}", [P, RING, BLK, c.kv, c.hd + 1]) for c in CFGS]
        row_max = sb("row_max", [P, 2, 3, 16])
        max_t = sb("max_t", [P, 2, S], F32R)
        probs = sb("probs", [P, 4, 2, 512])
        recip = sb("recip", [P, 2, BLK * 16])
        o_both = sb("o_both", [P, 2, 2, S])
        o_tok = o_both[:, 0].rearrange("p a (k d) -> p a k d", d=D)
        o_t = o_both[:, 1]
        y_tok = sb("y_tok", [P, 2, BLK, D])

        zeros = probs[:, 0, 0, :]

        ht_all = probs[:].rearrange("p a b c -> p (a b c)")
        gates_all = sb("gates_all", [P, NB, D])
        stage = gates_all[:].rearrange("p b d -> p (b d)")
        logits = sb("logits", [P, NB * BLK, 8])
        rt = mod[:].rearrange("p r a d -> p (r a d)").rearrange("p (n k e) -> p n k e", n=6, e=8)
        rt1 = sb("rt1", [P, 12, NB * BLK])
        one_hot = sb("one_hot", [P, NB * BLK, 8], BF16)
        slot_put = sb("slot_put", [P, NB * BLK], I32)
        slot_get = sb("slot_get", [P, NB * BLK], I32)
        weight_t = sb("weight_t", [P, 4, 8])
        tanh_g = h_tok[:].rearrange("p a b c -> p (a b c)").rearrange("p (s t) -> p s t", s=2)
        gated = rope_ab[:].rearrange("p a b c -> p (a b c)").rearrange("p (s t) -> p s t", s=2)
        act_t = o_both[:].rearrange("p a b c -> p (a b c)").rearrange("p (s t) -> p s t", s=2)
        acc = y_tok[:].rearrange("p a k d -> p (a k) d")
        moe_y = sb("moe_y", [P, 2, 4, D])
        w12 = wd[:].rearrange("p e c d -> p (e c d)")
        w1 = w12[:, 0:2 * F1].rearrange("p (s f) -> p s f", s=2)
        w2 = w12[:, 2 * F1:].rearrange("p (s f d) -> p s f d", s=2, f=F1 // P)
        rows_e = tanh_g.rearrange("p s (k d) -> p s k d", d=D)
        rows_t = gated
        hid_t = wgu[:].rearrange("p a e f -> p (a e f)").rearrange("p (s f t) -> p s f t", s=2, f=F1 // P)
        y_rows = act_t.rearrange("p s (k d) -> p s k d", d=D)
        y_all = probs[:].rearrange("p a b (c d) -> p (a b c) d", d=D)
        slots_dram = nc.dram_tensor("slots_dram", [2 * TOKENS, D], F32, kind="Internal").ap()
        y_dram = nc.dram_tensor("y_dram", [TOKENS, D], F32, kind="Internal").ap()

        loads = sem("loads")
        x_load = sem("x_load")
        sel_load = sem("sel_load")
        select_ready = sem("select_ready")
        zeros_ready = sem("zeros_ready")
        ones_ready = sem("ones_ready")
        folded = sem("folded")
        rotated = sem("rotated")
        zero_store = sem("zero_store")
        pro_dve = sem("pro_dve")
        pro_pe = sem("pro_pe")
        pro_act = sem("pro_act")
        x_done = sem("x_done")
        res_done = sem("res_done")
        c_bcast_done = sem("c_bcast_done")
        mod_mm = sem("mod_mm")
        mod_out = sem("mod_out")
        mod_scale = sem("mod_scale")
        gate_a = sem("gate_a")
        gate_b = sem("gate_b")
        gate_done = sem("gate_done")
        stats_done = sem("stats_done")
        mv_done = sem("mv_done")
        var_done = sem("var_done")
        rstd_done = sem("rstd_done")
        xhat_done = sem("xhat_done")
        h_mul = sem("h_mul")
        h_done = sem("h_done")
        ssq_done = sem("ssq_done")
        ssq_eps_done = sem("ssq_eps_done")
        rrms_done = sem("rrms_done")
        hn_done = sem("hn_done")
        ht_mm = sem("ht_mm")
        ht_out = sem("ht_out")
        q_mm = sem("q_mm")
        q_rope = sem("q_rope")
        q_sum = sem("q_sum")
        qd_mm = sem("qd_mm")
        q_hi = sem("q_hi")
        q_lo = sem("q_lo")
        k_mm = sem("k_mm")
        k_rope = sem("k_rope")
        k_sum = sem("k_sum")
        k_lo = sem("k_lo")
        v_mm = sem("v_mm")
        v_out = sem("v_out")
        sel_mm = sem("sel_mm")
        sel_out = sem("sel_out")
        max_mm = sem("max_mm")
        max_done = sem("max_done")
        max_all = sem("max_all")
        mt_mm = sem("mt_mm")
        mt_hi = sem("mt_hi")
        mt_out = sem("mt_out")
        exp_mm = sem("exp_mm")
        exp_done = sem("exp_done")
        pv_pair = sem("pv_pair")
        recip_done = sem("recip_done")
        o_done = sem("o_done")
        ot_mm = sem("ot_mm")
        ot_out = sem("ot_out")
        y_mm = sem("y_mm")
        y_out = sem("y_out")  

        moe_done = sem("moe_done")
        rt_bcast = sem("rt_bcast")
        rt_mod_mm = sem("rt_mod_mm")
        rt_mod_out = sem("rt_mod_out")
        rt_mod_scale = sem("rt_mod_scale")
        rt_gate_a = sem("rt_gate_a")
        rt_gate_b = sem("rt_gate_b")
        rt_gate = sem("rt_gate")
        rt_stats = sem("rt_stats")
        rt_mv = sem("rt_mv")
        rt_var = sem("rt_var")
        rt_rstd = sem("rt_rstd")
        rt_xhat = sem("rt_xhat")
        rt_mul = sem("rt_mul")
        rt_h = sem("rt_h")
        rt_kept = sem("rt_kept")
        rt_ssq = sem("rt_ssq")
        rt_ht_mm = sem("rt_ht_mm")
        rt_ht_out = sem("rt_ht_out")
        rt_logit_mm = sem("rt_logit_mm")
        rt_logit = sem("rt_logit")
        rt_chain = sem("rt_chain")
        rt_diff = sem("rt_diff")
        rt_exp = sem("rt_exp")
        rt_onehot = sem("rt_onehot")
        rt_rank_mm = sem("rt_rank_mm")
        routed = sem("routed")
        gu_mm = sem("gu_mm")
        tanh_done = sem("tanh_done")
        gated_done = sem("gated_done")
        act_done = sem("act_done")
        down_mm = sem("down_mm")
        weight_done = sem("weight_done")
        acc_done = sem("acc_done")
        moe_sum = sem("moe_sum")
        moe_clip = sem("moe_clip")
        moe_gated = sem("moe_gated")
        scattered = sem("scattered")
        ffn_load = [sem("ffn_load0"), sem("ffn_load1")]
        xt_mm = sem("xt_mm")
        xt_out = sem("xt_out")
        up_mm = sem("up_mm")
        relu_done = sem("relu_done")
        ffn_mm = sem("ffn_mm")
        ffn_out = sem("ffn_out")
        ffn_store = [sem("ffn_store0"), sem("ffn_store1")]
        gathered = sem("gathered")
        y_gated = sem("y_gated")
        final_done = sem("final_done")
        out_store = sem("out_store")

        X = a["L0_attn_x"].rearrange("b (k p) d -> p (b k) d", p=P)
        OUT = out.rearrange("b (k p) d -> p (b k) d", p=P)
        dma_list = [
            (squares[:], a["squares"]), (rope[:], a["rope"]), (expert_c[:], a["experts"]),
            (c_rows[:, 0, :], a["L0_c"]), (c_rows[:, 1, :], a["L1_c"]),
            (wmod[:, 0, :], a["L0_wmod"]), (wmod[:, 1, :], a["L1_wmod"]),
            (wq[:, 0, 0, :], a["L0_attn_Wq"]), (wk[:, 0, 0, 0:64], a["L0_attn_Wk"]),
            (wv[:, 0, 0:64], a["L0_attn_Wv"]), (wo[:, 0, :], a["L0_attn_Wo"]),
            (dirs[:, 0:3], a["L0_attn_head_dirs"]),
            (dirs[:, 3:4], a["L0_attn_head_scales"].rearrange("(h o) -> h o", o=1)),
            (wq[:, 1, 0, :], a["L0_ffn_Wq"]), (wk[:, 1, 0, 0:32], a["L0_ffn_Wk"]),
            (wv[:, 1, 0:32], a["L0_ffn_Wv"]), (wo[:, 1, :], a["L0_ffn_Wo"]),
            (ln_w[:, 0:1], a["L0_ffn_ln1_w"].rearrange("(h o) -> h o", o=1)),
            (ln_w[:, 1:2], a["L0_ffn_ln2_w"].rearrange("(h o) -> h o", o=1)),
            (wq[:, 2, 0, :], a["L1_attn_WqT"]), (wk[:, 2, 0, :], a["L1_attn_WkT"]),
            (wv[:, 2, :], a["L1_attn_WvT"]), (wo[:, 2, :], a["L1_attn_WoT"]),
            (wr[:, 0, :], a["L0_ffn_Wr"]), (wr[:, 1, :], a["L1_ffn_Wr"]),
            (wg, a["L0_ffn_Wg"].rearrange("e d f -> d e f")),
            (wu, a["L0_ffn_Wu"].rearrange("e d f -> d e f")),
            (wd[:], a["L0_ffn_Wd"].rearrange("e (c p) d -> p e c d", p=P)),
        ]
        N_LOADS = len(dma_list)

        def n_of(c, b):
            return b + c.first

        SLOT_STEPS = ["mod", "ht", "q", "qd", "k", "v", "sel0", "sel1", "sel2", "sel3"]

        def slots(c, with_post, with_prep):
            names = ["ot", "y"] if with_post else []
            if with_prep:
                names = names + [n for n in SLOT_STEPS if n != "qd" or c.index == 0]
            table = [[] for _ in range(c.heads)]
            for j, name in enumerate(names):
                table[1 + j * (c.heads - 2) // max(len(names), 1)].append(name)
            return table

        def at_least(eng, semaphore, value):
            if not isinstance(value, int) or value > 0:
                eng.wait_ge(semaphore, value)

        def n_of(c, b):
            return b + c.first

        def pairs_until(c, b):
            if isinstance(b, int) and b < 0:
                return PAIRS_BEFORE[c.index]
            return (b + 1) * c.pairs + PAIRS_BEFORE[c.index]

        def run(eng, c, start, segment, finish):
            start(c)
            segment(c, 0, 0)
            with eng.Fori(0, (NB - RING) // RING) as g:
                for r in range(RING):
                    segment(c, g * RING + (1 + r), (1 + r) % RING)
            for b in range(NB - RING + 1, NB):
                segment(c, b, b % RING)
            finish(c)

        def flags(b):
            if not isinstance(b, int):
                return True, True, True
            return b > 0, b + 2 < NB, b + 1 < NB

        block = ctx.enter_context(nc.Block())

        def block_of(x, i):
            return x[:, bass.ds(i, 1), :].rearrange("p o d -> p (o d)")

        def entries(eng, f):
            for b in range(2):
                f(b, b)
            with eng.Fori(0, NB // 2 - 1) as g:
                for r in range(2):
                    f(g * 2 + (2 + r), r)

        def sp_tail(sp):
            def load(e, s):
                at_least(sp, ffn_mm, e - 1)
                at_least(sp, xt_mm, e - 1)
                sp.dma_start(w1[:, s, :], a["L1_ffn_W1"][bass.ds(e, 1), :, :].rearrange("o d f -> d (o f)")
                             ).then_inc(ffn_load[s], 16)
                sp.dma_start(w2[:, s], a["L1_ffn_W2"][bass.ds(e, 1), :, :].rearrange("o (c p) d -> p (o c) d", p=P)
                             ).then_inc(ffn_load[s], 16)
                sp.dma_start(rows_e[:, s].rearrange("p k d -> p (k d)"),
                             slots_dram[bass.ds(e * CAP, CAP), :].rearrange("(p k) d -> p (k d)", p=P)
                             ).then_inc(ffn_load[s], 16)

            def store(e, s):
                sp.wait_ge(ffn_out, e + 1)
                sp.dma_start(y_dram[bass.ds(e * CAP, CAP), :].rearrange("(p k) d -> p (k d)", p=P),
                             y_rows[:, s].rearrange("p k d -> p (k d)")).then_inc(ffn_store[s], 16)

            sp.wait_ge(pv_pair, PAIRS_BEFORE[2] + NB * CFGS[2].pairs)
            sp.wait_ge(scattered, 16 * NB * BLK)
            load(0, 0)
            load(1, 1)
            with sp.Fori(0, E1 // 2 - 1) as g:
                for s in range(2):
                    store(g * 2 + s, s)
                    load(g * 2 + (2 + s), s)
            store(E1 - 2, 0)
            store(E1 - 1, 1)

            def put(b):
                sp.wait_ge(final_done, b + 1)
                sp.dma_start(OUT[:, bass.ds(b * BLK, BLK), :], x_all[:, bass.ds(b * BLK, BLK), :]
                             ).then_inc(out_store, 16)

            with sp.Fori(0, NB) as b:
                put(b)
            sp.wait_ge(out_store, 16 * NB)

        def pool_route(pool, layer):
            def entry(b, r2):
                n = layer * NB + b
                if layer == 0:
                    pool.wait_ge(rt_ssq, b + 1)
                    nc.gpsimd.tensor_tensor(var_eps[:, r2, :], ssq[:, r2, :], eps[:], ALU.add).then_inc(rt_var, 1)
                else:
                    pool.wait_ge(rt_mv, b + 1)
                    nc.gpsimd.tensor_tensor(var_eps[:, r2, :], mean_var[:, r2, :, 1], eps[:], ALU.add
                                            ).then_inc(rt_var, 1)
                pool.wait_ge(rt_var, n + 1)
                nc.gpsimd.tensor_tensor(rstd[:, r2, :], var_eps[:, r2, :], half_neg[:],
                                        ALU.pow).then_inc(rt_rstd, 1)
                if layer == 1:
                    pool.wait_ge(rt_mod_out, n + 1)
                    nc.gpsimd.tensor_tensor(mod[:, r2, 1, :], mod[:, r2, 1, :], one[:].to_broadcast([P, D]),
                                            ALU.add).then_inc(rt_mod_scale, 1)
                    pool.wait_ge(rt_mul, n + 1)
                    nc.gpsimd.tensor_tensor(h_tok[:, r2], h_tok[:, r2], mod[:, r2, 0:1, :].to_broadcast([P, BLK, D]),
                                            ALU.add).then_inc(rt_h, 1)
            entries(pool, entry)

        def pool_moe(pool):
            pool_route(pool, 0)

            def chunk(t, s):
                pool.wait_ge(moe_gated, t + 1)
                xs = x_all[:, bass.ds(t * 4, 4), :]
                nc.gpsimd.tensor_tensor(xs, xs, moe_y[:, s], ALU.add).then_inc(moe_done, 1)

            with pool.Fori(0, NB // 4) as g:
                for s in range(2):
                    chunk(g * 2 + s, s)

        def pool_route1(pool):
            pool_route(pool, 1)
            pool.wait_ge(routed, 1)
            pool.wait_ge(zero_store, 16 * 8)
            pool.wait_ge(rt_kept, NB)
            for k in range(NB * BLK):
                nc.gpsimd.indirect_dma_start(slots_dram[:], bass.IndirectOffsetOnAxis(ap=slot_put[:, k:k + 1], axis=0),
                                             res_all[:, k, :], None).then_inc(scattered, 16)
            for s in range(2):
                pool.wait_ge(ffn_store[s], 16 * (E1 // 2))
            for k in range(NB * BLK):
                nc.gpsimd.indirect_dma_start(y_all[:, k, :], None, y_dram[:],
                                             bass.IndirectOffsetOnAxis(ap=slot_get[:, k:k + 1], axis=0)
                                             ).then_inc(gathered, 16)

        def act_prologue(act):
            act.wait_ge(pro_pe, 1)
            nc.scalar.activation(rt[:, 0, 0:2 * NB // 8, :].rearrange("p a b -> p (a b)"), ps_work[:, 0:2 * NB],
                                 ACT.Exp, scale=-1.0).then_inc(pro_act, 1)

        def act_route(act, layer):
            def entry(b, r2):
                n = layer * NB + b
                act.wait_ge(rt_mod_mm, n + 1)
                at_least(act, rt_gate, n - 1)
                if layer == 1:
                    at_least(act, rt_h, b - 1)
                if layer == 0 and isinstance(b, int) and b == 0:
                    act.wait_ge(y_out, 2 * NB)
                if layer == 1 and isinstance(b, int) and b == 0:
                    act.wait_ge(y_out, 3 * NB)
                nc.scalar.copy(mod[:, r2].rearrange("p a d -> p (a d)"), ps_work[:, 0:3 * D]).then_inc(rt_mod_out, 1)
                if layer == 0:
                    act.wait_ge(res_done, b + 1)
                    at_least(act, rt_var, n - 1)
                    for k in range(BLK):
                        last = nc.scalar.activation(sq_junk[:, k, :], block_of(res_all, b * BLK + k),
                                                    ACT.Square, scale=RSQRT_D, accum_out=ssq[:, r2, k:k + 1])
                    last.then_inc(rt_ssq, 1)
                act.wait_ge(rt_ht_mm, n + 1)
                at_least(act, rt_logit_mm, n - 1)
                if layer == 0:
                    nc.scalar.copy(ht_all[:, bass.ds(b * S, S)], ps_work[:, 0:S])
                nc.scalar.copy(h_t[:, r2, :], ps_work[:, 0:S]).then_inc(rt_ht_out, 1)
                if layer == 1:
                    nc.scalar.copy(res_all[:, bass.ds(b * BLK, BLK), :], h_tok[:, r2]).then_inc(rt_kept, 1)
                act.wait_ge(rt_logit_mm, n + 1)
                nc.scalar.copy(logits[:, bass.ds(b * BLK, BLK), :],
                               ps_out[:, 0:BLK * 8].rearrange("p (k e) -> p k e", e=8)).then_inc(rt_logit, 1)
            entries(act, entry)
            act.wait_ge(rt_diff, layer + 1)
            nc.scalar.activation(rt[:, 1], rt[:, 0], ACT.Exp).then_inc(rt_exp, 1)

        def act_moe(act):
            act_route(act, 0)

            def chunk(t):
                for u in range(2 * E0):
                    n = t * 2 * E0 + u
                    act.wait_ge(gu_mm, n + 1)
                    at_least(act, gated_done, n - 1)
                    nc.scalar.activation(tanh_g[:, u % 2, :], ps_exp[:, u % 2, 0, :], ACT.Tanh,
                                         scale=0.5).then_inc(tanh_done, 1)
            chunk(0)
            with act.Fori(0, TOKENS // 512 - 1) as g:
                chunk(g + 1)

        def act_route1(act):
            act_route(act, 1)

            def expert(e, s):
                act.wait_ge(xt_mm, e + 1)
                at_least(act, up_mm, 4 * e - 4)
                nc.scalar.copy(rows_t[:, s, :], ps_work[:]).then_inc(xt_out, 1)
                for f in range(F1 // P):
                    act.wait_ge(up_mm, 4 * e + f + 1)
                    at_least(act, ffn_mm, e - 1)
                    nc.scalar.activation(hid_t[:, s, f, :], ps_exp[:, f // 2, f % 2, :], ACT.Relu
                                         ).then_inc(relu_done, 1)
            for e in range(2):
                expert(e, e)
            with act.Fori(0, E1 // 2 - 1) as g:
                for s in range(2):
                    expert(g * 2 + (2 + s), s)

        def dve_prologue(dve):
            nc.vector.memset(dir_rows[:], 0.0).then_inc(pro_dve, 1)
            dve.wait_ge(loads, 16 * N_LOADS)
            dve.wait_ge(pro_dve, 1)
            nc.vector.tensor_tensor(dir_rows[:, 0, :].rearrange("p (h e) -> p h e", e=16)[:, :, 0:3],
                                    ident[0:8, 0:8].unsqueeze(2).to_broadcast([8, 8, 3]),
                                    dirs[:, 0:3].unsqueeze(1).to_broadcast([8, 8, 3]), ALU.mult).then_inc(pro_dve, 1)
            dve.wait_ge(pro_dve, 2)
            nc.vector.tensor_scalar(dir_rows[:, 1, :], dir_rows[:, 0, :], dirs[:, 3:4], None,
                                    ALU.mult).then_inc(pro_dve, 1)
            dve.wait_ge(pro_act, 1)
            e = rt[:, 0, 0:2 * NB // 8, :].rearrange("p a b -> p (a b)")
            nc.vector.tensor_scalar(e, e, 1.0, None, ALU.add).then_inc(pro_dve, 1)
            dve.wait_ge(pro_dve, 4)
            nc.vector.reciprocal(e, e).then_inc(pro_dve, 1)
            dve.wait_ge(pro_dve, 5)
            nc.vector.tensor_tensor(silu_c[:].rearrange("p l b -> p (l b)"), ps_work[:, 0:2 * NB], e,
                                    ALU.mult).then_inc(pro_dve, 1)
            dve.wait_ge(pro_dve, 6)
            dve.wait_ge(pro_pe, 2)
            nc.vector.scalar_tensor_tensor(dir_mix[:], ident, 0.25, ps_work[:, P:2 * P], ALU.mult,
                                           ALU.add).then_inc(pro_dve, 1)

        chain = [0]

        def dve_route(dve, layer):
            def entry(b, r2):
                n = layer * NB + b
                if layer == 1:
                    dve.wait_ge(x_done, NB + b + 1)
                    for k in range(BLK):
                        last = nc.vector.bn_stats(stats6[:, r2, k, :], block_of(x_all, b * BLK + k))
                    last.then_inc(rt_stats, 1)
                    dve.wait_ge(rt_stats, b + 1)
                    at_least(dve, rt_mod_mm, n - 1)
                    if isinstance(b, int) and b < 2:
                        dve.wait_ge(mod_mm, (3 if layer else 2) * NB)
                    nc.vector.tensor_copy(c_bcast[:, r2, :], silu_c[:, layer, bass.ds(b, 1)].to_broadcast([P, P])
                                          ).then_inc(rt_bcast, 1)
                    for k in range(BLK):
                        last = nc.vector.bn_aggr(mean_var[:, r2, k, :], stats6[:, r2, k, :])
                    last.then_inc(rt_mv, 1)
                else:
                    at_least(dve, rt_mod_mm, n - 1)
                    if isinstance(b, int) and b < 2:
                        dve.wait_ge(mod_mm, (3 if layer else 2) * NB)
                    nc.vector.tensor_copy(c_bcast[:, r2, :], silu_c[:, layer, bass.ds(b, 1)].to_broadcast([P, P])
                                          ).then_inc(rt_bcast, 1)
                dve.wait_ge(rt_mod_out, n + 1)
                nc.vector.tensor_scalar(gate_tmp[:, 0, :], mod[:, r2, 2, :], 0.0, 0.5, ALU.is_ge, ALU.subtract)
                nc.vector.scalar_tensor_tensor(gate_tmp[:, 1, :], mod[:, r2, 2, :], -1.0, mod[:, r2, 2, :],
                                               ALU.mult, ALU.max).then_inc(rt_gate_a, 1)
                dve.wait_ge(rt_gate_a, n + 1)
                nc.vector.tensor_scalar(gate_tmp[:, 1, :], gate_tmp[:, 1, :], 0.25, 2.0, ALU.max, ALU.mult).then_inc(rt_gate_b, 1)
                dve.wait_ge(rt_gate_b, n + 1)
                nc.vector.tensor_tensor(block_of(gates_all, b), gate_tmp[:, 0, :], gate_tmp[:, 1, :], ALU.mult).then_inc(rt_gate, 1)
                dve.wait_ge(rt_rstd, n + 1)
                if layer == 0:
                    at_least(dve, rt_ht_mm, n - 1)
                    for k in range(BLK):
                        last = nc.vector.tensor_scalar(hn_tok[:, r2, k, :], block_of(res_all, b * BLK + k),
                                                       rstd[:, r2, k:k + 1], None, ALU.mult)
                    last.then_inc(rt_mul, 1)
                else:
                    for k in range(BLK):
                        last = nc.vector.tensor_scalar(hn_tok[:, r2, k, :], block_of(x_all, b * BLK + k),
                                                       mean_var[:, r2, k, 0:1], rstd[:, r2, k:k + 1],
                                                       ALU.subtract, ALU.mult)
                    last.then_inc(rt_xhat, 1)
                    dve.wait_ge(rt_xhat, b + 1)
                    dve.wait_ge(rt_mod_scale, b + 1)
                    at_least(dve, rt_ht_mm, n - 1)
                    at_least(dve, rt_kept, b - 1)
                    nc.vector.tensor_tensor(h_tok[:, r2], hn_tok[:, r2], mod[:, r2, 1:2, :].to_broadcast([P, BLK, D]),
                                            ALU.mult).then_inc(rt_mul, 1)
            entries(dve, entry)

            def link(ins):
                chain[0] += 1
                ins.then_inc(rt_chain, 1)
                dve.wait_ge(rt_chain, chain[0])

            shape = [P, NB * BLK, 8]

            def wide(x):
                return x.unsqueeze(2).to_broadcast(shape)

            index_down = expert_c[:, 0:1, :].to_broadcast(shape)

            def first_of(prob, best, hot):
                link(nc.vector.tensor_reduce(best, prob, AX_X, ALU.max))
                link(nc.vector.tensor_tensor(rt[:, 3], prob, wide(best), ALU.is_equal))
                link(nc.vector.tensor_tensor(rt[:, 3], rt[:, 3], index_down, ALU.mult))
                link(nc.vector.tensor_reduce(rt1[:, 5, :], rt[:, 3], AX_X, ALU.max))
                link(nc.vector.tensor_tensor(hot, rt[:, 3], wide(rt1[:, 5, :]), ALU.is_equal))

            dve.wait_ge(rt_logit, (layer + 1) * NB)
            link(nc.vector.tensor_reduce(rt1[:, 0, :], logits[:], AX_X, ALU.max))
            nc.vector.tensor_tensor(rt[:, 0], logits[:], wide(rt1[:, 0, :]), ALU.subtract).then_inc(rt_diff, 1)
            dve.wait_ge(rt_exp, layer + 1)
            link(nc.vector.tensor_reduce(rt1[:, 1, :], rt[:, 1], AX_X, ALU.add))
            link(nc.vector.reciprocal(rt1[:, 2, :], rt1[:, 1, :]))
            link(nc.vector.tensor_tensor(rt[:, 1], rt[:, 1], wide(rt1[:, 2, :]), ALU.mult))
            first_of(rt[:, 1], rt1[:, 3, :], rt[:, 2])
            if layer == 0:
                link(nc.vector.scalar_tensor_tensor(rt[:, 4], rt[:, 2], -2.0, rt[:, 1], ALU.mult, ALU.add))
                first_of(rt[:, 4], rt1[:, 4, :], rt[:, 5])
                link(nc.vector.tensor_tensor(rt[:, 2], rt[:, 2], rt[:, 5], ALU.add))
                link(nc.vector.tensor_tensor(rt[:, 2], rt[:, 2], rt[:, 1], ALU.mult))
                link(nc.vector.tensor_reduce(rt1[:, 6, :], rt[:, 2], AX_X, ALU.add))
                link(nc.vector.reciprocal(rt1[:, 7, :], rt1[:, 6, :]))
                link(nc.vector.scalar_tensor_tensor(rt[:, 2], rt[:, 2], 0.5, wide(rt1[:, 7, :]), ALU.mult, ALU.mult))
                return
            nc.vector.tensor_copy(one_hot[:], rt[:, 2]).then_inc(rt_onehot, 1)
            dve.wait_ge(rt_rank_mm, 1)
            n = NB * BLK
            earlier = ps_max[:, 0, 0:n * 8].rearrange("p (k e) -> p k e", e=8)
            counts = ps_max[:, 1, 0:n * 8].rearrange("p (k e) -> p k e", e=8)
            link(nc.vector.tensor_copy(rt[:, 3], counts))
            src, dst = 3, 4
            shift = 1
            while shift < n:
                link(nc.vector.tensor_copy(rt[:, dst, 0:shift], rt[:, src, 0:shift]))
                link(nc.vector.tensor_tensor(rt[:, dst, shift:], rt[:, src, shift:], rt[:, src, 0:n - shift], ALU.add))
                src, dst = dst, src
                shift *= 2
            link(nc.vector.tensor_tensor(rt[:, src], rt[:, src], counts, ALU.subtract))
            link(nc.vector.tensor_tensor(rt[:, src], rt[:, src], earlier, ALU.add))
            link(nc.vector.tensor_tensor(rt[:, src], rt[:, src], rt[:, 2], ALU.mult))
            link(nc.vector.tensor_reduce(rt1[:, 6, :], rt[:, src], AX_X, ALU.add))
            link(nc.vector.tensor_tensor(rt[:, 5], rt[:, 2], expert_c[:, 1:2, :].to_broadcast(shape), ALU.mult))
            link(nc.vector.tensor_reduce(rt1[:, 7, :], rt[:, 5], AX_X, ALU.add))
            token = expert_c[:, 2:6, :].rearrange("p a b -> p (a b)")
            link(nc.vector.tensor_scalar(rt1[:, 8, :], rt1[:, 6, :], float(CAP), None, ALU.is_lt))
            link(nc.vector.tensor_tensor(rt1[:, 7, :], rt1[:, 7, :], rt1[:, 6, :], ALU.add))
            link(nc.vector.tensor_tensor(rt1[:, 9, :], rt1[:, 7, :], token, ALU.subtract))
            link(nc.vector.tensor_tensor(rt1[:, 9, :], rt1[:, 9, :], rt1[:, 8, :], ALU.mult))
            link(nc.vector.tensor_tensor(slot_put[:], rt1[:, 9, :], token, ALU.add))
            link(nc.vector.tensor_tensor(slot_get[:], rt1[:, 7, :], rt1[:, 8, :], ALU.mult))
            nc.vector.tensor_tensor(rt1[:, 3, :], rt1[:, 3, :], rt1[:, 8, :], ALU.mult).then_inc(routed, 1)

        def dve_moe(dve):
            dve_route(dve, 0)

            def chunk(t, s):
                last = t * 2 * E0

                def unit(u):
                    n = t * 2 * E0 + u
                    dve.wait_ge(tanh_done, n + 1)
                    nc.vector.scalar_tensor_tensor(gated[:, u % 2, :], tanh_g[:, u % 2, :], 1.0,
                                                   ps_exp[:, u % 2, 0, :], ALU.add, ALU.mult).then_inc(gated_done, 1)
                    dve.wait_ge(gated_done, n + 1)
                    at_least(dve, down_mm, n - 1)
                    nc.vector.tensor_tensor(act_t[:, u % 2, :], gated[:, u % 2, :], ps_exp[:, u % 2, 1, :],
                                            ALU.mult).then_inc(act_done, 1)

                def accumulate(e):
                    n = t * E0 + e
                    dve.wait_ge(down_mm, 2 * n + 2)
                    at_least(dve, acc_done, n)
                    if e == 0:
                        dve.wait_ge(weight_done, t + 1)
                        at_least(dve, moe_sum, t)
                    for k in range(4):
                        y = ps_max[:, e % 2, k * D:(k + 1) * D]
                        if e == 0:
                            ins = nc.vector.tensor_scalar(acc[:, k, :], y, weight_t[:, k, e:e + 1], None, ALU.mult)
                        else:
                            ins = nc.vector.scalar_tensor_tensor(acc[:, k, :], y, weight_t[:, k, e:e + 1],
                                                                 acc[:, k, :], ALU.mult, ALU.add)
                    ins.then_inc(acc_done, 1)

                at_least(dve, acc_done, t * E0)
                nc.vector.tensor_copy(weight_t[:], rt[:, 2, bass.ds(t * 4, 4), :]).then_inc(weight_done, 1)
                for e in range(E0):
                    unit(2 * e)
                    if e > 0:
                        accumulate(e - 1)
                    unit(2 * e + 1)
                accumulate(E0 - 1)
                dve.wait_ge(acc_done, (t + 1) * E0)
                at_least(dve, moe_done, t - 1)
                nc.vector.tensor_tensor(moe_y[:, s], acc[:], res_all[:, bass.ds(t * 4, 4), :], ALU.add
                                        ).then_inc(moe_sum, 1)
                dve.wait_ge(moe_sum, t + 1)
                nc.vector.tensor_scalar(moe_y[:, s], moe_y[:, s], CLIP, -CLIP, ALU.min, ALU.max
                                        ).then_inc(moe_clip, 1)
                dve.wait_ge(moe_clip, t + 1)
                for k in range(2):
                    ins = nc.vector.tensor_tensor(moe_y[:, s, 2 * k:2 * k + 2, :], moe_y[:, s, 2 * k:2 * k + 2, :],
                                                  gates_all[:, bass.ds(t * 2 + k, 1), :].to_broadcast([P, BLK, D]),
                                                  ALU.mult)
                ins.then_inc(moe_gated, 1)

            chunk(0, 0)
            chunk(1, 1)
            with dve.Fori(0, TOKENS // 1024 - 1) as g:
                for s in range(2):
                    chunk(g * 2 + (2 + s), s)

        def dve_route1(dve):
            dve_route(dve, 1)

            def expert(e, s):
                dve.wait_ge(ffn_mm, e + 1)
                if not isinstance(e, int) or e >= 2:
                    dve.wait_ge(ffn_store[s], 8 * (e - s))
                nc.vector.tensor_copy(y_rows[:, s].rearrange("p k d -> p (k d)"), ps_max[:, s, :]).then_inc(ffn_out, 1)
            for e in range(2):
                expert(e, e)
            with dve.Fori(0, E1 // 2 - 1) as g:
                for s in range(2):
                    expert(g * 2 + (2 + s), s)
            dve.wait_ge(gathered, 16 * NB * BLK)
            for b in range(NB):
                for k in range(BLK):
                    j = b * BLK + k
                    last = nc.vector.scalar_tensor_tensor(y_all[:, j, :], y_all[:, j, :], rt1[:, 3, j:j + 1],
                                                          gates_all[:, b, :], ALU.mult, ALU.mult)
                last.then_inc(y_gated, 1)
                dve.wait_ge(y_gated, b + 1)
                xs = x_all[:, b * BLK:(b + 1) * BLK, :]
                nc.vector.tensor_tensor(xs, xs, y_all[:, b * BLK:(b + 1) * BLK, :], ALU.add).then_inc(final_done, 1)

        def pe_prologue(pe):
            pe.wait_ge(loads, 16 * N_LOADS)
            for layer in range(2):
                last = nc.tensor.transpose(ps_work[:, layer * NB:(layer + 1) * NB], c_rows[:, layer, :],
                                           ident[0:NB, 0:NB])
            last.then_inc(pro_pe, 1)
            pe.wait_ge(pro_dve, 6)
            nc.tensor.matmul(ps_work[:, P:2 * P], dir_rows[:, 0, :], dir_rows[:, 1, :], start=True, stop=True
                             ).then_inc(pro_pe, 1)
            pe.wait_ge(pro_dve, 7)
            pe.wait_ge(rotated, 1)
            pe.wait_ge(select_ready, 1)
            pe.wait_ge(ones_ready, 4)

        def pe_route(pe, layer):
            def entry(b, r2):
                n = layer * NB + b
                pe.wait_ge(rt_bcast, n + 1)
                if isinstance(b, int) and b == 0:
                    pe.wait_ge(y_out, (3 if layer else 2) * NB)
                at_least(pe, rt_ht_out, n)
                nc.tensor.matmul(ps_work[:, 0:3 * D], c_bcast[:, r2, :], wmod[:, layer, 3 * D:6 * D],
                                 start=True, stop=True).then_inc(rt_mod_mm, 1)
                pe.wait_ge(rt_mod_out, n + 1)
                if layer == 0:
                    pe.wait_ge(rt_mul, n + 1)
                else:
                    pe.wait_ge(rt_h, b + 1)
                for k in range(BLK):
                    src = hn_tok[:, r2, k, :] if layer == 0 else h_tok[:, r2, k, :]
                    last = nc.tensor.transpose(ps_work[:, k * P:(k + 1) * P], src, ident)
                last.then_inc(rt_ht_mm, 1)
                pe.wait_ge(rt_ht_out, n + 1)
                at_least(pe, rt_logit, n)
                if isinstance(b, int) and b == 0:
                    pe.wait_ge(o_done, (3 if layer else 2) * NB)
                for k in range(BLK):
                    lhs = h_t[:, r2, k * P:(k + 1) * P]
                    last = nc.tensor.matmul(ps_out[:, k * 8:(k + 1) * 8], lhs, wr[:, layer, :], start=True, stop=True)
                last.then_inc(rt_logit_mm, 1)
            entries(pe, entry)

        def pe_moe(pe):
            pe.wait_ge(folded, 2)
            pe_route(pe, 0)

            def chunk(t):
                x_t = ht_all[:, bass.ds(t * 512, 512)]

                def up(u):
                    n = t * 2 * E0 + u
                    e, f = u // 2, u % 2
                    at_least(pe, act_done, n - 1)
                    for i, w in enumerate((wg, wu)):
                        last = nc.tensor.matmul(ps_exp[:, f, i, :], w[:, e, f * P:(f + 1) * P], x_t,
                                                start=True, stop=True)
                    last.then_inc(gu_mm, 1)

                def down(u):
                    n = t * 2 * E0 + u
                    e, f = u // 2, u % 2
                    pe.wait_ge(act_done, n + 1)
                    if f == 0:
                        at_least(pe, acc_done, t * E0 + e - 1)
                    for k in range(4):
                        last = nc.tensor.matmul(ps_max[:, e % 2, k * D:(k + 1) * D], act_t[:, f, k * P:(k + 1) * P],
                                                wd[:, e, f, :], start=(f == 0 and k == 0), stop=(f == 1),
                                                skip_group_check=True)
                    last.then_inc(down_mm, 1)

                for u in range(2 * E0):
                    up(u)
                    if u > 0:
                        down(u - 1)
                down(2 * E0 - 1)

            chunk(0)
            with pe.Fori(0, TOKENS // 512 - 1) as g:
                chunk(g + 1)

        def pe_route1(pe):
            pe_route(pe, 1)
            pe.wait_ge(rt_onehot, 1)
            pe.wait_ge(max_done, HEADS_BEFORE[2] + NB * CFGS[2].heads)
            hot = one_hot[:].rearrange("p k e -> p (k e)")
            n = NB * BLK * 8
            nc.tensor.matmul(ps_max[:, 0, 0:n], upper_ones[:, 0, :], hot, start=True, stop=True)
            nc.tensor.matmul(ps_max[:, 1, 0:n], upper_ones[:, 1, :], hot, start=True, stop=True).then_inc(rt_rank_mm, 1)

            def expert(e, s):
                pe.wait_ge(ffn_load[s], 24 * (e - s) + 48)
                at_least(pe, xt_out, e)
                for k in range(4):
                    last = nc.tensor.transpose(ps_work[:, k * P:(k + 1) * P], rows_e[:, s, k, :], ident)
                last.then_inc(xt_mm, 1)
                pe.wait_ge(xt_out, e + 1)
                for f in range(F1 // P):
                    at_least(pe, relu_done, 4 * e + f - 3)
                    nc.tensor.matmul(ps_exp[:, f // 2, f % 2, :], w1[:, s, f * P:(f + 1) * P], rows_t[:, s, :],
                                     start=True, stop=True).then_inc(up_mm, 1)
                pe.wait_ge(relu_done, 4 * e + 4)
                at_least(pe, ffn_out, e - 1)
                for k in range(4):
                    for f in range(F1 // P):
                        last = nc.tensor.matmul(ps_max[:, s, k * D:(k + 1) * D], hid_t[:, s, f, k * P:(k + 1) * P],
                                                w2[:, s, f, :], start=(f == 0), stop=(f == F1 // P - 1))
                last.then_inc(ffn_mm, 1)
            pe.wait_ge(routed, 1)
            for e in range(2):
                expert(e, e)
            with pe.Fori(0, E1 // 2 - 1) as g:
                for s in range(2):
                    expert(g * 2 + (2 + s), s)

        @block.sync
        def _(sp):
            for dst, src in dma_list:
                sp.dma_start(dst, src).then_inc(loads, 16)
            stage_sel = stage.rearrange("p (a b) -> p a b", a=4)
            sel_dram = a["select"].rearrange("p a b g m -> p a b (g m)")
            sp.dma_start(stage.rearrange("p (a b) -> p a b", a=16), a["max_select"]).then_inc(sel_load, 16)
            k = NB * BLK // 8
            for n in range(8):
                sp.dma_start(x_all[:, n * k:(n + 1) * k, :], X[:, n * k:(n + 1) * k, :]).then_inc(x_load, 16)
            sp.wait_ge(zeros_ready, 1)
            for n in range(8):
                sp.dma_start(slots_dram[n * CAP:(n + 1) * CAP, :].rearrange("(p k) d -> p (k d)", p=P),
                             zeros).then_inc(zero_store, 16)
            for n in range(3):
                sp.wait_ge(select_ready, n + 1)
                if n == 2:
                    sp.wait_ge(moe_done, NB // 2)
                sp.dma_start(stage_sel, sel_dram[:, n]).then_inc(sel_load, 16)
            sp_tail(sp)

        @block.gpsimd
        def _(pool):
            nc.gpsimd.memset(zeros, 0.0).then_inc(zeros_ready, 1)
            nc.gpsimd.memset(half_neg[:], -0.5)
            nc.gpsimd.memset(eps[:], LN_EPS)
            nc.gpsimd.memset(one[:], 1.0)
            for v in v_tok:
                nc.gpsimd.memset(v[:], 1.0).then_inc(ones_ready, 1)
            nc.gpsimd.memset(max_t[:].bitcast(F32), 0.0).then_inc(ones_ready, 1)
            pool.wait_ge(loads, 16 * N_LOADS)
            nc.gpsimd.tensor_copy(ident_bf[:], squares[:, 0, :])
            nc.gpsimd.tensor_copy(masks[:], squares[:, 1:5, :])
            nc.gpsimd.tensor_copy(upper_ones[:], squares[:, 5:7, :])
            nc.gpsimd.tensor_scalar(wq[:, 1, 0, :], wq[:, 1, 0, :], ln_w[:, 0:1], None, ALU.mult)
            nc.gpsimd.tensor_scalar(wk[:, 1, 0, 0:32], wk[:, 1, 0, 0:32], ln_w[:, 0:1], None, ALU.mult)
            nc.gpsimd.tensor_scalar(wv[:, 1, 0:32], wv[:, 1, 0:32], ln_w[:, 0:1], None, ALU.mult).then_inc(folded, 1)
            pool.wait_ge(folded, 1)
            for w, cols in ((wq, (D, D, D)), (wk, (64, 32, D))):
                for c in CFGS:
                    half = c.hd // 2
                    src = w[:, c.index, 0, 0:cols[c.index]].rearrange("p (h e) -> p h e", e=c.hd)
                    dst = w[:, c.index, 1, 0:cols[c.index]].rearrange("p (h e) -> p h e", e=c.hd)
                    if c.layer == 0:
                        nc.gpsimd.tensor_copy(dst[:, :, 0:half], src[:, :, half:])
                        last = nc.gpsimd.tensor_copy(dst[:, :, half:], src[:, :, 0:half])
                    else:
                        nc.gpsimd.tensor_copy(dst[:, :, 0:half], src[:, :, 1::2])
                        last = nc.gpsimd.tensor_copy(dst[:, :, half:], src[:, :, 0::2])
            last.then_inc(rotated, 1)
            pool.wait_ge(sel_load, 16)
            nc.gpsimd.tensor_copy(max_select[:].rearrange("p h m -> p (h m)"), stage).then_inc(select_ready, 1)

            def load_select(c):
                at_least(pool, sel_mm, 4 * c.first)
                pool.wait_ge(sel_load, 16 * (c.index + 2))
                nc.gpsimd.tensor_copy(select[:].rearrange("p b g m -> p (b g m)"), stage).then_inc(select_ready, 1)

            load_select(CFGS[0])
            nc.gpsimd.tensor_scalar(wr[:, 0, :], wr[:, 0, :], ln_w[:, 1:2], None, ALU.mult)
            nc.gpsimd.tensor_scalar(wg, wg, ln_w[:, 1:2], None, ALU.mult)
            nc.gpsimd.tensor_scalar(wu, wu, ln_w[:, 1:2], None, ALU.mult).then_inc(folded, 1)

            def prep(c, b, r, name):
                n, r2 = n_of(c, b), r % 2
                if name == "mod":
                    pool.wait_ge(mv_done, n + 1)
                    nc.gpsimd.tensor_tensor(var_eps[:, r2, :], mean_var[:, r2, :, 1], eps[:], ALU.add
                                            ).then_inc(var_done, 1)
                    pool.wait_ge(var_done, n + 1)
                    nc.gpsimd.tensor_tensor(rstd[:, r2, :], var_eps[:, r2, :], half_neg[:],
                                            ALU.pow).then_inc(rstd_done, 1)
                    pool.wait_ge(mod_out, n + 1)
                    nc.gpsimd.tensor_tensor(mod[:, r, 1, :], mod[:, r, 1, :], one[:].to_broadcast([P, D]),
                                            ALU.add).then_inc(mod_scale, 1)
                    pool.wait_ge(h_mul, n + 1)
                    nc.gpsimd.tensor_tensor(h_tok[:, r], h_tok[:, r],
                                            mod[:, r, 0:1, :].to_broadcast([P, BLK, D]), ALU.add).then_inc(h_done, 1)
                    if c.index == 1:
                        pool.wait_ge(ssq_done, n - NB + 1)
                        nc.gpsimd.tensor_tensor(ssq_eps[:, r2, :], ssq[:, r2, :], eps[:], ALU.add
                                                ).then_inc(ssq_eps_done, 1)
                        pool.wait_ge(ssq_eps_done, n - NB + 1)
                        nc.gpsimd.tensor_tensor(rrms[:, r2, :], ssq_eps[:, r2, :], half_neg[:],
                                                ALU.pow).then_inc(rrms_done, 1)
                if name in ("q", "k"):
                    i = 0 if name == "q" else 1
                    m = P if name == "q" else c.kv * c.hd
                    rope_done, sum_done, lo_done = ((q_rope, q_sum, q_lo), (k_rope, k_sum, k_lo))[i]
                    pool.wait_ge(rope_done, n + 1)
                    if c.index > 0 or i == 1:
                        at_least(pool, sel_mm, 4 * n)
                    if c.index > 0 or i == 1:
                        nc.gpsimd.tensor_tensor(split[0:m, i, 0, :], rope_a[0:m, i, :], rope_b[0:m, i, :], ALU.add)
                        nc.gpsimd.tensor_tensor(roped[0:m, i, :], rope_a[0:m, i, :], rope_b[0:m, i, :],
                                                ALU.add).then_inc(sum_done, 1)
                        pool.wait_ge(sum_done, n + 1)
                        nc.gpsimd.tensor_tensor(split[0:m, i, 1, :], roped[0:m, i, :],
                                                split[0:m, i, 0, :].bitcast(F32), ALU.subtract).then_inc(lo_done, 1)
                    else:
                        nc.gpsimd.tensor_tensor(roped[0:m, i, :], rope_a[0:m, i, :], rope_b[0:m, i, :],
                                                ALU.add).then_inc(sum_done, 1)

            def post(c, b, r, name):
                if name == "y" and c.index != 1:
                    pool.wait_ge(y_out, n_of(c, b) + 1)
                    xs = x_all[:, bass.ds(b * BLK, BLK), :]
                    nc.gpsimd.tensor_tensor(xs, xs, y_tok[:, r % 2], ALU.add).then_inc(x_done, 1)

            def start(c):
                if c.index > 0:
                    load_select(c)
                for b in (0, 1):
                    for name in SLOT_STEPS:
                        prep(c, b, b, name)

            def segment(c, b, r):
                with_post, with_prep, _ = flags(b)
                for names in slots(c, with_post, with_prep):
                    for name in names:
                        if name in ("ot", "y"):
                            post(c, b - 1, (r - 1) % RING, name)
                        else:
                            prep(c, b + 2, (r + 2) % RING, name)

            def finish(c):
                post(c, NB - 1, (NB - 1) % RING, "y")

            run(pool, CFGS[0], start, segment, finish)
            run(pool, CFGS[1], start, segment, finish)
            pool_moe(pool)
            run(pool, CFGS[2], start, segment, finish)
            pool_route1(pool)

        @block.scalar
        def _(act):
            act_prologue(act)

            def prep(c, b, r, name):
                n, r2 = n_of(c, b), r % 2
                if name == "mod":
                    act.wait_ge(mod_mm, n + 1)
                    at_least(act, y_out, n - RING + 1)
                    nc.scalar.copy(mod[:, r].rearrange("p a d -> p (a d)"), ps_work[:, 0:3 * D]).then_inc(mod_out, 1)
                    if c.index == 1:
                        act.wait_ge(h_done, n + 1)
                        at_least(act, ssq_eps_done, n - NB - 1)
                        for k in range(BLK):
                            last = nc.scalar.activation(sq_junk[:, k, :], h_tok[:, r, k, :], ACT.Square, scale=RSQRT_D,
                                                        accum_out=ssq[:, r2, k:k + 1])
                        last.then_inc(ssq_done, 1)
                if name == "ht":
                    act.wait_ge(ht_mm, n + 1)
                    at_least(act, v_mm, n - 1)
                    nc.scalar.copy(h_t[:, r2, :], ps_work[:, 0:S]).then_inc(ht_out, 1)
                if name == "qd":
                    act.wait_ge(qd_mm, n + 1)
                    at_least(act, sel_mm, 4 * n)
                    nc.scalar.copy(split[:, 0, 0, :], ps_work[:, 0:S]).then_inc(q_hi, 1)
                if name == "v":
                    act.wait_ge(v_mm, n + 1)
                    at_least(act, pv_pair, pairs_until(c, b - RING))
                    nc.scalar.copy(v_tok[c.index][:, r, :, :, 0:c.hd],
                                   ps_work[:, 0:S].rearrange("p (k c) -> p k c", k=BLK)[:, :, 0:c.kv * c.hd]
                                   .rearrange("p k (h e) -> p k h e", e=c.hd)).then_inc(v_out, 1)
                if name[:3] == "sel":
                    j = int(name[3])
                    act.wait_ge(sel_mm, 4 * n + j + 1)
                    if j % 2 == 0:
                        at_least(act, pv_pair, pairs_until(c, b - RING))
                    dst = (q_st, k_st)[j // 2][:, r, 2 * (j % 2):2 * (j % 2) + 2, :]
                    nc.scalar.copy(dst, ps_work[:].rearrange("p (g s) -> p g s", g=2)).then_inc(sel_out, 1)

            def post(c, b, r, name):
                n, r2 = n_of(c, b), r % 2
                if name == "ot":
                    act.wait_ge(ot_mm, n + 1)
                    at_least(act, y_mm, n)
                    nc.scalar.copy(o_t[:, r2, :], ps_work[:, 0:S]).then_inc(ot_out, 1)

            def max_rows(c, b, r):
                n, r2 = n_of(c, b), r % 2
                act.wait_ge(mt_mm, n + 1)
                at_least(act, exp_done, pairs_until(c, b - 2))
                nc.scalar.copy(max_t[0:c.heads, r2, :], ps_work[0:c.heads, 0:S]).then_inc(mt_hi, 1)

            def start(c):
                if c.index == 0:
                    act.wait_ge(ones_ready, 4)
                    act.wait_ge(zero_store, 16 * 8)
                for b in (0, 1):
                    for name in SLOT_STEPS:
                        if name != "qd" or c.index == 0:
                            prep(c, b, b, name)
                max_rows(c, 0, 0)

            def segment(c, b, r):
                with_post, with_prep, with_next = flags(b)
                w = c.q_cols()
                for h, names in enumerate(slots(c, with_post, with_prep)):
                    if h % 2:
                        p = h // 2
                        pn = PAIRS_BEFORE[c.index] + b * c.pairs + p
                        act.wait_ge(exp_mm, pn + 1)
                        at_least(act, pv_pair, pn - 3)
                        nc.scalar.activation(probs[:, p % 4, :, 0:w], ps_exp[:, p % 2, :, 0:w], ACT.Exp,
                                             scale=c.scale).then_inc(exp_done, 1)
                    for name in names:
                        if name in ("ot", "y"):
                            post(c, b - 1, (r - 1) % RING, name)
                        else:
                            prep(c, b + 2, (r + 2) % RING, name)
                if with_next:
                    max_rows(c, b + 1, (r + 1) % RING)

            def finish(c):
                post(c, NB - 1, (NB - 1) % RING, "ot")

            run(act, CFGS[0], start, segment, finish)
            run(act, CFGS[1], start, segment, finish)
            act_moe(act)
            run(act, CFGS[2], start, segment, finish)
            act_route1(act)

        @block.vector
        def _(dve):
            dve_prologue(dve)

            def prep(c, b, r, name):
                n, r2 = n_of(c, b), r % 2
                if name == "mod":
                    if c.index == 0:
                        dve.wait_ge(x_load, 16 * 8)
                    elif c.index == 1:
                        dve.wait_ge(x_done, b + 1)
                    else:
                        dve.wait_ge(moe_done, NB // 2)
                    for k in range(BLK):
                        last = nc.vector.bn_stats(stats6[:, r2, k, :], block_of(x_all, b * BLK + k))
                    last.then_inc(stats_done, 1)
                    dve.wait_ge(stats_done, n + 1)
                    at_least(dve, mod_mm, n - 1)
                    nc.vector.tensor_copy(c_bcast[:, r2, :], silu_c[:, c.layer, bass.ds(b, 1)].to_broadcast([P, P])
                                          ).then_inc(c_bcast_done, 1)
                    for k in range(BLK):
                        last = nc.vector.bn_aggr(mean_var[:, r2, k, :], stats6[:, r2, k, :])
                    last.then_inc(mv_done, 1)
                    dve.wait_ge(mod_out, n + 1)
                    nc.vector.tensor_scalar(gate_tmp[:, 0, :], mod[:, r, 2, :], 0.0, 0.5, ALU.is_ge, ALU.subtract)
                    nc.vector.scalar_tensor_tensor(gate_tmp[:, 1, :], mod[:, r, 2, :], -1.0, mod[:, r, 2, :],
                                                   ALU.mult, ALU.max).then_inc(gate_a, 1)
                    dve.wait_ge(gate_a, n + 1)
                    nc.vector.tensor_scalar(gate_tmp[:, 1, :], gate_tmp[:, 1, :], 0.25, 2.0, ALU.max, ALU.mult).then_inc(gate_b, 1)
                    dve.wait_ge(gate_b, n + 1)
                    nc.vector.tensor_tensor(mod[:, r, 2, :], gate_tmp[:, 0, :], gate_tmp[:, 1, :], ALU.mult).then_inc(gate_done, 1)
                    dve.wait_ge(rstd_done, n + 1)
                    for k in range(BLK):
                        last = nc.vector.tensor_scalar(h_tok[:, r, k, :], block_of(x_all, b * BLK + k),
                                                       mean_var[:, r2, k, 0:1], rstd[:, r2, k:k + 1],
                                                       ALU.subtract, ALU.mult)
                    last.then_inc(xhat_done, 1)
                    dve.wait_ge(xhat_done, n + 1)
                    dve.wait_ge(mod_scale, n + 1)
                    nc.vector.tensor_tensor(h_tok[:, r], h_tok[:, r], mod[:, r, 1:2, :].to_broadcast([P, BLK, D]),
                                            ALU.mult).then_inc(h_mul, 1)
                    if c.index == 1:
                        dve.wait_ge(rrms_done, n - NB + 1)
                        at_least(dve, ht_mm, n - 1)
                        for k in range(BLK):
                            last = nc.vector.tensor_scalar(hn_tok[:, r2, k, :], h_tok[:, r, k, :],
                                                           rrms[:, r2, k:k + 1], None, ALU.mult)
                        last.then_inc(hn_done, 1)
                if name in ("q", "k"):
                    i = 0 if name == "q" else 1
                    m = P if name == "q" else c.kv * c.hd
                    mm_done, rope_done, sum_done = ((q_mm, q_rope, q_sum), (k_mm, k_rope, k_sum))[i]
                    t = 0 if c.hd == 16 else 2
                    dve.wait_ge(mm_done, n + 1)
                    at_least(dve, sum_done, n)
                    nc.vector.tensor_tensor(rope_a[0:m, i, :], ps_work[0:m, 0:S], rope[0:m, t, :], ALU.mult)
                    nc.vector.tensor_tensor(rope_b[0:m, i, :], ps_work[0:m, S:2 * S], rope[0:m, t + 1, :],
                                            ALU.mult).then_inc(rope_done, 1)
                if name == "qd":
                    dve.wait_ge(q_hi, n + 1)
                    nc.vector.tensor_tensor(split[:, 0, 1, :], ps_work[:, 0:S], split[:, 0, 0, :].bitcast(F32),
                                            ALU.subtract).then_inc(q_lo, 1)

            def post(c, b, r, name):
                n, r2 = n_of(c, b), r % 2
                if name == "ot":
                    dve.wait_ge(pv_pair, pairs_until(c, b))
                    at_least(dve, ot_mm, n)
                    rows = BLK * c.heads
                    po = ps_out[:, 0:rows * (c.hd + 1)].rearrange("p (h e) -> p h e", e=c.hd + 1)
                    nc.vector.reciprocal(recip[:, r2, 0:rows], po[:, :, c.hd]).then_inc(recip_done, 1)
                    dve.wait_ge(recip_done, n + 1)
                    nc.vector.tensor_tensor(o_tok[:, r2].rearrange("p k (h e) -> p (k h) e", e=c.hd),
                                            po[:, :, 0:c.hd],
                                            recip[:, r2, 0:rows].unsqueeze(2).to_broadcast([P, rows, c.hd]),
                                            ALU.mult).then_inc(o_done, 1)
                if name == "y":
                    dve.wait_ge(y_mm, n + 1)
                    y = ps_work[:, 0:S].rearrange("p (k d) -> p k d", k=BLK)
                    if c.index != 1:
                        if isinstance(b, int):
                            at_least(dve, x_done, NB * (c.index == 2) + b)
                        nc.vector.tensor_tensor(y_tok[:, r2], y, mod[:, r, 2:3, :].to_broadcast([P, BLK, D]),
                                                ALU.mult).then_inc(y_out, 1)
                    else:
                        nc.vector.tensor_tensor(y_tok[:, r2], y, h_tok[:, r], ALU.add).then_inc(y_out, 1)
                        dve.wait_ge(y_out, n + 1)
                        nc.vector.tensor_scalar(res_all[:, bass.ds(b * BLK, BLK), :], y_tok[:, r2], CLIP, -CLIP,
                                                ALU.min, ALU.max).then_inc(res_done, 1)

            def head_max(c, b, r, h):
                n, r2 = n_of(c, b), r % 2
                hn = HEADS_BEFORE[c.index] + b * c.heads + h
                parts = 3 if c.causal else 2
                dve.wait_ge(max_mm, hn + 1)
                if h == 0:
                    at_least(dve, mt_mm, n - 1)
                src = ps_max[:, h % 2, 0:c.q_cols()].rearrange("p (k s) -> p k s", k=parts)
                nc.vector.tensor_reduce(row_max[:, r2, 0:parts, h], src, AX_X, ALU.max).then_inc(max_done, 1)
                if h == c.heads - 1 and c.causal:
                    dve.wait_ge(max_done, hn + 1)
                    nc.vector.tensor_tensor(row_max[:, r2, 1, 0:c.heads], row_max[:, r2, 1, 0:c.heads],
                                            row_max[:, r2, 2, 0:c.heads], ALU.max).then_inc(max_all, 1)

            def max_rows(c, b, r):
                n, r2 = n_of(c, b), r % 2
                dve.wait_ge(mt_hi, n + 1)
                nc.vector.tensor_tensor(max_t[32:32 + c.heads, r2, :], ps_work[0:c.heads, 0:S],
                                        max_t[0:c.heads, r2, :].bitcast(F32), ALU.subtract).then_inc(mt_out, 1)

            def start(c):
                for b in (0, 1):
                    for name in SLOT_STEPS:
                        if name != "qd" or c.index == 0:
                            prep(c, b, b, name)
                for h in range(c.heads):
                    head_max(c, 0, 0, h)
                max_rows(c, 0, 0)

            def segment(c, b, r):
                with_post, with_prep, with_next = flags(b)
                for h, names in enumerate(slots(c, with_post, with_prep)):
                    if with_next:
                        head_max(c, b + 1, (r + 1) % RING, h)
                    for name in names:
                        if name in ("ot", "y"):
                            post(c, b - 1, (r - 1) % RING, name)
                        else:
                            prep(c, b + 2, (r + 2) % RING, name)
                if with_next:
                    max_rows(c, b + 1, (r + 1) % RING)

            def finish(c):
                for name in ("ot", "y"):
                    post(c, NB - 1, (NB - 1) % RING, name)

            run(dve, CFGS[0], start, segment, finish)
            run(dve, CFGS[1], start, segment, finish)
            dve_moe(dve)
            run(dve, CFGS[2], start, segment, finish)
            dve_route1(dve)

        @block.tensor
        def _(pe):
            pe_prologue(pe)

            def prep(c, b, r, name, free):
                n, r2 = n_of(c, b), r % 2
                m = c.kv * c.hd
                if name == "mod":
                    pe.wait_ge(c_bcast_done, n + 1)
                    if free:
                        at_least(pe, *free)
                    nc.tensor.matmul(ps_work[:, 0:3 * D], c_bcast[:, r2, :], wmod[:, c.layer, c.mod:c.mod + 3 * D],
                                     start=True, stop=True).then_inc(mod_mm, 1)
                if name == "ht":
                    pe.wait_ge(mod_out, n + 1)
                    if c.index == 1:
                        pe.wait_ge(hn_done, n - NB + 1)
                        src = hn_tok[:, r2]
                    else:
                        pe.wait_ge(h_done, n + 1)
                        src = h_tok[:, r]
                    for k in range(BLK):
                        last = nc.tensor.transpose(ps_work[:, k * P:(k + 1) * P], src[:, k, :], ident)
                    last.then_inc(ht_mm, 1)
                if name == "q":
                    pe.wait_ge(ht_out, n + 1)
                    for i in range(2):
                        last = nc.tensor.matmul(ps_work[:, i * S:(i + 1) * S], wq[:, c.index, i, :], h_t[:, r2, :],
                                                start=True, stop=True)
                    last.then_inc(q_mm, 1)
                if name == "qd":
                    pe.wait_ge(q_sum, n + 1)
                    nc.tensor.matmul(ps_work[:, 0:S], dir_mix[:], roped[:, 0, :], start=True, stop=True
                                     ).then_inc(qd_mm, 1)
                if name == "k":
                    if c.index == 0:
                        pe.wait_ge(q_lo, n + 1)
                    else:
                        pe.wait_ge(q_rope, n + 1)
                    for i in range(2):
                        last = nc.tensor.matmul(ps_work[0:m, i * S:(i + 1) * S], wk[:, c.index, i, 0:m],
                                                h_t[:, r2, :], start=True, stop=True)
                    last.then_inc(k_mm, 1)
                if name == "v":
                    pe.wait_ge(k_rope, n + 1)
                    for k in range(BLK):
                        last = nc.tensor.matmul(ps_work[:, k * P:k * P + m], h_t[:, r2, k * P:(k + 1) * P],
                                                wv[:, c.index, 0:m], start=True, stop=True)
                    last.then_inc(v_mm, 1)
                if name[:3] == "sel":
                    j = int(name[3])
                    i, rows = j // 2, (P, m)[j // 2]
                    if j == 0:
                        pe.wait_ge(v_out, n + 1)
                        pe.wait_ge(q_lo, n + 1)
                    else:
                        pe.wait_ge(sel_out, 4 * n + j)
                    if j == 2:
                        pe.wait_ge(k_lo, n + 1)
                    for g in range(2):
                        for part in range(2):
                            last = nc.tensor.matmul(ps_work[:, g * S:(g + 1) * S],
                                                    select[0:rows, 2 * i + part, 2 * (j % 2) + g, :],
                                                    split[0:rows, i, part, :], start=(part == 0), stop=(part == 1))
                    last.then_inc(sel_mm, 1)

            def post(c, b, r, name, free):
                n, r2 = n_of(c, b), r % 2
                if name == "ot":
                    pe.wait_ge(o_done, n + 1)
                    pe.wait_ge(*free)
                    for k in range(BLK):
                        last = nc.tensor.transpose(ps_work[:, k * P:(k + 1) * P], o_tok[:, r2, k, :], ident)
                    last.then_inc(ot_mm, 1)
                if name == "y":
                    pe.wait_ge(ot_out, n + 1)
                    for k in range(BLK):
                        last = nc.tensor.matmul(ps_work[:, k * P:(k + 1) * P], o_t[:, r2, k * P:(k + 1) * P],
                                                wo[:, c.index, :], start=True, stop=True)
                    last.then_inc(y_mm, 1)

            def max_scores(c, b, r, h):
                n = n_of(c, b)
                hn = HEADS_BEFORE[c.index] + b * c.heads + h
                g, base = h // c.per_group, (h % c.per_group) * c.strip
                rows = slice(base, base + c.krows)
                if h == 0:
                    pe.wait_ge(sel_out, 4 * n + 4)
                at_least(pe, max_done, hn - 1)
                bank = ps_max[:, h % 2, :]
                if c.causal:
                    nc.tensor.matmul(bank[:, 0:P], ident_bf[:], masks[:, 0, :], start=True, stop=False,
                                     skip_group_check=True)
                    nc.tensor.matmul(bank[:, 2 * P:3 * P], ident_bf[:], masks[:, 0, :], start=False, stop=False,
                                     skip_group_check=True)
                    if c.window:
                        nc.tensor.matmul(bank[:, P:2 * P], ident_bf[:], masks[:, 1, :], start=False, stop=False,
                                         skip_group_check=True)
                    nc.tensor.matmul(bank[:, 0:P], q_st[rows, r, g, 0:P], k_st[rows, r, g, 0:P], start=False,
                                     stop=True, skip_group_check=True)
                    nc.tensor.matmul(bank[:, P:3 * P], q_st[rows, r, g, P:S], k_st[rows, r, g, :], start=False,
                                     stop=True, skip_group_check=True).then_inc(max_mm, 1)
                else:
                    for k in range(BLK):
                        last = nc.tensor.matmul(bank[:, k * S:(k + 1) * S], q_st[rows, r, g, k * P:(k + 1) * P],
                                                k_st[rows, r, g, :], start=True, stop=True)
                    last.then_inc(max_mm, 1)

            def exp_scores(c, b, r, h):
                n = n_of(c, b)
                p = h // 2
                pn = PAIRS_BEFORE[c.index] + b * c.pairs + p
                g, base = h // c.per_group, (h % c.per_group) * c.strip
                rows = slice(base, base + c.krows)
                if h == 0:
                    pe.wait_ge(mt_out, n + 1)
                if h % 2 == 0:
                    at_least(pe, exp_done, pn - 1)
                bank = ps_exp[:, p % 2, h % 2, :]
                second = slice(P, S) if c.causal else slice(0, S)
                w = second.stop - second.start
                nc.tensor.matmul(bank[:, 0:S], max_select[:, h, :], max_t[:, r % 2, :], start=True, stop=False,
                                 skip_group_check=True)
                nc.tensor.matmul(bank[:, S:S + w], max_select[:, h, :], max_t[:, r % 2, second], start=False,
                                 stop=False, skip_group_check=True)
                if c.causal:
                    nc.tensor.matmul(bank[:, 0:P], ident_bf[:], masks[:, 2, :], start=False, stop=False,
                                     skip_group_check=True)
                    nc.tensor.matmul(bank[:, S:S + P], ident_bf[:], masks[:, 2, :], start=False, stop=False,
                                     skip_group_check=True)
                    if c.window:
                        nc.tensor.matmul(bank[:, P:S], ident_bf[:], masks[:, 3, :], start=False, stop=False,
                                         skip_group_check=True)
                nc.tensor.matmul(bank[:, 0:S], k_st[rows, r, g, 0:P], q_st[rows, r, g, :], start=False, stop=True,
                                 skip_group_check=True)
                last = nc.tensor.matmul(bank[:, S:S + w], k_st[rows, r, g, P:S], q_st[rows, r, g, second],
                                        start=False, stop=True, skip_group_check=True)
                if h % 2:
                    last.then_inc(exp_mm, 1)

            def values(c, b, r, p):
                n = n_of(c, b)
                pn = PAIRS_BEFORE[c.index] + b * c.pairs + p
                pe.wait_ge(exp_done, pn + 1)
                if p == 0:
                    at_least(pe, o_done, n)
                    pe.wait_ge(v_out, n + 1)
                for i in range(2):
                    h = 2 * p + i
                    kv = h // (c.heads // c.kv)
                    for qb in range(BLK):
                        keys = [0] if c.causal and qb == 0 else [0, 1]
                        at = (qb * c.heads + h) * (c.hd + 1)
                        for kb in keys:
                            col = qb * P if kb == 0 else S + (qb - (1 if c.causal else 0)) * P
                            last = nc.tensor.matmul(ps_out[:, at:at + c.hd + 1], probs[:, p % 4, i, col:col + P],
                                                    v_tok[c.index][:, r, kb, kv, :], start=(kb == 0),
                                                    stop=(kb == keys[-1]))
                last.then_inc(pv_pair, 1)

            def max_rows(c, b, r, free):
                n, r2 = n_of(c, b), r % 2
                if c.causal:
                    pe.wait_ge(max_all, n + 1)
                else:
                    pe.wait_ge(max_done, HEADS_BEFORE[c.index] + (b + 1) * c.heads)
                pe.wait_ge(*free)
                for k in range(BLK):
                    last = nc.tensor.transpose(ps_work[0:c.heads, k * P:(k + 1) * P],
                                               row_max[:, r2, k, 0:c.heads], ident)
                last.then_inc(mt_mm, 1)

            def start(c):
                free = (rt_ht_out, NB) if c.index == 2 else (y_out, c.first)
                for b in (0, 1):
                    for name in SLOT_STEPS:
                        if name != "qd" or c.index == 0:
                            prep(c, b, b, name, free)
                    free = (sel_out, 4 * n_of(c, b) + 4)
                for h in range(c.heads):
                    max_scores(c, 0, 0, h)
                max_rows(c, 0, 0, free)

            def segment(c, b, r):
                with_post, with_prep, with_next = flags(b)
                free = (mt_out, n_of(c, b) + 1)
                for h, names in enumerate(slots(c, with_post, with_prep)):
                    if with_next:
                        max_scores(c, b + 1, (r + 1) % RING, h)
                    exp_scores(c, b, r, h)
                    if h % 2 and h > 1:
                        values(c, b, r, h // 2 - 1)
                    for name in names:
                        if name in ("ot", "y"):
                            post(c, b - 1, (r - 1) % RING, name, free)
                            free = (y_out, n_of(c, b - 1) + 1)
                        else:
                            prep(c, b + 2, (r + 2) % RING, name, free)
                values(c, b, r, c.pairs - 1)
                if with_next:
                    if with_prep:
                        free = (sel_out, 4 * n_of(c, b + 2) + 4)
                    max_rows(c, b + 1, (r + 1) % RING, free)

            def finish(c):
                for name in ("ot", "y"):
                    post(c, NB - 1, (NB - 1) % RING, name, (y_out, n_of(c, NB - 2) + 1))

            run(pe, CFGS[0], start, segment, finish)
            run(pe, CFGS[1], start, segment, finish)
            pe_moe(pe)
            run(pe, CFGS[2], start, segment, finish)
            pe_route1(pe)


_SHAPES = {"squares": square_constants, "rope": rope_tables, "experts": expert_constants,
           "select": select_constants, "max_select": max_select_constant}
_INS = ["L0_attn_x", "L0_attn_Wq", "L0_attn_Wk", "L0_attn_Wv", "L0_attn_Wo", "L0_attn_head_scales",
        "L0_attn_head_dirs", "L0_ffn_ln1_w", "L0_ffn_ln2_w", "L0_ffn_Wq", "L0_ffn_Wk", "L0_ffn_Wv", "L0_ffn_Wo",
        "L0_ffn_Wr", "L0_ffn_Wg", "L0_ffn_Wu", "L0_ffn_Wd", "L0_c", "L0_wmod", "L1_ffn_Wr", "L1_ffn_W1", "L1_ffn_W2",
        "L1_c", "L1_wmod"]
_TRANSPOSED = ["L1_attn_Wq", "L1_attn_Wk", "L1_attn_Wv", "L1_attn_Wo"]


def kernel(**inputs):
    import numpy as _np
    import concourse.bacc as _bacc
    from concourse import mybir as _mybir
    from concourse.bass_utils import run_bass_kernel_spmd as _run

    nc = _bacc.Bacc("TRN2", target_bir_lowering=False, num_devices=1)
    arrays = {name: _np.ascontiguousarray(inputs[name]) for name in _INS}
    arrays.update({name + "T": _np.ascontiguousarray(_np.asarray(inputs[name]).T) for name in _TRANSPOSED})
    arrays.update({name: make() for name, make in _SHAPES.items()})
    aps = {name: nc.dram_tensor(f"in_{name}", v.shape, _mybir.dt.from_np(v.dtype), kind="ExternalInput").ap()
           for name, v in arrays.items()}
    out = nc.dram_tensor("out_x", (NB, S, D), F32, kind="ExternalOutput").ap()
    adaln_two_layers(nc, aps, out)
    r = _run(nc, [{f"in_{name}": v for name, v in arrays.items()}], core_ids=[0])
    return r.results[0]["out_x"]
```

```python
from contextlib import ExitStack

import numpy as np

import concourse.bass as bass
from concourse import mybir

ALU = mybir.AluOpType
ACT = mybir.ActivationFunctionType
F32 = mybir.dt.float32
F32R = mybir.dt.float32r
BF16 = mybir.dt.bfloat16
I32 = mybir.dt.int32
AX_X = mybir.AxisListType.X

P = 128
D = 128
S = 256
NB = 16
BLK = S // P
TOKENS = NB * S
LN_EPS = 1e-5
MASKED = -1e30
CLIP = 100.0
RSQRT_D = float(D) ** -0.5

E0, F0 = 8, 256
E1, F1 = 8, 512
CAP = TOKENS // E1

RING = 4


class Attn:

    def __init__(self, index, layer, mod, heads, kv, causal, window, scale):
        self.index = index
        self.layer = layer
        self.mod = mod
        self.heads = heads
        self.hd = D // heads
        self.kv = kv
        self.causal = causal
        self.window = window
        self.scale = scale
        self.strip = 32 if self.hd == 8 else 64
        self.per_group = P // self.strip
        self.krows = 3 * self.hd
        self.kind = 0 if self.hd == 16 else 1
        self.pairs = heads // 2
        self.first = NB * index

    def q_cols(self):
        return 384 if self.causal else 512


CFGS = [
    Attn(0, 0, 0, 8, 4, True, True, 1.0),
    Attn(1, 0, 3 * D, 16, 4, True, False, float(1.0 / np.sqrt(np.float32(8.0)))),
    Attn(2, 1, 0, 16, 16, False, False, float(np.sqrt(8.0))),
]
GROUPS = 4
HEADS_BEFORE = [0, NB * 8, NB * 24]
PAIRS_BEFORE = [0, NB * 4, NB * 12]


def rope_tables():
    out = []
    for hd in (16, 8):
        inv = (1.0 / np.float32(10000.0) ** (np.arange(0, hd, 2, dtype=np.float32) / np.float32(hd))).astype(np.float32)
        f = (np.arange(S, dtype=np.float32)[:, None] * inv[None, :]).astype(np.float32)
        c, s = np.cos(f).T, np.sin(f).T
        out.append(np.tile(np.concatenate([c, c]), (D // hd, 1)))
        out.append(np.tile(np.concatenate([-s, s]), (D // hd, 1)))
    return np.stack(out, 1).astype(np.float32)


def square_constants():
    a = np.arange(P)
    row, col = a[:, None], a[None, :]
    causal = np.where(col > row, MASKED, 0.0)
    window = np.where((col < 4) | (col >= row + 1), 0.0, MASKED)
    return np.stack([np.eye(P), causal, window, causal.T, window.T, row < col, np.ones((P, P))], 1).astype(np.float32)


def select_constants():
    out = np.zeros((P, 3, 4, GROUPS, P), np.float32)
    for c in CFGS:
        for g in range(GROUPS):
            for j in range(c.per_group):
                head = g * c.per_group + j
                kv = head // (c.heads // c.kv)
                for d in range(c.hd):
                    for slot, (qp, kp) in enumerate(((0, 0), (0, 1), (1, 0))):
                        row = j * c.strip + slot * c.hd + d
                        out[head * c.hd + d, c.index, qp, g, row] = 1.0
                        out[kv * c.hd + d, c.index, 2 + kp, g, row] = 1.0
    return out


def max_place_constant():
    out = np.zeros((P, 2, GROUPS, P), np.float32)
    for c in CFGS[0:2]:
        for h in range(c.heads):
            row = (h % c.per_group) * c.strip + c.krows
            out[h, c.kind, h // c.per_group, row] = 1.0
            out[32 + h, c.kind, h // c.per_group, row + 1] = 1.0
    return out


def strip_constants():
    out = np.zeros((P, 2, 1 + 4 * 17), np.float32)
    for c in CFGS[0:2]:
        for j in range(c.per_group):
            out[j * c.strip + c.krows:j * c.strip + c.krows + 2, c.kind, 0] = -1.0
        for j in range(4):
            for d in range(c.hd + 1):
                out[j * 32 + d, c.kind, 1 + j * (c.hd + 1) + d] = 1.0
    return out


def expert_constants():
    out = np.zeros((P, 6, 8), np.float32)
    out[:, 0] = 8 - np.arange(8)
    out[:, 1] = CAP * np.arange(8)
    out[:, 2:] = (TOKENS + P * np.arange(NB * BLK)[None, :] + np.arange(P)[:, None]).reshape(P, 4, 8)
    return out


def adaln_two_layers(nc, a, out):
    with ExitStack() as ctx:
        def sb(name, shape, dt=F32):
            return ctx.enter_context(nc.sbuf_tensor(name, shape, dt))

        def psum(name, shape, dt=F32):
            return ctx.enter_context(nc.psum_tensor(name, shape, dt))

        def sem(name):
            return ctx.enter_context(nc.semaphore(name))

        ps_max = psum("ps_max", [P, 2, 512])
        ps_four = psum("ps_four", [P, 4, 512])
        ps_exp = ps_four[:, 0:3, :]
        ps_out = psum("ps_out", [P, 512])
        ps_work = psum("ps_work", [P, 512])
        work = (ps_work[:], ps_four[:, 3, :])

        x_all = sb("x_all", [P, NB * BLK, D])
        res_all = sb("res_all", [P, NB * BLK, D])
        res_words = res_all[:].rearrange("p a d -> p (a d)")
        squares = res_words[:, 0:7 * P].rearrange("p (n m) -> p n m", n=7)
        ident_sb = sb("ident", [P, P])
        ident = ident_sb[:]
        ident_bf = sb("ident_bf", [P, P], BF16)
        masks = sb("masks", [P, 4, P], BF16)
        upper_ones = sb("upper_ones", [P, 2, P], BF16)
        rope = sb("rope", [P, 4, S])
        select = sb("select", [P, 4, GROUPS, P], F32R)
        max_place = sb("max_place", [P, 2, GROUPS, P], F32R)
        strips = sb("strips", [P, 2, 1 + 4 * 17])
        mod_t = sb("mod_t", [P, 2, 2, NB])
        expert_c = sb("expert_c", [P, 6, 8])
        half_neg = sb("half_neg", [P, 2])
        eps = sb("eps", [P, 2])
        one = sb("one", [P, 1])
        ln_w = sb("ln_w", [P, 2])
        silu_c = sb("silu_c", [P, 2, NB])
        c_rows = res_words[0:NB, 7 * P:9 * P].rearrange("p (n m) -> p n m", n=2)
        wmod = sb("wmod", [P, 2, 6 * D])
        wq = sb("wq", [P, 3, 2, D])
        kv_cols = [c.kv * c.hd for c in CFGS]
        wk_all = sb("wk_all", [P, 2 * sum(kv_cols)])
        wv_all = sb("wv_all", [P, sum(kv_cols)])
        wk = [wk_all[:, 2 * sum(kv_cols[:i]):2 * sum(kv_cols[:i + 1])].rearrange("p (t m) -> p t m", t=2)
              for i in range(3)]
        wv = [wv_all[:, sum(kv_cols[:i]):sum(kv_cols[:i + 1])] for i in range(3)]
        wo = sb("wo", [P, 3, D])
        dirs = sb("dirs", [8, 4])
        dir_rows = res_words[0:8, 9 * P:11 * P].rearrange("p (n m) -> p n m", n=2)
        dir_mix = sb("dir_mix", [P, D])
        wr = sb("wr", [P, 2, 8])
        wgu = sb("wgu", [P, 2, E0, F0])
        wg, wu = wgu[:, 0], wgu[:, 1]
        wd = sb("wd", [P, E0, F0 // P, D])

        c_bcast = sb("c_bcast", [P, 2, P])
        mod = sb("mod", [P, RING, 3, D])
        gate_tmp = sb("gate_tmp", [P, 2, D])
        stats6 = sb("stats6", [P, 2, BLK, 6])
        mean_var = sb("mean_var", [P, 2, BLK, 2])
        var_eps = sb("var_eps", [P, 2, BLK])
        rstd = sb("rstd", [P, 2, BLK])
        h_tok = sb("h_tok", [P, RING, BLK, D])
        ssq = sb("ssq", [P, 2, BLK])
        ssq_eps = sb("ssq_eps", [P, 2, BLK])
        rrms = sb("rrms", [P, 2, BLK])
        h_both = sb("h_both", [P, 2, 2, S])
        hn_tok = h_both[:, 0].rearrange("p a (k d) -> p a k d", d=D)
        h_t = h_both[:, 1]
        rope_ab = sb("rope_ab", [P, 2, 2, S])
        rope_a, rope_b = rope_ab[:, 0], rope_ab[:, 1]
        split = sb("split", [P, 2, 2, S], F32R)
        q_st = sb("q_st", [P, RING, GROUPS, S], F32R)
        k_st = sb("k_st", [P, RING, GROUPS, S], F32R)
        v_all = sb("v_all", [P, RING * BLK * 16 * 9])
        v_tok = [v_all[:, 0:RING * BLK * c.kv * (c.hd + 1)].rearrange(
            "p (r k h e) -> p r k h e", r=RING, k=BLK, h=c.kv) for c in CFGS]
        row_max = sb("row_max", [P, 2, 3, 16])
        max_t = sb("max_t", [P, 2, S], F32R)
        attn_f32 = sb("attn_f32", [P, 4, 2, 512])
        probs = attn_f32[:, 0:2].rearrange("p a b c -> p (a b) c")
        o_strips = attn_f32[:, 2]
        recip = sb("recip", [P, 2, BLK * 16])
        o_both = sb("o_both", [P, 2, 2, S])
        o_tok = o_both[:, 0].rearrange("p a (k d) -> p a k d", d=D)
        o_t = o_both[:, 1]
        y_tok = sb("y_tok", [P, 2, BLK, D])

        zeros = attn_f32[:, 0, 0, :]

        ht_all = attn_f32[:].rearrange("p a b c -> p (a b c)")
        gates_all = sb("gates_all", [P, NB, D])
        stage = gates_all[:].rearrange("p b d -> p (b d)")
        logits = rope_b[:].rearrange("p a s -> p (a s)")[:, 0:NB * BLK * 8].rearrange("p (k e) -> p k e", e=8)
        rt = mod[:].rearrange("p r a d -> p (r a d)").rearrange("p (n k e) -> p n k e", n=6, e=8)
        rt1 = sb("rt1", [P, 12, NB * BLK])
        one_hot = sb("one_hot", [P, NB * BLK, 8], BF16)
        slot_put = sb("slot_put", [P, NB * BLK], I32)
        slot_get = sb("slot_get", [P, NB * BLK], I32)
        weight_t = sb("weight_t", [P, 4, 8])
        tanh_g = h_tok[:].rearrange("p a b c -> p (a b c)").rearrange("p (s t) -> p s t", s=2)
        gated = rope_ab[:].rearrange("p a b c -> p (a b c)").rearrange("p (s t) -> p s t", s=2)
        act_t = o_both[:].rearrange("p a b c -> p (a b c)").rearrange("p (s t) -> p s t", s=2)
        acc = y_tok[:].rearrange("p a k d -> p (a k) d")
        moe_y = h_both[:].rearrange("p s a (k d) -> p s (a k) d", d=D)
        w12 = wd[:].rearrange("p e c d -> p (e c d)")
        w1 = w12[:, 0:2 * F1].rearrange("p (s f) -> p s f", s=2)
        w2 = w12[:, 2 * F1:].rearrange("p (s f d) -> p s f d", s=2, f=F1 // P)
        rows_e = tanh_g.rearrange("p s (k d) -> p s k d", d=D)
        rows_t = gated
        hid_t = wgu[:].rearrange("p a e f -> p (a e f)").rearrange("p (s f t) -> p s f t", s=2, f=F1 // P)
        y_rows = act_t.rearrange("p s (k d) -> p s k d", d=D)
        y_all = attn_f32[:].rearrange("p a b (c d) -> p (a b c) d", d=D)
        slots_dram = nc.dram_tensor("slots_dram", [2 * TOKENS, D], F32, kind="Internal").ap()
        y_dram = nc.dram_tensor("y_dram", [TOKENS, D], F32, kind="Internal").ap()

        loads = sem("loads")
        x_load = sem("x_load")
        sel_load = sem("sel_load")
        select_ready = sem("select_ready")
        zeros_ready = sem("zeros_ready")
        ones_ready = sem("ones_ready")
        folded = sem("folded")
        rotated = sem("rotated")
        zero_store = sem("zero_store")
        pro_dve = sem("pro_dve")
        pro_pe = sem("pro_pe")
        pro_act = sem("pro_act")
        x_done = sem("x_done")
        res_done = sem("res_done")
        c_bcast_done = sem("c_bcast_done")
        mod_mm = sem("mod_mm")
        mod_out = sem("mod_out")
        mod_scale = sem("mod_scale")
        gate_a = sem("gate_a")
        gate_b = sem("gate_b")
        gate_done = sem("gate_done")
        stats_done = sem("stats_done")
        mv_done = sem("mv_done")
        var_done = sem("var_done")
        rstd_done = sem("rstd_done")
        xhat_done = sem("xhat_done")
        h_mul = sem("h_mul")
        h_done = sem("h_done")
        ssq_done = sem("ssq_done")
        ssq_eps_done = sem("ssq_eps_done")
        rrms_done = sem("rrms_done")
        hn_done = sem("hn_done")
        ht_mm = sem("ht_mm")
        ht_out = sem("ht_out")
        q_mm = sem("q_mm")
        q_rope = sem("q_rope")
        q_sum = sem("q_sum")
        qd_mm = sem("qd_mm")
        q_hi = sem("q_hi")
        q_lo = sem("q_lo")
        k_mm = sem("k_mm")
        k_rope = sem("k_rope")
        k_sum = sem("k_sum")
        k_lo = sem("k_lo")
        v_mm = sem("v_mm")
        v_out = sem("v_out")
        sel_mm = sem("sel_mm")
        sel_out = sem("sel_out")
        max_mm = sem("max_mm")
        max_done = sem("max_done")
        max_all = sem("max_all")
        mt_mm = sem("mt_mm")
        mt_hi = sem("mt_hi")
        mt_out = sem("mt_out")
        exp_mm = sem("exp_mm")
        exp_done = sem("exp_done")
        values_mm = sem("values_mm")
        strips_out = sem("strips_out")
        combined = sem("combined")
        place_mm = sem("place_mm")
        place_done = sem("place_done")
        recip_done = sem("recip_done")
        o_done = sem("o_done")
        ot_mm = sem("ot_mm")
        ot_out = sem("ot_out")
        y_mm = sem("y_mm")
        y_out = sem("y_out")  

        moe_done = sem("moe_done")
        rt_bcast = sem("rt_bcast")
        rt_mod_mm = sem("rt_mod_mm")
        rt_mod_out = sem("rt_mod_out")
        rt_mod_scale = sem("rt_mod_scale")
        rt_gate_a = sem("rt_gate_a")
        rt_gate_b = sem("rt_gate_b")
        rt_gate = sem("rt_gate")
        rt_stats = sem("rt_stats")
        rt_mv = sem("rt_mv")
        rt_var = sem("rt_var")
        rt_rstd = sem("rt_rstd")
        rt_xhat = sem("rt_xhat")
        rt_mul = sem("rt_mul")
        rt_h = sem("rt_h")
        rt_kept = sem("rt_kept")
        rt_ssq = sem("rt_ssq")
        rt_ht_mm = sem("rt_ht_mm")
        rt_ht_out = sem("rt_ht_out")
        rt_logit_mm = sem("rt_logit_mm")
        rt_logit = sem("rt_logit")
        rt_chain = sem("rt_chain")
        rt_diff = sem("rt_diff")
        rt_exp = sem("rt_exp")
        rt_onehot = sem("rt_onehot")
        rt_rank_mm = sem("rt_rank_mm")
        routed = sem("routed")
        gu_mm = sem("gu_mm")
        tanh_done = sem("tanh_done")
        gated_done = sem("gated_done")
        act_done = sem("act_done")
        down_mm = sem("down_mm")
        weight_done = sem("weight_done")
        acc_done = sem("acc_done")
        moe_sum = sem("moe_sum")
        moe_clip = sem("moe_clip")
        moe_gated = sem("moe_gated")
        scattered = sem("scattered")
        ffn_load = [sem("ffn_load0"), sem("ffn_load1")]
        xt_mm = sem("xt_mm")
        xt_out = sem("xt_out")
        up_mm = sem("up_mm")
        relu_done = sem("relu_done")
        ffn_mm = sem("ffn_mm")
        ffn_out = sem("ffn_out")
        ffn_store = [sem("ffn_store0"), sem("ffn_store1")]
        gathered = sem("gathered")
        y_gated = sem("y_gated")
        final_done = sem("final_done")
        out_store = sem("out_store")

        X = a["L0_attn_x"].rearrange("b (k p) d -> p (b k) d", p=P)
        OUT = out.rearrange("b (k p) d -> p (b k) d", p=P)
        dma_list = [
            (squares, a["squares"]), (ident, a["squares"][:, 0, :]), (rope[:], a["rope"]), (expert_c[:], a["experts"]),
            (strips[:], a["strips"]),
            (c_rows[:, 0, :], a["L0_c"]), (c_rows[:, 1, :], a["L1_c"]),
            (wmod[:, 0, :], a["L0_wmod"]), (wmod[:, 1, :], a["L1_wmod"]),
            (wq[:, 0, 0, :], a["L0_attn_Wq"]), (wk[0][:, 0, :], a["L0_attn_Wk"]),
            (wv[0], a["L0_attn_Wv"]), (wo[:, 0, :], a["L0_attn_Wo"]),
            (dirs[:, 0:3], a["L0_attn_head_dirs"]),
            (dirs[:, 3:4], a["L0_attn_head_scales"].rearrange("(h o) -> h o", o=1)),
            (wq[:, 1, 0, :], a["L0_ffn_Wq"]), (wk[1][:, 0, :], a["L0_ffn_Wk"]),
            (wv[1], a["L0_ffn_Wv"]), (wo[:, 1, :], a["L0_ffn_Wo"]),
            (ln_w[:, 0:1], a["L0_ffn_ln1_w"].rearrange("(h o) -> h o", o=1)),
            (ln_w[:, 1:2], a["L0_ffn_ln2_w"].rearrange("(h o) -> h o", o=1)),
            (wq[:, 2, 0, :], a["L1_attn_WqT"]), (wk[2][:, 0, :], a["L1_attn_WkT"]),
            (wv[2], a["L1_attn_WvT"]), (wo[:, 2, :], a["L1_attn_WoT"]),
            (wr[:, 0, :], a["L0_ffn_Wr"]), (wr[:, 1, :], a["L1_ffn_Wr"]),
            (wg, a["L0_ffn_Wg"].rearrange("e d f -> d e f")),
            (wu, a["L0_ffn_Wu"].rearrange("e d f -> d e f")),
            (wd[:], a["L0_ffn_Wd"].rearrange("e (c p) d -> p e c d", p=P)),
        ]
        N_LOADS = len(dma_list)

        def n_of(c, b):
            return b + c.first

        PREP = ["mod", "ht", "q", "k", "qd", "v", "sel0", "sel1", "sel2", "sel3"]
        POST = ["combine", "ot", "y"]
        MAXIMA = ["rows", "place0", "place1"]
        BANK = {"mod": 0, "combine": 1, "ot": 0, "ht": 1, "y": 0, "q": 1, "k": 0, "qd": 1, "v": 0,
                "sel0": 1, "sel1": 0, "sel2": 1, "sel3": 0, "rows": 1, "place0": 0, "place1": 1}

        def slots(c, with_post, with_prep, with_next):
            prep = [n for n in PREP if n != "qd" or c.index == 0]
            names = ["mod", "combine", "ot", "ht", "y"] + prep[2:] + MAXIMA
            early = 3 * c.heads // 4
            table = [([], [], []) for _ in range(c.heads)]
            if with_next:
                for h in range(c.heads):
                    table[h * early // c.heads][0].append(h)
            for j, name in enumerate(names):
                at = 3 + j * (2 * c.heads - 3) // len(names)
                if (name in POST and with_post) or (name in prep and with_prep) or (name in MAXIMA and with_next):
                    table[at // 2][1 + at % 2].append(name)
            return table

        def walk(c, b, r, post, prep, maxima, names):
            for name in names:
                if name in POST:
                    post(c, b - 1, (r - 1) % RING, name)
                elif name in MAXIMA:
                    maxima(c, b + 1, (r + 1) % RING, name)
                else:
                    prep(c, b + 2, (r + 2) % RING, name)

        def at_least(eng, semaphore, value):
            if not isinstance(value, int) or value > 0:
                eng.wait_ge(semaphore, value)

        def n_of(c, b):
            return b + c.first

        def pairs_until(c, b):
            if isinstance(b, int) and b < 0:
                return PAIRS_BEFORE[c.index]
            return (b + 1) * c.pairs + PAIRS_BEFORE[c.index]

        def run(eng, c, start, segment, finish):
            start(c)
            segment(c, 0, 0)
            with eng.Fori(0, (NB - RING) // RING) as g:
                for r in range(RING):
                    segment(c, g * RING + (1 + r), (1 + r) % RING)
            for b in range(NB - RING + 1, NB):
                segment(c, b, b % RING)
            finish(c)

        def heads_until(c, b):
            if isinstance(b, int) and b < 0:
                return HEADS_BEFORE[c.index]
            return (b + 1) * c.heads + HEADS_BEFORE[c.index]

        def v_in_work(c):
            return work[BANK["v"]][:, 0:S].rearrange("p (k c) -> p k c", k=BLK)[:, :, 0:c.kv * c.hd].rearrange(
                "p k (h e) -> p k h e", e=c.hd)

        def flags(b):
            if not isinstance(b, int):
                return True, True, True
            return b > 0, b + 2 < NB, b + 1 < NB

        block = ctx.enter_context(nc.Block())

        def block_of(x, i):
            return x[:, bass.ds(i, 1), :].rearrange("p o d -> p (o d)")

        def entries(eng, f):
            for b in range(2):
                f(b, b)
            with eng.Fori(0, NB // 2 - 1) as g:
                for r in range(2):
                    f(g * 2 + (2 + r), r)

        def sp_tail(sp):
            def load(e, s):
                at_least(sp, ffn_mm, e - 1)
                at_least(sp, xt_mm, e - 1)
                sp.dma_start(w1[:, s, :], a["L1_ffn_W1"][bass.ds(e, 1), :, :].rearrange("o d f -> d (o f)")
                             ).then_inc(ffn_load[s], 16)
                sp.dma_start(w2[:, s], a["L1_ffn_W2"][bass.ds(e, 1), :, :].rearrange("o (c p) d -> p (o c) d", p=P)
                             ).then_inc(ffn_load[s], 16)
                sp.dma_start(rows_e[:, s].rearrange("p k d -> p (k d)"),
                             slots_dram[bass.ds(e * CAP, CAP), :].rearrange("(p k) d -> p (k d)", p=P)
                             ).then_inc(ffn_load[s], 16)

            def store(e, s):
                sp.wait_ge(ffn_out, e + 1)
                sp.dma_start(y_dram[bass.ds(e * CAP, CAP), :].rearrange("(p k) d -> p (k d)", p=P),
                             y_rows[:, s].rearrange("p k d -> p (k d)")).then_inc(ffn_store[s], 16)

            sp.wait_ge(values_mm, heads_until(CFGS[2], NB - 1))
            sp.wait_ge(scattered, 16 * NB * BLK)
            load(0, 0)
            load(1, 1)
            with sp.Fori(0, E1 // 2 - 1) as g:
                for s in range(2):
                    store(g * 2 + s, s)
                    load(g * 2 + (2 + s), s)
            store(E1 - 2, 0)
            store(E1 - 1, 1)

            def put(b):
                sp.wait_ge(final_done, b + 1)
                sp.dma_start(OUT[:, bass.ds(b * BLK, BLK), :], x_all[:, bass.ds(b * BLK, BLK), :]
                             ).then_inc(out_store, 16)

            with sp.Fori(0, NB) as b:
                put(b)
            sp.wait_ge(out_store, 16 * NB)

        def pool_route(pool, layer):
            def entry(b, r2):
                n = layer * NB + b
                if layer == 0:
                    pool.wait_ge(rt_ssq, b + 1)
                    nc.gpsimd.tensor_tensor(var_eps[:, r2, :], ssq[:, r2, :], eps[:], ALU.add).then_inc(rt_var, 1)
                else:
                    pool.wait_ge(rt_mv, b + 1)
                    nc.gpsimd.tensor_tensor(var_eps[:, r2, :], mean_var[:, r2, :, 1], eps[:], ALU.add
                                            ).then_inc(rt_var, 1)
                pool.wait_ge(rt_var, n + 1)
                nc.gpsimd.tensor_tensor(rstd[:, r2, :], var_eps[:, r2, :], half_neg[:],
                                        ALU.pow).then_inc(rt_rstd, 1)
                if layer == 1:
                    pool.wait_ge(rt_mod_out, n + 1)
                    nc.gpsimd.tensor_tensor(mod[:, r2, 1, :], mod[:, r2, 1, :], one[:].to_broadcast([P, D]),
                                            ALU.add).then_inc(rt_mod_scale, 1)
                    pool.wait_ge(rt_mul, n + 1)
                    nc.gpsimd.tensor_tensor(h_tok[:, r2], h_tok[:, r2], mod[:, r2, 0:1, :].to_broadcast([P, BLK, D]),
                                            ALU.add).then_inc(rt_h, 1)
            entries(pool, entry)

        def pool_moe(pool):
            pool_route(pool, 0)

            def chunk(t, s):
                pool.wait_ge(moe_gated, t + 1)
                xs = x_all[:, bass.ds(t * 4, 4), :]
                nc.gpsimd.tensor_tensor(xs, xs, moe_y[:, s], ALU.add).then_inc(moe_done, 1)

            with pool.Fori(0, NB // 4) as g:
                for s in range(2):
                    chunk(g * 2 + s, s)

        def pool_route1(pool):
            pool_route(pool, 1)
            pool.wait_ge(routed, 1)
            pool.wait_ge(zero_store, 16 * 8)
            pool.wait_ge(rt_kept, NB)
            for k in range(NB * BLK):
                nc.gpsimd.indirect_dma_start(slots_dram[:], bass.IndirectOffsetOnAxis(ap=slot_put[:, k:k + 1], axis=0),
                                             res_all[:, k, :], None).then_inc(scattered, 16)
            for s in range(2):
                pool.wait_ge(ffn_store[s], 16 * (E1 // 2))
            for k in range(NB * BLK):
                nc.gpsimd.indirect_dma_start(y_all[:, k, :], None, y_dram[:],
                                             bass.IndirectOffsetOnAxis(ap=slot_get[:, k:k + 1], axis=0)
                                             ).then_inc(gathered, 16)

        def act_prologue(act):
            act.wait_ge(pro_pe, 1)
            nc.scalar.activation(rt[:, 0, 0:2 * NB // 8, :].rearrange("p a b -> p (a b)"), ps_work[:, 0:2 * NB],
                                 ACT.Exp, scale=-1.0).then_inc(pro_act, 1)

        def act_route(act, layer):
            def entry(b, r2):
                n = layer * NB + b
                act.wait_ge(rt_mod_mm, n + 1)
                at_least(act, rt_gate, n - 1)
                if layer == 1:
                    at_least(act, rt_h, b - 1)
                if layer == 0 and isinstance(b, int) and b == 0:
                    act.wait_ge(y_out, 2 * NB)
                if layer == 1 and isinstance(b, int) and b == 0:
                    act.wait_ge(y_out, 3 * NB)
                nc.scalar.copy(mod[:, r2].rearrange("p a d -> p (a d)"), ps_work[:, 0:3 * D]).then_inc(rt_mod_out, 1)
                if layer == 0:
                    act.wait_ge(res_done, b + 1)
                    at_least(act, rt_ht_mm, n - 1)
                    for k in range(BLK):
                        last = nc.scalar.activation(hn_tok[:, r2, k, :], block_of(res_all, b * BLK + k),
                                                    ACT.Square, scale=RSQRT_D, accum_out=ssq[:, r2, k:k + 1])
                    last.then_inc(rt_ssq, 1)
                act.wait_ge(rt_ht_mm, n + 1)
                at_least(act, rt_logit_mm, n - 1)
                if layer == 0:
                    nc.scalar.copy(ht_all[:, bass.ds(b * S, S)], ps_work[:, 0:S])
                nc.scalar.copy(h_t[:, r2, :], ps_work[:, 0:S]).then_inc(rt_ht_out, 1)
                if layer == 1:
                    nc.scalar.copy(res_all[:, bass.ds(b * BLK, BLK), :], h_tok[:, r2]).then_inc(rt_kept, 1)
                act.wait_ge(rt_logit_mm, n + 1)
                nc.scalar.copy(logits[:, bass.ds(b * BLK, BLK), :],
                               ps_out[:, 0:BLK * 8].rearrange("p (k e) -> p k e", e=8)).then_inc(rt_logit, 1)
            entries(act, entry)
            act.wait_ge(rt_diff, layer + 1)
            nc.scalar.activation(rt[:, 1], rt[:, 0], ACT.Exp).then_inc(rt_exp, 1)

        def act_moe(act):
            act_route(act, 0)

            def chunk(t):
                for u in range(2 * E0):
                    n = t * 2 * E0 + u
                    act.wait_ge(gu_mm, n + 1)
                    at_least(act, gated_done, n - 1)
                    nc.scalar.activation(tanh_g[:, u % 2, :], ps_four[:, 2 * (u % 2), :], ACT.Tanh,
                                         scale=0.5).then_inc(tanh_done, 1)
            chunk(0)
            with act.Fori(0, TOKENS // 512 - 1) as g:
                chunk(g + 1)

        def act_route1(act):
            act_route(act, 1)

            def expert(e, s):
                act.wait_ge(xt_mm, e + 1)
                at_least(act, up_mm, 4 * e - 4)
                nc.scalar.copy(rows_t[:, s, :], ps_work[:]).then_inc(xt_out, 1)
                for f in range(F1 // P):
                    act.wait_ge(up_mm, 4 * e + f + 1)
                    at_least(act, ffn_mm, e - 1)
                    nc.scalar.activation(hid_t[:, s, f, :], ps_four[:, f, :], ACT.Relu
                                         ).then_inc(relu_done, 1)
            for e in range(2):
                expert(e, e)
            with act.Fori(0, E1 // 2 - 1) as g:
                for s in range(2):
                    expert(g * 2 + (2 + s), s)

        def dve_prologue(dve):
            nc.vector.memset(dir_rows[:], 0.0).then_inc(pro_dve, 1)
            dve.wait_ge(loads, 16 * N_LOADS)
            dve.wait_ge(pro_dve, 1)
            nc.vector.tensor_tensor(dir_rows[:, 0, :].rearrange("p (h e) -> p h e", e=16)[:, :, 0:3],
                                    ident[0:8, 0:8].unsqueeze(2).to_broadcast([8, 8, 3]),
                                    dirs[:, 0:3].unsqueeze(1).to_broadcast([8, 8, 3]), ALU.mult).then_inc(pro_dve, 1)
            dve.wait_ge(pro_dve, 2)
            nc.vector.tensor_scalar(dir_rows[:, 1, :], dir_rows[:, 0, :], dirs[:, 3:4], None,
                                    ALU.mult).then_inc(pro_dve, 1)
            dve.wait_ge(pro_act, 1)
            e = rt[:, 0, 0:2 * NB // 8, :].rearrange("p a b -> p (a b)")
            nc.vector.tensor_scalar(e, e, 1.0, None, ALU.add).then_inc(pro_dve, 1)
            dve.wait_ge(pro_dve, 4)
            nc.vector.reciprocal(e, e).then_inc(pro_dve, 1)
            dve.wait_ge(pro_dve, 5)
            nc.vector.tensor_tensor(silu_c[:].rearrange("p l b -> p (l b)"), ps_work[:, 0:2 * NB], e,
                                    ALU.mult).then_inc(pro_dve, 1)
            dve.wait_ge(pro_dve, 6)
            dve.wait_ge(pro_pe, 2)
            nc.vector.scalar_tensor_tensor(dir_mix[:], ident, 0.25, ps_work[:, P:2 * P], ALU.mult,
                                           ALU.add).then_inc(pro_dve, 1)
            dve.wait_ge(pro_pe, 3)
            both = ps_work[:, 0:4 * NB].rearrange("p (l k b) -> p l k b", l=2, k=2)
            nc.vector.tensor_copy(mod_t[:, :, 0, :], both[:, :, 0, :])
            nc.vector.tensor_scalar(mod_t[:, :, 1, :], both[:, :, 1, :], 1.0, None, ALU.add).then_inc(pro_dve, 1)
            nc.vector.memset(o_strips, 0.0).then_inc(pro_dve, 1)

        chain = [0]

        def dve_route(dve, layer):
            def entry(b, r2):
                n = layer * NB + b
                if layer == 1:
                    dve.wait_ge(x_done, NB + b + 1)
                    for k in range(BLK):
                        last = nc.vector.bn_stats(stats6[:, r2, k, :], block_of(x_all, b * BLK + k))
                    last.then_inc(rt_stats, 1)
                    dve.wait_ge(rt_stats, b + 1)
                    at_least(dve, rt_mod_mm, n - 1)
                    if isinstance(b, int) and b < 2:
                        dve.wait_ge(mod_mm, (3 if layer else 2) * NB)
                    nc.vector.tensor_copy(c_bcast[:, r2, :], silu_c[:, layer, bass.ds(b, 1)].to_broadcast([P, P])
                                          ).then_inc(rt_bcast, 1)
                    for k in range(BLK):
                        last = nc.vector.bn_aggr(mean_var[:, r2, k, :], stats6[:, r2, k, :])
                    last.then_inc(rt_mv, 1)
                else:
                    at_least(dve, rt_mod_mm, n - 1)
                    if isinstance(b, int) and b < 2:
                        dve.wait_ge(mod_mm, (3 if layer else 2) * NB)
                    nc.vector.tensor_copy(c_bcast[:, r2, :], silu_c[:, layer, bass.ds(b, 1)].to_broadcast([P, P])
                                          ).then_inc(rt_bcast, 1)
                dve.wait_ge(rt_mod_out, n + 1)
                nc.vector.tensor_scalar(gate_tmp[:, 0, :], mod[:, r2, 2, :], 0.0, 0.5, ALU.is_ge, ALU.subtract)
                nc.vector.scalar_tensor_tensor(gate_tmp[:, 1, :], mod[:, r2, 2, :], -1.0, mod[:, r2, 2, :],
                                               ALU.mult, ALU.max).then_inc(rt_gate_a, 1)
                dve.wait_ge(rt_gate_a, n + 1)
                nc.vector.tensor_scalar(gate_tmp[:, 1, :], gate_tmp[:, 1, :], 0.25, 2.0, ALU.max, ALU.mult).then_inc(rt_gate_b, 1)
                dve.wait_ge(rt_gate_b, n + 1)
                nc.vector.tensor_tensor(block_of(gates_all, b), gate_tmp[:, 0, :], gate_tmp[:, 1, :], ALU.mult).then_inc(rt_gate, 1)
                dve.wait_ge(rt_rstd, n + 1)
                if layer == 0:
                    at_least(dve, rt_ht_mm, n - 1)
                    for k in range(BLK):
                        last = nc.vector.tensor_scalar(hn_tok[:, r2, k, :], block_of(res_all, b * BLK + k),
                                                       rstd[:, r2, k:k + 1], None, ALU.mult)
                    last.then_inc(rt_mul, 1)
                else:
                    for k in range(BLK):
                        last = nc.vector.tensor_scalar(hn_tok[:, r2, k, :], block_of(x_all, b * BLK + k),
                                                       mean_var[:, r2, k, 0:1], rstd[:, r2, k:k + 1],
                                                       ALU.subtract, ALU.mult)
                    last.then_inc(rt_xhat, 1)
                    dve.wait_ge(rt_xhat, b + 1)
                    dve.wait_ge(rt_mod_scale, b + 1)
                    at_least(dve, rt_ht_mm, n - 1)
                    at_least(dve, rt_kept, b - 1)
                    nc.vector.tensor_tensor(h_tok[:, r2], hn_tok[:, r2], mod[:, r2, 1:2, :].to_broadcast([P, BLK, D]),
                                            ALU.mult).then_inc(rt_mul, 1)
            entries(dve, entry)

            def link(ins):
                chain[0] += 1
                ins.then_inc(rt_chain, 1)
                dve.wait_ge(rt_chain, chain[0])

            shape = [P, NB * BLK, 8]

            def wide(x):
                return x.unsqueeze(2).to_broadcast(shape)

            index_down = expert_c[:, 0:1, :].to_broadcast(shape)

            def first_of(prob, best, hot):
                link(nc.vector.tensor_reduce(best, prob, AX_X, ALU.max))
                link(nc.vector.tensor_tensor(rt[:, 3], prob, wide(best), ALU.is_equal))
                link(nc.vector.tensor_tensor(rt[:, 3], rt[:, 3], index_down, ALU.mult))
                link(nc.vector.tensor_reduce(rt1[:, 5, :], rt[:, 3], AX_X, ALU.max))
                link(nc.vector.tensor_tensor(hot, rt[:, 3], wide(rt1[:, 5, :]), ALU.is_equal))

            dve.wait_ge(rt_logit, (layer + 1) * NB)
            link(nc.vector.tensor_reduce(rt1[:, 0, :], logits, AX_X, ALU.max))
            nc.vector.tensor_tensor(rt[:, 0], logits, wide(rt1[:, 0, :]), ALU.subtract).then_inc(rt_diff, 1)
            dve.wait_ge(rt_exp, layer + 1)
            link(nc.vector.tensor_reduce(rt1[:, 1, :], rt[:, 1], AX_X, ALU.add))
            link(nc.vector.reciprocal(rt1[:, 2, :], rt1[:, 1, :]))
            link(nc.vector.tensor_tensor(rt[:, 1], rt[:, 1], wide(rt1[:, 2, :]), ALU.mult))
            first_of(rt[:, 1], rt1[:, 3, :], rt[:, 2])
            if layer == 0:
                link(nc.vector.scalar_tensor_tensor(rt[:, 4], rt[:, 2], -2.0, rt[:, 1], ALU.mult, ALU.add))
                first_of(rt[:, 4], rt1[:, 4, :], rt[:, 5])
                link(nc.vector.tensor_tensor(rt[:, 2], rt[:, 2], rt[:, 5], ALU.add))
                link(nc.vector.tensor_tensor(rt[:, 2], rt[:, 2], rt[:, 1], ALU.mult))
                link(nc.vector.tensor_reduce(rt1[:, 6, :], rt[:, 2], AX_X, ALU.add))
                link(nc.vector.reciprocal(rt1[:, 7, :], rt1[:, 6, :]))
                link(nc.vector.scalar_tensor_tensor(rt[:, 2], rt[:, 2], 0.5, wide(rt1[:, 7, :]), ALU.mult, ALU.mult))
                return
            nc.vector.tensor_copy(one_hot[:], rt[:, 2]).then_inc(rt_onehot, 1)
            dve.wait_ge(rt_rank_mm, 1)
            n = NB * BLK
            earlier = ps_max[:, 0, 0:n * 8].rearrange("p (k e) -> p k e", e=8)
            counts = ps_max[:, 1, 0:n * 8].rearrange("p (k e) -> p k e", e=8)
            link(nc.vector.tensor_copy(rt[:, 3], counts))
            src, dst = 3, 4
            shift = 1
            while shift < n:
                link(nc.vector.tensor_copy(rt[:, dst, 0:shift], rt[:, src, 0:shift]))
                link(nc.vector.tensor_tensor(rt[:, dst, shift:], rt[:, src, shift:], rt[:, src, 0:n - shift], ALU.add))
                src, dst = dst, src
                shift *= 2
            link(nc.vector.tensor_tensor(rt[:, src], rt[:, src], counts, ALU.subtract))
            link(nc.vector.tensor_tensor(rt[:, src], rt[:, src], earlier, ALU.add))
            link(nc.vector.tensor_tensor(rt[:, src], rt[:, src], rt[:, 2], ALU.mult))
            link(nc.vector.tensor_reduce(rt1[:, 6, :], rt[:, src], AX_X, ALU.add))
            link(nc.vector.tensor_tensor(rt[:, 5], rt[:, 2], expert_c[:, 1:2, :].to_broadcast(shape), ALU.mult))
            link(nc.vector.tensor_reduce(rt1[:, 7, :], rt[:, 5], AX_X, ALU.add))
            token = expert_c[:, 2:6, :].rearrange("p a b -> p (a b)")
            link(nc.vector.tensor_scalar(rt1[:, 8, :], rt1[:, 6, :], float(CAP), None, ALU.is_lt))
            link(nc.vector.tensor_tensor(rt1[:, 7, :], rt1[:, 7, :], rt1[:, 6, :], ALU.add))
            link(nc.vector.tensor_tensor(rt1[:, 9, :], rt1[:, 7, :], token, ALU.subtract))
            link(nc.vector.tensor_tensor(rt1[:, 9, :], rt1[:, 9, :], rt1[:, 8, :], ALU.mult))
            link(nc.vector.tensor_tensor(slot_put[:], rt1[:, 9, :], token, ALU.add))
            link(nc.vector.tensor_tensor(slot_get[:], rt1[:, 7, :], rt1[:, 8, :], ALU.mult))
            nc.vector.tensor_tensor(rt1[:, 3, :], rt1[:, 3, :], rt1[:, 8, :], ALU.mult).then_inc(routed, 1)

        def dve_moe(dve):
            dve_route(dve, 0)

            def chunk(t, s):
                last = t * 2 * E0

                def unit(u):
                    n = t * 2 * E0 + u
                    dve.wait_ge(tanh_done, n + 1)
                    nc.vector.scalar_tensor_tensor(gated[:, u % 2, :], tanh_g[:, u % 2, :], 1.0,
                                                   ps_four[:, 2 * (u % 2), :], ALU.add, ALU.mult).then_inc(gated_done, 1)
                    dve.wait_ge(gated_done, n + 1)
                    at_least(dve, down_mm, n - 1)
                    nc.vector.tensor_tensor(act_t[:, u % 2, :], gated[:, u % 2, :], ps_four[:, 2 * (u % 2) + 1, :],
                                            ALU.mult).then_inc(act_done, 1)

                def accumulate(e):
                    n = t * E0 + e
                    dve.wait_ge(down_mm, 2 * n + 2)
                    at_least(dve, acc_done, n)
                    if e == 0:
                        dve.wait_ge(weight_done, t + 1)
                        at_least(dve, moe_sum, t)
                    for k in range(4):
                        y = ps_max[:, e % 2, k * D:(k + 1) * D]
                        if e == 0:
                            ins = nc.vector.tensor_scalar(acc[:, k, :], y, weight_t[:, k, e:e + 1], None, ALU.mult)
                        else:
                            ins = nc.vector.scalar_tensor_tensor(acc[:, k, :], y, weight_t[:, k, e:e + 1],
                                                                 acc[:, k, :], ALU.mult, ALU.add)
                    ins.then_inc(acc_done, 1)

                at_least(dve, acc_done, t * E0)
                nc.vector.tensor_copy(weight_t[:], rt[:, 2, bass.ds(t * 4, 4), :]).then_inc(weight_done, 1)
                for e in range(E0):
                    unit(2 * e)
                    if e > 0:
                        accumulate(e - 1)
                    unit(2 * e + 1)
                accumulate(E0 - 1)
                dve.wait_ge(acc_done, (t + 1) * E0)
                at_least(dve, moe_done, t - 1)
                nc.vector.tensor_tensor(moe_y[:, s], acc[:], res_all[:, bass.ds(t * 4, 4), :], ALU.add
                                        ).then_inc(moe_sum, 1)
                dve.wait_ge(moe_sum, t + 1)
                nc.vector.tensor_scalar(moe_y[:, s], moe_y[:, s], CLIP, -CLIP, ALU.min, ALU.max
                                        ).then_inc(moe_clip, 1)
                dve.wait_ge(moe_clip, t + 1)
                for k in range(2):
                    ins = nc.vector.tensor_tensor(moe_y[:, s, 2 * k:2 * k + 2, :], moe_y[:, s, 2 * k:2 * k + 2, :],
                                                  gates_all[:, bass.ds(t * 2 + k, 1), :].to_broadcast([P, BLK, D]),
                                                  ALU.mult)
                ins.then_inc(moe_gated, 1)

            chunk(0, 0)
            chunk(1, 1)
            with dve.Fori(0, TOKENS // 1024 - 1) as g:
                for s in range(2):
                    chunk(g * 2 + (2 + s), s)

        def dve_route1(dve):
            dve_route(dve, 1)

            def expert(e, s):
                dve.wait_ge(ffn_mm, e + 1)
                if not isinstance(e, int) or e >= 2:
                    dve.wait_ge(ffn_store[s], 8 * (e - s))
                nc.vector.tensor_copy(y_rows[:, s].rearrange("p k d -> p (k d)"), ps_max[:, s, :]).then_inc(ffn_out, 1)
            for e in range(2):
                expert(e, e)
            with dve.Fori(0, E1 // 2 - 1) as g:
                for s in range(2):
                    expert(g * 2 + (2 + s), s)
            dve.wait_ge(gathered, 16 * NB * BLK)
            for b in range(NB):
                for k in range(BLK):
                    j = b * BLK + k
                    last = nc.vector.scalar_tensor_tensor(y_all[:, j, :], y_all[:, j, :], rt1[:, 3, j:j + 1],
                                                          gates_all[:, b, :], ALU.mult, ALU.mult)
                last.then_inc(y_gated, 1)
                dve.wait_ge(y_gated, b + 1)
                xs = x_all[:, b * BLK:(b + 1) * BLK, :]
                nc.vector.tensor_tensor(xs, xs, y_all[:, b * BLK:(b + 1) * BLK, :], ALU.add).then_inc(final_done, 1)

        def pe_prologue(pe):
            pe.wait_ge(loads, 16 * N_LOADS)
            for layer in range(2):
                last = nc.tensor.transpose(ps_work[:, layer * NB:(layer + 1) * NB], c_rows[:, layer, :],
                                           ident[0:NB, 0:NB])
            last.then_inc(pro_pe, 1)
            pe.wait_ge(pro_dve, 6)
            nc.tensor.matmul(ps_work[:, P:2 * P], dir_rows[:, 0, :], dir_rows[:, 1, :], start=True, stop=True
                             ).then_inc(pro_pe, 1)
            pe.wait_ge(pro_dve, 7)
            for layer in range(2):
                for k in range(2):
                    last = nc.tensor.matmul(ps_work[:, (2 * layer + k) * NB:(2 * layer + k + 1) * NB],
                                            wmod[:, layer, k * D:(k + 1) * D], silu_c[:, layer, :],
                                            start=True, stop=True)
            last.then_inc(pro_pe, 1)
            pe.wait_ge(pro_dve, 9)
            pe.wait_ge(rotated, 1)
            pe.wait_ge(select_ready, 1)
            pe.wait_ge(ones_ready, 2)

        def pe_route(pe, layer):
            def entry(b, r2):
                n = layer * NB + b
                pe.wait_ge(rt_bcast, n + 1)
                if isinstance(b, int) and b == 0:
                    pe.wait_ge(y_out, (3 if layer else 2) * NB)
                at_least(pe, rt_ht_out, n)
                nc.tensor.matmul(ps_work[:, 0:3 * D], c_bcast[:, r2, :], wmod[:, layer, 3 * D:6 * D],
                                 start=True, stop=True).then_inc(rt_mod_mm, 1)
                pe.wait_ge(rt_mod_out, n + 1)
                if layer == 0:
                    pe.wait_ge(rt_mul, n + 1)
                else:
                    pe.wait_ge(rt_h, b + 1)
                for k in range(BLK):
                    src = hn_tok[:, r2, k, :] if layer == 0 else h_tok[:, r2, k, :]
                    last = nc.tensor.transpose(ps_work[:, k * P:(k + 1) * P], src, ident)
                last.then_inc(rt_ht_mm, 1)
                pe.wait_ge(rt_ht_out, n + 1)
                at_least(pe, rt_logit, n)
                if isinstance(b, int) and b == 0:
                    pe.wait_ge(o_done, (3 if layer else 2) * NB)
                for k in range(BLK):
                    lhs = h_t[:, r2, k * P:(k + 1) * P]
                    last = nc.tensor.matmul(ps_out[:, k * 8:(k + 1) * 8], lhs, wr[:, layer, :], start=True, stop=True)
                last.then_inc(rt_logit_mm, 1)
            entries(pe, entry)

        def pe_moe(pe):
            pe.wait_ge(folded, 2)
            pe_route(pe, 0)

            def chunk(t):
                x_t = ht_all[:, bass.ds(t * 512, 512)]

                def up(u):
                    n = t * 2 * E0 + u
                    e, f = u // 2, u % 2
                    at_least(pe, act_done, n - 1)
                    for i, w in enumerate((wg, wu)):
                        last = nc.tensor.matmul(ps_four[:, 2 * f + i, :], w[:, e, f * P:(f + 1) * P], x_t,
                                                start=True, stop=True)
                    last.then_inc(gu_mm, 1)

                def down(u):
                    n = t * 2 * E0 + u
                    e, f = u // 2, u % 2
                    pe.wait_ge(act_done, n + 1)
                    if f == 0:
                        at_least(pe, acc_done, t * E0 + e - 1)
                    for k in range(4):
                        last = nc.tensor.matmul(ps_max[:, e % 2, k * D:(k + 1) * D], act_t[:, f, k * P:(k + 1) * P],
                                                wd[:, e, f, :], start=(f == 0 and k == 0), stop=(f == 1),
                                                skip_group_check=True)
                    last.then_inc(down_mm, 1)

                for u in range(2 * E0):
                    up(u)
                    if u > 0:
                        down(u - 1)
                down(2 * E0 - 1)

            chunk(0)
            with pe.Fori(0, TOKENS // 512 - 1) as g:
                chunk(g + 1)

        def pe_route1(pe):
            pe_route(pe, 1)
            pe.wait_ge(rt_onehot, 1)
            pe.wait_ge(max_done, HEADS_BEFORE[2] + NB * CFGS[2].heads)
            hot = one_hot[:].rearrange("p k e -> p (k e)")
            n = NB * BLK * 8
            nc.tensor.matmul(ps_max[:, 0, 0:n], upper_ones[:, 0, :], hot, start=True, stop=True)
            nc.tensor.matmul(ps_max[:, 1, 0:n], upper_ones[:, 1, :], hot, start=True, stop=True).then_inc(rt_rank_mm, 1)

            def expert(e, s):
                pe.wait_ge(ffn_load[s], 24 * (e - s) + 48)
                at_least(pe, xt_out, e)
                for k in range(4):
                    last = nc.tensor.transpose(ps_work[:, k * P:(k + 1) * P], rows_e[:, s, k, :], ident)
                last.then_inc(xt_mm, 1)
                pe.wait_ge(xt_out, e + 1)
                for f in range(F1 // P):
                    at_least(pe, relu_done, 4 * e + f - 3)
                    nc.tensor.matmul(ps_four[:, f, :], w1[:, s, f * P:(f + 1) * P], rows_t[:, s, :],
                                     start=True, stop=True).then_inc(up_mm, 1)
                pe.wait_ge(relu_done, 4 * e + 4)
                at_least(pe, ffn_out, e - 1)
                for k in range(4):
                    for f in range(F1 // P):
                        last = nc.tensor.matmul(ps_max[:, s, k * D:(k + 1) * D], hid_t[:, s, f, k * P:(k + 1) * P],
                                                w2[:, s, f, :], start=(f == 0), stop=(f == F1 // P - 1))
                last.then_inc(ffn_mm, 1)
            pe.wait_ge(routed, 1)
            for e in range(2):
                expert(e, e)
            with pe.Fori(0, E1 // 2 - 1) as g:
                for s in range(2):
                    expert(g * 2 + (2 + s), s)

        @block.sync
        def _(sp):
            for dst, src in dma_list:
                sp.dma_start(dst, src).then_inc(loads, 16)
            stage_sel = stage.rearrange("p (a b) -> p a b", a=4)
            sel_dram = a["select"].rearrange("p a b g m -> p a b (g m)")
            sp.dma_start(stage[:, 0:2 * GROUPS * P], a["max_place"].rearrange("p k g m -> p (k g m)")
                         ).then_inc(sel_load, 16)
            k = NB * BLK // 8
            for n in range(8):
                sp.dma_start(x_all[:, n * k:(n + 1) * k, :], X[:, n * k:(n + 1) * k, :]).then_inc(x_load, 16)
            sp.wait_ge(zeros_ready, 1)
            for n in range(8):
                sp.dma_start(slots_dram[n * CAP:(n + 1) * CAP, :].rearrange("(p k) d -> p (k d)", p=P),
                             zeros).then_inc(zero_store, 16)
            for n in range(3):
                sp.wait_ge(select_ready, n + 1)
                if n == 2:
                    sp.wait_ge(moe_done, NB // 2)
                sp.dma_start(stage_sel, sel_dram[:, n]).then_inc(sel_load, 16)
            sp_tail(sp)

        @block.gpsimd
        def _(pool):
            def ones_column(c):
                if c.index > 0:
                    pool.wait_ge(values_mm, HEADS_BEFORE[c.index])
                v = v_all[:, 0:RING * BLK * c.kv * (c.hd + 1)].rearrange("p (n e) -> p n e", e=c.hd + 1)
                nc.gpsimd.memset(v[:, :, c.hd:c.hd + 1], 1.0).then_inc(ones_ready, 1)

            nc.gpsimd.memset(zeros, 0.0).then_inc(zeros_ready, 1)
            nc.gpsimd.memset(half_neg[:], -0.5)
            nc.gpsimd.memset(eps[:], LN_EPS)
            nc.gpsimd.memset(one[:], 1.0)
            ones_column(CFGS[0])
            nc.gpsimd.memset(max_t[:].bitcast(F32), 0.0).then_inc(ones_ready, 1)
            pool.wait_ge(loads, 16 * N_LOADS)
            nc.gpsimd.tensor_copy(ident_bf[:], squares[:, 0, :])
            nc.gpsimd.tensor_copy(masks[:], squares[:, 1:5, :])
            nc.gpsimd.tensor_copy(upper_ones[:], squares[:, 5:7, :])
            nc.gpsimd.tensor_scalar(wq[:, 1, 0, :], wq[:, 1, 0, :], ln_w[:, 0:1], None, ALU.mult)
            nc.gpsimd.tensor_scalar(wk[1][:, 0, :], wk[1][:, 0, :], ln_w[:, 0:1], None, ALU.mult)
            nc.gpsimd.tensor_scalar(wv[1], wv[1], ln_w[:, 0:1], None, ALU.mult).then_inc(folded, 1)
            pool.wait_ge(folded, 1)
            for c in CFGS:
                for w in (wq[:, c.index], wk[c.index]):
                    half = c.hd // 2
                    src = w[:, 0, :].rearrange("p (h e) -> p h e", e=c.hd)
                    dst = w[:, 1, :].rearrange("p (h e) -> p h e", e=c.hd)
                    if c.layer == 0:
                        nc.gpsimd.tensor_copy(dst[:, :, 0:half], src[:, :, half:])
                        last = nc.gpsimd.tensor_copy(dst[:, :, half:], src[:, :, 0:half])
                    else:
                        nc.gpsimd.tensor_copy(dst[:, :, 0:half], src[:, :, 1::2])
                        last = nc.gpsimd.tensor_copy(dst[:, :, half:], src[:, :, 0::2])
            last.then_inc(rotated, 1)
            pool.wait_ge(sel_load, 16)
            nc.gpsimd.tensor_copy(max_place[:].rearrange("p k g m -> p (k g m)"), stage[:, 0:2 * GROUPS * P]
                                  ).then_inc(select_ready, 1)

            def load_select(c):
                at_least(pool, sel_mm, 4 * c.first)
                pool.wait_ge(sel_load, 16 * (c.index + 2))
                nc.gpsimd.tensor_copy(select[:].rearrange("p b g m -> p (b g m)"), stage).then_inc(select_ready, 1)

            load_select(CFGS[0])
            nc.gpsimd.tensor_scalar(wr[:, 0, :], wr[:, 0, :], ln_w[:, 1:2], None, ALU.mult)
            nc.gpsimd.tensor_scalar(wg, wg, ln_w[:, 1:2], None, ALU.mult)
            nc.gpsimd.tensor_scalar(wu, wu, ln_w[:, 1:2], None, ALU.mult).then_inc(folded, 1)

            def prep(c, b, r, name):
                n, r2 = n_of(c, b), r % 2
                if name == "mod":
                    pool.wait_ge(mv_done, n + 1)
                    nc.gpsimd.tensor_tensor(var_eps[:, r2, :], mean_var[:, r2, :, 1], eps[:], ALU.add
                                            ).then_inc(var_done, 1)
                    pool.wait_ge(var_done, n + 1)
                    nc.gpsimd.tensor_tensor(rstd[:, r2, :], var_eps[:, r2, :], half_neg[:],
                                            ALU.pow).then_inc(rstd_done, 1)
                    if c.index == 1:
                        pool.wait_ge(mod_out, n + 1)
                        nc.gpsimd.tensor_tensor(mod[:, r, 1, :], mod[:, r, 1, :], one[:].to_broadcast([P, D]),
                                                ALU.add).then_inc(mod_scale, 1)
                        pool.wait_ge(h_mul, n - NB + 1)
                        nc.gpsimd.tensor_tensor(h_tok[:, r], h_tok[:, r],
                                                mod[:, r, 0:1, :].to_broadcast([P, BLK, D]), ALU.add
                                                ).then_inc(h_done, 1)
                    if c.index == 1:
                        pool.wait_ge(ssq_done, n - NB + 1)
                        nc.gpsimd.tensor_tensor(ssq_eps[:, r2, :], ssq[:, r2, :], eps[:], ALU.add
                                                ).then_inc(ssq_eps_done, 1)
                        pool.wait_ge(ssq_eps_done, n - NB + 1)
                        nc.gpsimd.tensor_tensor(rrms[:, r2, :], ssq_eps[:, r2, :], half_neg[:],
                                                ALU.pow).then_inc(rrms_done, 1)
                if name in ("q", "k"):
                    i = 0 if name == "q" else 1
                    m = P if name == "q" else c.kv * c.hd
                    rope_done, sum_done, lo_done = ((q_rope, q_sum, q_lo), (k_rope, k_sum, k_lo))[i]
                    pool.wait_ge(rope_done, n + 1)
                    if c.index > 0 or i == 1:
                        at_least(pool, sel_mm, 4 * n)
                    if c.index > 0 or i == 1:
                        nc.gpsimd.tensor_tensor(split[0:m, i, 0, :], rope_a[0:m, i, :], rope_b[0:m, i, :], ALU.add)
                        nc.gpsimd.tensor_tensor(rope_a[0:m, i, :], rope_a[0:m, i, :], rope_b[0:m, i, :],
                                                ALU.add).then_inc(sum_done, 1)
                        pool.wait_ge(sum_done, n + 1)
                        nc.gpsimd.tensor_tensor(split[0:m, i, 1, :], rope_a[0:m, i, :],
                                                split[0:m, i, 0, :].bitcast(F32), ALU.subtract).then_inc(lo_done, 1)
                    else:
                        nc.gpsimd.tensor_tensor(rope_a[0:m, i, :], rope_a[0:m, i, :], rope_b[0:m, i, :],
                                                ALU.add).then_inc(sum_done, 1)

            def post(c, b, r, name):
                if name == "y" and c.index != 1:
                    pool.wait_ge(y_out, n_of(c, b) + 1)
                    xs = x_all[:, bass.ds(b * BLK, BLK), :]
                    nc.gpsimd.tensor_tensor(xs, xs, y_tok[:, r % 2], ALU.add).then_inc(x_done, 1)

            def maxima(c, b, r, name):
                pass

            def start(c):
                if c.index > 0:
                    load_select(c)
                    ones_column(c)
                for b in (0, 1):
                    for name in PREP:
                        prep(c, b, b, name)

            def segment(c, b, r):
                for _, before, behind in slots(c, *flags(b)):
                    walk(c, b, r, post, prep, maxima, before + behind)

            def finish(c):
                post(c, NB - 1, (NB - 1) % RING, "y")

            run(pool, CFGS[0], start, segment, finish)
            run(pool, CFGS[1], start, segment, finish)
            pool_moe(pool)
            run(pool, CFGS[2], start, segment, finish)
            pool_route1(pool)

        @block.scalar
        def _(act):
            act_prologue(act)

            def prep(c, b, r, name):
                n, r2 = n_of(c, b), r % 2
                if name == "mod":
                    act.wait_ge(mod_mm, n + 1)
                    at_least(act, y_out, n - RING + 1)
                    if c.index == 1:
                        nc.scalar.copy(mod[:, r].rearrange("p a d -> p (a d)"), work[BANK[name]][:, 0:3 * D]
                                       ).then_inc(mod_out, 1)
                        act.wait_ge(h_done, n - NB + 1)
                    else:
                        nc.scalar.copy(mod[:, r, 2, :], work[BANK[name]][:, 0:D]).then_inc(mod_out, 1)
                    if c.index == 1:
                        at_least(act, ht_mm, n - 1)
                        for k in range(BLK):
                            last = nc.scalar.activation(hn_tok[:, r2, k, :], h_tok[:, r, k, :], ACT.Square, scale=RSQRT_D,
                                                        accum_out=ssq[:, r2, k:k + 1])
                        last.then_inc(ssq_done, 1)
                if name == "ht":
                    act.wait_ge(ht_mm, n + 1)
                    at_least(act, v_mm, n - 1)
                    if c.index == 1:
                        nc.scalar.copy(h_t[:, r2, :], work[BANK[name]][:, 0:S]).then_inc(ht_out, 1)
                    else:
                        nc.scalar.activation(h_t[:, r2, :], work[BANK[name]][:, 0:S], ACT.Identity,
                                             bias=mod_t[:, c.layer, 0, bass.ds(b, 1)],
                                             scale=mod_t[:, c.layer, 1, bass.ds(b, 1)]).then_inc(ht_out, 1)
                if name == "qd":
                    act.wait_ge(qd_mm, n + 1)
                    at_least(act, sel_mm, 4 * n)
                    nc.scalar.copy(split[:, 0, 0, :], work[BANK[name]][:, 0:S]).then_inc(q_hi, 1)
                if name == "v":
                    act.wait_ge(v_mm, n + 1)
                    at_least(act, values_mm, heads_until(c, b - RING))
                    nc.scalar.copy(v_tok[c.index][:, r, :, :, 0:c.hd], v_in_work(c)).then_inc(v_out, 1)
                if name[:3] == "sel":
                    j = int(name[3])
                    act.wait_ge(sel_mm, 4 * n + j + 1)
                    if j % 2 == 0:
                        at_least(act, values_mm, heads_until(c, b - RING))
                    dst = (q_st, k_st)[j // 2][:, r, 2 * (j % 2):2 * (j % 2) + 2, :]
                    src = work[BANK[name]].rearrange("p (g s) -> p g s", g=2)
                    if j < 2:
                        nc.scalar.copy(dst, src).then_inc(sel_out, 1)
                    else:
                        nc.scalar.activation(dst, src, ACT.Identity, bias=strips[:, c.kind, 0:1]
                                             ).then_inc(sel_out, 1)

            def post(c, b, r, name):
                n, r2 = n_of(c, b), r % 2
                if name == "ot":
                    act.wait_ge(ot_mm, n + 1)
                    at_least(act, y_mm, n)
                    nc.scalar.copy(o_t[:, r2, :], work[BANK[name]][:, 0:S]).then_inc(ot_out, 1)

            def maxima(c, b, r, name):
                n, r2 = n_of(c, b), r % 2
                if name != "rows":
                    return
                act.wait_ge(mt_mm, n + 1)
                at_least(act, place_mm, 2 * n - 2)
                nc.scalar.copy(max_t[0:c.heads, r2, :], work[BANK[name]][0:c.heads, 0:S]).then_inc(mt_hi, 1)

            def start(c):
                if c.index == 0:
                    act.wait_ge(ones_ready, 2)
                    act.wait_ge(zero_store, 16 * 8)
                for b in (0, 1):
                    for name in PREP:
                        if name != "qd" or c.index == 0:
                            prep(c, b, b, name)
                maxima(c, 0, 0, "rows")

            def pair_out(c, b, p):
                base = 32 * (p % 4)
                act.wait_ge(values_mm, HEADS_BEFORE[c.index] + b * c.heads + 2 * p + 2)
                if p == 0:
                    at_least(act, combined, n_of(c, b))
                nc.scalar.copy(o_strips[base:base + c.hd + 1, p // 4, :], ps_out[0:c.hd + 1, :]
                               ).then_inc(strips_out, 1)

            def segment(c, b, r):
                w = c.q_cols()
                for h, (_, before, behind) in enumerate(slots(c, *flags(b))):
                    walk(c, b, r, post, prep, maxima, before)
                    hn = HEADS_BEFORE[c.index] + b * c.heads + h
                    act.wait_ge(exp_mm, hn + 1)
                    at_least(act, values_mm, hn - 3)
                    nc.scalar.activation(probs[:, h % 4, 0:w], ps_exp[:, h % 3, 0:w], ACT.Exp, scale=c.scale
                                         ).then_inc(exp_done, 1)
                    if h == 1 and flags(b)[0]:
                        pair_out(c, b - 1, c.pairs - 1)
                    if h % 2 and h > 2:
                        pair_out(c, b, (h - 3) // 2)
                    walk(c, b, r, post, prep, maxima, behind)

            def finish(c):
                pair_out(c, NB - 1, c.pairs - 1)
                post(c, NB - 1, (NB - 1) % RING, "ot")

            run(act, CFGS[0], start, segment, finish)
            run(act, CFGS[1], start, segment, finish)
            act_moe(act)
            run(act, CFGS[2], start, segment, finish)
            act_route1(act)

        @block.vector
        def _(dve):
            dve_prologue(dve)

            def prep(c, b, r, name):
                n, r2 = n_of(c, b), r % 2
                if name == "mod":
                    if c.index == 0:
                        dve.wait_ge(x_load, 16 * 8)
                    elif c.index == 1:
                        dve.wait_ge(x_done, b + 1)
                    else:
                        dve.wait_ge(moe_done, NB // 2)
                    for k in range(BLK):
                        last = nc.vector.bn_stats(stats6[:, r2, k, :], block_of(x_all, b * BLK + k))
                    last.then_inc(stats_done, 1)
                    dve.wait_ge(stats_done, n + 1)
                    at_least(dve, mod_mm, n - 1)
                    nc.vector.tensor_copy(c_bcast[:, r2, :], silu_c[:, c.layer, bass.ds(b, 1)].to_broadcast([P, P])
                                          ).then_inc(c_bcast_done, 1)
                    for k in range(BLK):
                        last = nc.vector.bn_aggr(mean_var[:, r2, k, :], stats6[:, r2, k, :])
                    last.then_inc(mv_done, 1)
                    dve.wait_ge(mod_out, n + 1)
                    nc.vector.tensor_scalar(gate_tmp[:, 0, :], mod[:, r, 2, :], 0.0, 0.5, ALU.is_ge, ALU.subtract)
                    nc.vector.scalar_tensor_tensor(gate_tmp[:, 1, :], mod[:, r, 2, :], -1.0, mod[:, r, 2, :],
                                                   ALU.mult, ALU.max).then_inc(gate_a, 1)
                    dve.wait_ge(gate_a, n + 1)
                    nc.vector.tensor_scalar(gate_tmp[:, 1, :], gate_tmp[:, 1, :], 0.25, 2.0, ALU.max, ALU.mult).then_inc(gate_b, 1)
                    dve.wait_ge(gate_b, n + 1)
                    nc.vector.tensor_tensor(mod[:, r, 2, :], gate_tmp[:, 0, :], gate_tmp[:, 1, :], ALU.mult).then_inc(gate_done, 1)
                    dve.wait_ge(rstd_done, n + 1)
                    for k in range(BLK):
                        last = nc.vector.tensor_scalar(h_tok[:, r, k, :], block_of(x_all, b * BLK + k),
                                                       mean_var[:, r2, k, 0:1], rstd[:, r2, k:k + 1],
                                                       ALU.subtract, ALU.mult)
                    last.then_inc(xhat_done, 1)
                    if c.index == 1:
                        dve.wait_ge(xhat_done, n + 1)
                        dve.wait_ge(mod_scale, n - NB + 1)
                        nc.vector.tensor_tensor(h_tok[:, r], h_tok[:, r],
                                                mod[:, r, 1:2, :].to_broadcast([P, BLK, D]), ALU.mult
                                                ).then_inc(h_mul, 1)
                        dve.wait_ge(rrms_done, n - NB + 1)
                        at_least(dve, ht_mm, n - 1)
                        for k in range(BLK):
                            last = nc.vector.tensor_scalar(hn_tok[:, r2, k, :], h_tok[:, r, k, :],
                                                           rrms[:, r2, k:k + 1], None, ALU.mult)
                        last.then_inc(hn_done, 1)
                if name in ("q", "k"):
                    i = 0 if name == "q" else 1
                    m = P if name == "q" else c.kv * c.hd
                    mm_done, rope_done, sum_done = ((q_mm, q_rope, q_sum), (k_mm, k_rope, k_sum))[i]
                    t = 0 if c.hd == 16 else 2
                    dve.wait_ge(mm_done, n + 1)
                    at_least(dve, qd_mm if c.index == 0 and i == 0 else (q_lo, k_lo)[i], n)
                    nc.vector.tensor_tensor(rope_a[0:m, i, :], work[BANK[name]][0:m, 0:S], rope[0:m, t, :], ALU.mult)
                    nc.vector.tensor_tensor(rope_b[0:m, i, :], work[BANK[name]][0:m, S:2 * S], rope[0:m, t + 1, :],
                                            ALU.mult).then_inc(rope_done, 1)
                if name == "qd":
                    dve.wait_ge(q_hi, n + 1)
                    nc.vector.tensor_tensor(split[:, 0, 1, :], work[BANK[name]][:, 0:S], split[:, 0, 0, :].bitcast(F32),
                                            ALU.subtract).then_inc(q_lo, 1)

            def post(c, b, r, name):
                n, r2 = n_of(c, b), r % 2
                if name == "combine":
                    dve.wait_ge(combined, n + 1)
                    at_least(dve, ot_mm, n)
                    rows = BLK * c.heads
                    po = work[BANK[name]][:, 0:rows * (c.hd + 1)].rearrange("p (h e) -> p h e", e=c.hd + 1)
                    nc.vector.reciprocal(recip[:, r2, 0:rows], po[:, :, c.hd]).then_inc(recip_done, 1)
                    dve.wait_ge(recip_done, n + 1)
                    nc.vector.tensor_tensor(o_tok[:, r2].rearrange("p k (h e) -> p (k h) e", e=c.hd),
                                            po[:, :, 0:c.hd],
                                            recip[:, r2, 0:rows].unsqueeze(2).to_broadcast([P, rows, c.hd]),
                                            ALU.mult).then_inc(o_done, 1)
                if name == "y":
                    dve.wait_ge(y_mm, n + 1)
                    y = work[BANK[name]][:, 0:S].rearrange("p (k d) -> p k d", k=BLK)
                    if c.index != 1:
                        if isinstance(b, int):
                            at_least(dve, x_done, NB * (c.index == 2) + b)
                        nc.vector.tensor_tensor(y_tok[:, r2], y, mod[:, r, 2:3, :].to_broadcast([P, BLK, D]),
                                                ALU.mult).then_inc(y_out, 1)
                    else:
                        nc.vector.tensor_tensor(y_tok[:, r2], y, h_tok[:, r], ALU.add).then_inc(y_out, 1)
                        dve.wait_ge(y_out, n + 1)
                        nc.vector.tensor_scalar(res_all[:, bass.ds(b * BLK, BLK), :], y_tok[:, r2], CLIP, -CLIP,
                                                ALU.min, ALU.max).then_inc(res_done, 1)

            def head_max(c, b, r, h):
                n, r2 = n_of(c, b), r % 2
                hn = HEADS_BEFORE[c.index] + b * c.heads + h
                parts = 3 if c.causal else 2
                dve.wait_ge(max_mm, hn + 1)
                if h == 0:
                    at_least(dve, mt_mm, n - 1)
                src = ps_max[:, h % 2, 0:c.q_cols()].rearrange("p (k s) -> p k s", k=parts)
                nc.vector.tensor_reduce(row_max[:, r2, 0:parts, h], src, AX_X, ALU.max).then_inc(max_done, 1)
                if h == c.heads - 1 and c.causal:
                    dve.wait_ge(max_done, hn + 1)
                    nc.vector.tensor_tensor(row_max[:, r2, 1, 0:c.heads], row_max[:, r2, 1, 0:c.heads],
                                            row_max[:, r2, 2, 0:c.heads], ALU.max).then_inc(max_all, 1)

            def maxima(c, b, r, name):
                n, r2 = n_of(c, b), r % 2
                if name == "rows":
                    dve.wait_ge(mt_hi, n + 1)
                    nc.vector.tensor_tensor(max_t[32:32 + c.heads, r2, :], work[BANK[name]][0:c.heads, 0:S],
                                            max_t[0:c.heads, r2, :].bitcast(F32), ALU.subtract).then_inc(mt_out, 1)
                else:
                    j = int(name[5])
                    dve.wait_ge(place_mm, 2 * n + j + 1)
                    half = q_st[:, r, 2 * j:2 * j + 2, :]
                    nc.vector.tensor_tensor(half, half.bitcast(F32), work[BANK[name]].rearrange("p (g s) -> p g s", g=2),
                                            ALU.add).then_inc(place_done, 1)

            def start(c):
                for b in (0, 1):
                    for name in PREP:
                        if name != "qd" or c.index == 0:
                            prep(c, b, b, name)
                for h in range(c.heads):
                    head_max(c, 0, 0, h)
                for name in MAXIMA:
                    maxima(c, 0, 0, name)

            def segment(c, b, r):
                for h, (max_heads, before, behind) in enumerate(slots(c, *flags(b))):
                    for k in max_heads:
                        head_max(c, b + 1, (r + 1) % RING, k)
                    walk(c, b, r, post, prep, maxima, before)
                    walk(c, b, r, post, prep, maxima, behind)

            def finish(c):
                for name in POST:
                    post(c, NB - 1, (NB - 1) % RING, name)

            run(dve, CFGS[0], start, segment, finish)
            run(dve, CFGS[1], start, segment, finish)
            dve_moe(dve)
            run(dve, CFGS[2], start, segment, finish)
            dve_route1(dve)

        @block.tensor
        def _(pe):
            pe_prologue(pe)

            def prep(c, b, r, name, free):
                n, r2 = n_of(c, b), r % 2
                m = c.kv * c.hd
                bank = work[BANK[name]]
                at_least(pe, *free)
                if name == "mod":
                    pe.wait_ge(c_bcast_done, n + 1)
                    first, w = (0, 3 * D) if c.index == 1 else (2 * D, D)
                    nc.tensor.matmul(bank[:, 0:w], c_bcast[:, r2, :],
                                     wmod[:, c.layer, c.mod + first:c.mod + first + w],
                                     start=True, stop=True).then_inc(mod_mm, 1)
                if name == "ht":
                    if c.index == 1:
                        pe.wait_ge(hn_done, n - NB + 1)
                        src = hn_tok[:, r2]
                    else:
                        pe.wait_ge(xhat_done, n + 1)
                        src = h_tok[:, r]
                    for k in range(BLK):
                        last = nc.tensor.transpose(bank[:, k * P:(k + 1) * P], src[:, k, :], ident)
                    last.then_inc(ht_mm, 1)
                if name == "q":
                    pe.wait_ge(ht_out, n + 1)
                    for i in range(2):
                        last = nc.tensor.matmul(bank[:, i * S:(i + 1) * S], wq[:, c.index, i, :], h_t[:, r2, :],
                                                start=True, stop=True)
                    last.then_inc(q_mm, 1)
                if name == "k":
                    for i in range(2):
                        last = nc.tensor.matmul(bank[0:m, i * S:(i + 1) * S], wk[c.index][:, i, :],
                                                h_t[:, r2, :], start=True, stop=True)
                    last.then_inc(k_mm, 1)
                if name == "qd":
                    pe.wait_ge(q_sum, n + 1)
                    nc.tensor.matmul(bank[:, 0:S], dir_mix[:], rope_a[:, 0, :], start=True, stop=True
                                     ).then_inc(qd_mm, 1)
                if name == "v":
                    for k in range(BLK):
                        last = nc.tensor.matmul(bank[:, k * P:k * P + m], h_t[:, r2, k * P:(k + 1) * P],
                                                wv[c.index], start=True, stop=True)
                    last.then_inc(v_mm, 1)
                if name[:3] == "sel":
                    j = int(name[3])
                    i, rows = j // 2, (P, m)[j // 2]
                    if j % 2 == 0:
                        pe.wait_ge((q_lo, k_lo)[i], n + 1)
                    for g in range(2):
                        for part in range(2):
                            last = nc.tensor.matmul(bank[:, g * S:(g + 1) * S],
                                                    select[0:rows, 2 * i + part, 2 * (j % 2) + g, :],
                                                    split[0:rows, i, part, :], start=(part == 0), stop=(part == 1))
                    last.then_inc(sel_mm, 1)

            def post(c, b, r, name, free):
                n, r2 = n_of(c, b), r % 2
                bank = work[BANK[name]]
                pe.wait_ge(*free)
                if name == "combine":
                    pe.wait_ge(strips_out, pairs_until(c, b))
                    w = 4 * (c.hd + 1)
                    columns = bank[:, 0:BLK * c.heads * (c.hd + 1)].rearrange(
                        "p (k g j i e) -> p k g i j e", k=BLK, g=c.pairs // 4, i=2, e=c.hd + 1)
                    for k in range(BLK):
                        for g in range(c.pairs // 4):
                            for i in range(2):
                                at = i * S + k * P
                                last = nc.tensor.matmul(columns[:, k, g, i], o_strips[:, g, at:at + P],
                                                        strips[:, c.kind, 1:1 + w], start=True, stop=True)
                    last.then_inc(combined, 1)
                if name == "ot":
                    pe.wait_ge(o_done, n + 1)
                    for k in range(BLK):
                        last = nc.tensor.transpose(bank[:, k * P:(k + 1) * P], o_tok[:, r2, k, :], ident)
                    last.then_inc(ot_mm, 1)
                if name == "y":
                    pe.wait_ge(ot_out, n + 1)
                    for k in range(BLK):
                        last = nc.tensor.matmul(bank[:, k * P:(k + 1) * P], o_t[:, r2, k * P:(k + 1) * P],
                                                wo[:, c.index, :], start=True, stop=True)
                    last.then_inc(y_mm, 1)

            def max_scores(c, b, r, h):
                n = n_of(c, b)
                hn = HEADS_BEFORE[c.index] + b * c.heads + h
                g, base = h // c.per_group, (h % c.per_group) * c.strip
                rows = slice(base, base + c.krows)
                if h == 0:
                    pe.wait_ge(sel_out, 4 * n + 4)
                at_least(pe, max_done, hn - 1)
                bank = ps_max[:, h % 2, :]
                if c.causal:
                    nc.tensor.matmul(bank[:, 0:P], ident_bf[:], masks[:, 0, :], start=True, stop=False,
                                     skip_group_check=True)
                    nc.tensor.matmul(bank[:, 2 * P:3 * P], ident_bf[:], masks[:, 0, :], start=False, stop=False,
                                     skip_group_check=True)
                    if c.window:
                        nc.tensor.matmul(bank[:, P:2 * P], ident_bf[:], masks[:, 1, :], start=False, stop=False,
                                         skip_group_check=True)
                    nc.tensor.matmul(bank[:, 0:P], q_st[rows, r, g, 0:P], k_st[rows, r, g, 0:P], start=False,
                                     stop=True, skip_group_check=True)
                    nc.tensor.matmul(bank[:, P:3 * P], q_st[rows, r, g, P:S], k_st[rows, r, g, :], start=False,
                                     stop=True, skip_group_check=True).then_inc(max_mm, 1)
                else:
                    for k in range(BLK):
                        last = nc.tensor.matmul(bank[:, k * S:(k + 1) * S], q_st[rows, r, g, k * P:(k + 1) * P],
                                                k_st[rows, r, g, :], start=True, stop=True)
                    last.then_inc(max_mm, 1)

            def exp_scores(c, b, r, h):
                n = n_of(c, b)
                hn = HEADS_BEFORE[c.index] + b * c.heads + h
                g, base = h // c.per_group, (h % c.per_group) * c.strip
                rows = slice(base, base + c.krows + 2)
                if h == 0:
                    pe.wait_ge(place_done, 2 * n + 2)
                if h >= 3:
                    pe.wait_ge(exp_done, hn - 2)
                elif isinstance(b, int) and b == 0:
                    at_least(pe, exp_done, HEADS_BEFORE[c.index])
                else:
                    at_least(pe, exp_done, hn + 1 - (h + c.heads - max(k for k in range(c.heads) if k % 3 == h)))
                bank = ps_exp[:, h % 3, :]
                second = slice(P, S) if c.causal else slice(0, S)
                w = second.stop - second.start
                if c.causal:
                    nc.tensor.matmul(bank[:, 0:P], ident_bf[:], masks[:, 2, :], start=True, stop=False,
                                     skip_group_check=True)
                    nc.tensor.matmul(bank[:, S:S + P], ident_bf[:], masks[:, 2, :], start=False, stop=False,
                                     skip_group_check=True)
                    if c.window:
                        nc.tensor.matmul(bank[:, P:S], ident_bf[:], masks[:, 3, :], start=False, stop=False,
                                         skip_group_check=True)
                nc.tensor.matmul(bank[:, 0:S], k_st[rows, r, g, 0:P], q_st[rows, r, g, :], start=not c.causal,
                                 stop=True, skip_group_check=True)
                last = nc.tensor.matmul(bank[:, S:S + w], k_st[rows, r, g, P:S], q_st[rows, r, g, second],
                                        start=False, stop=True, skip_group_check=True)
                last.then_inc(exp_mm, 1)

            def values(c, b, r, h):
                hn = HEADS_BEFORE[c.index] + b * c.heads + h
                pe.wait_ge(exp_done, hn + 1)
                if h % 2 == 0:
                    at_least(pe, strips_out, PAIRS_BEFORE[c.index] + b * c.pairs + h // 2)
                if h == 0:
                    pe.wait_ge(v_out, n_of(c, b) + 1)
                kv = h // (c.heads // c.kv)
                for kb in range(BLK):
                    first = P if c.causal and kb == 1 else 0
                    last = nc.tensor.matmul(ps_out[0:c.hd + 1, (h % 2) * S + first:(h % 2 + 1) * S],
                                            v_tok[c.index][:, r, kb, kv, :],
                                            probs[:, h % 4, kb * S:kb * S + S - first],
                                            start=(kb == 0), stop=(kb == 1), skip_group_check=True)
                last.then_inc(values_mm, 1)

            def maxima(c, b, r, name, free):
                n, r2 = n_of(c, b), r % 2
                bank = work[BANK[name]]
                pe.wait_ge(*free)
                if name == "rows":
                    if c.causal:
                        pe.wait_ge(max_all, n + 1)
                    else:
                        pe.wait_ge(max_done, HEADS_BEFORE[c.index] + (b + 1) * c.heads)
                    for k in range(BLK):
                        last = nc.tensor.transpose(bank[0:c.heads, k * P:(k + 1) * P],
                                                   row_max[:, r2, k, 0:c.heads], ident)
                    last.then_inc(mt_mm, 1)
                else:
                    j = int(name[5])
                    pe.wait_ge(mt_out, n + 1)
                    for g in range(2):
                        last = nc.tensor.matmul(bank[:, g * S:(g + 1) * S], max_place[:, c.kind, 2 * j + g, :],
                                                max_t[:, r2, :], start=True, stop=True)
                    last.then_inc(place_mm, 1)

            readers = {"mod": (mod_out, 1, 1), "ht": (ht_out, 1, 1), "q": (q_rope, 1, 1), "k": (k_rope, 1, 1),
                       "v": (v_out, 1, 1), "combine": (o_done, 1, 1), "ot": (ot_out, 1, 1), "y": (y_out, 1, 1),
                       "rows": (mt_out, 1, 1), "place0": (place_done, 2, 1), "place1": (place_done, 2, 2)}

            def reader_of(c, b, name):
                if name[:3] == "sel":
                    semaphore, count, which = sel_out, 4, int(name[3]) + 1
                elif name == "qd":
                    semaphore, count, which = q_lo, 1, 1
                else:
                    semaphore, count, which = readers[name]
                return semaphore, count * n_of(c, b) + which

            def tracked(free):
                def step(f):
                    def g(c, b, r, name):
                        f(c, b, r, name, free[BANK[name]])
                        free[BANK[name]] = reader_of(c, b, name)
                    return g
                return step(post), step(prep), step(maxima)

            def start(c):
                first = (rt_ht_out, NB) if c.index == 2 else (y_out, c.first)
                post_step, prep_step, maxima_step = tracked({0: first, 1: (o_done, c.first)})
                if c.index > 0:
                    pe.wait_ge(ones_ready, c.index + 2)
                for b in (0, 1):
                    for name in PREP:
                        if name != "qd" or c.index == 0:
                            prep_step(c, b, b, name)
                for h in range(c.heads):
                    max_scores(c, 0, 0, h)
                for name in MAXIMA:
                    maxima_step(c, 0, 0, name)

            def segment(c, b, r):
                n = n_of(c, b)
                steps = tracked({0: (place_done, 2 * n + 1), 1: (place_done, 2 * n + 2)})
                for h, (max_heads, before, behind) in enumerate(slots(c, *flags(b))):
                    for k in max_heads:
                        max_scores(c, b + 1, (r + 1) % RING, k)
                    walk(c, b, r, *steps, before)
                    exp_scores(c, b, r, h)
                    if h > 1:
                        values(c, b, r, h - 2)
                    elif flags(b)[0]:
                        values(c, b - 1, (r - 1) % RING, c.heads - 2 + h)
                    walk(c, b, r, *steps, behind)

            def finish(c):
                n = n_of(c, NB - 2)
                for h in (c.heads - 2, c.heads - 1):
                    values(c, NB - 1, (NB - 1) % RING, h)
                post_step, _, _ = tracked({0: (y_out, n + 1), 1: (o_done, n + 1)})
                for name in POST:
                    post_step(c, NB - 1, (NB - 1) % RING, name)

            run(pe, CFGS[0], start, segment, finish)
            run(pe, CFGS[1], start, segment, finish)
            pe_moe(pe)
            run(pe, CFGS[2], start, segment, finish)
            pe_route1(pe)


_SHAPES = {"squares": square_constants, "rope": rope_tables, "experts": expert_constants,
           "select": select_constants, "max_place": max_place_constant, "strips": strip_constants}
_INS = ["L0_attn_x", "L0_attn_Wq", "L0_attn_Wk", "L0_attn_Wv", "L0_attn_Wo", "L0_attn_head_scales",
        "L0_attn_head_dirs", "L0_ffn_ln1_w", "L0_ffn_ln2_w", "L0_ffn_Wq", "L0_ffn_Wk", "L0_ffn_Wv", "L0_ffn_Wo",
        "L0_ffn_Wr", "L0_ffn_Wg", "L0_ffn_Wu", "L0_ffn_Wd", "L0_c", "L0_wmod", "L1_ffn_Wr", "L1_ffn_W1", "L1_ffn_W2",
        "L1_c", "L1_wmod"]
_TRANSPOSED = ["L1_attn_Wq", "L1_attn_Wk", "L1_attn_Wv", "L1_attn_Wo"]


def kernel(**inputs):
    import numpy as _np
    import concourse.bacc as _bacc
    from concourse import mybir as _mybir
    from concourse.bass_utils import run_bass_kernel_spmd as _run

    nc = _bacc.Bacc("TRN2", target_bir_lowering=False, num_devices=1)
    arrays = {name: _np.ascontiguousarray(inputs[name]) for name in _INS}
    arrays.update({name + "T": _np.ascontiguousarray(_np.asarray(inputs[name]).T) for name in _TRANSPOSED})
    arrays.update({name: make() for name, make in _SHAPES.items()})
    aps = {name: nc.dram_tensor(f"in_{name}", v.shape, _mybir.dt.from_np(v.dtype), kind="ExternalInput").ap()
           for name, v in arrays.items()}
    out = nc.dram_tensor("out_x", (NB, S, D), F32, kind="ExternalOutput").ap()
    adaln_two_layers(nc, aps, out)
    r = _run(nc, [{f"in_{name}": v for name, v in arrays.items()}], core_ids=[0])
    return r.results[0]["out_x"]
```

```python
from contextlib import ExitStack

import numpy as np

import concourse.bass as bass
from concourse import mybir

ALU = mybir.AluOpType
ACT = mybir.ActivationFunctionType
F32 = mybir.dt.float32
F32R = mybir.dt.float32r
BF16 = mybir.dt.bfloat16
I32 = mybir.dt.int32
AX_X = mybir.AxisListType.X

P = 128
D = 128
S = 256
NB = 16
BLK = S // P
TOKENS = NB * S
LN_EPS = 1e-5
LEAST = -3e38
MASKED = -1e30
CLIP = 100.0
RSQRT_D = float(D) ** -0.5

E0, F0 = 8, 256
E1, F1 = 8, 512
CAP = TOKENS // E1

RING = 4


class Attn:

    def __init__(self, index, layer, mod, heads, kv, causal, window, scale):
        self.index = index
        self.layer = layer
        self.mod = mod
        self.parts = (1, 3, 4)[index]
        self.gates = ((0,), (2,), (0, 3))[index]
        self.heads = heads
        self.hd = D // heads
        self.kv = kv
        self.causal = causal
        self.window = window
        self.scale = scale
        self.strip = 32 if self.hd == 8 else 64
        self.per_group = P // self.strip
        self.krows = 3 * self.hd
        self.kind = 0 if self.hd == 16 else 1
        self.pairs = heads // 2
        self.first = NB * index

    def q_cols(self):
        return 384 if self.causal else 512


CFGS = [
    Attn(0, 0, 2 * D, 8, 4, True, True, 1.0),
    Attn(1, 0, 3 * D, 16, 4, True, False, float(1.0 / np.sqrt(np.float32(8.0)))),
    Attn(2, 1, 2 * D, 16, 16, False, False, float(np.sqrt(8.0))),
]
GROUPS = 4
HEADS_BEFORE = [0, NB * 8, NB * 24]
PAIRS_BEFORE = [0, NB * 4, NB * 12]


def rope_tables():
    out = []
    for hd in (16, 8):
        inv = (1.0 / np.float32(10000.0) ** (np.arange(0, hd, 2, dtype=np.float32) / np.float32(hd))).astype(np.float32)
        f = (np.arange(S, dtype=np.float32)[:, None] * inv[None, :]).astype(np.float32)
        c, s = np.cos(f).T, np.sin(f).T
        out.append(np.tile(np.concatenate([c, c]), (D // hd, 1)))
        out.append(np.tile(np.concatenate([-s, s]), (D // hd, 1)))
    return np.stack(out, 1).astype(np.float32)


def square_constants():
    a = np.arange(P)
    row, col = a[:, None], a[None, :]
    causal = np.where(col > row, MASKED, 0.0)
    window = np.where((col < 4) | (col >= row + 1), 0.0, MASKED)
    return np.stack([np.eye(P), causal, window, causal.T, window.T, row < col, np.ones((P, P))], 1).astype(np.float32)


def select_constants():
    out = np.zeros((P, 3, 4, GROUPS, P), np.float32)
    for c in CFGS:
        for g in range(GROUPS):
            for j in range(c.per_group):
                head = g * c.per_group + j
                kv = head // (c.heads // c.kv)
                for d in range(c.hd):
                    for slot, (qp, kp) in enumerate(((0, 0), (0, 1), (1, 0))):
                        row = j * c.strip + slot * c.hd + d
                        out[head * c.hd + d, c.index, qp, g, row] = 1.0
                        out[kv * c.hd + d, c.index, 2 + kp, g, row] = 1.0
    return out


def max_place_constant():
    out = np.zeros((P, 2, GROUPS, P), np.float32)
    for c in CFGS[0:2]:
        for h in range(c.heads):
            row = (h % c.per_group) * c.strip + c.krows
            out[h, c.kind, h // c.per_group, row] = 1.0
            out[32 + h, c.kind, h // c.per_group, row + 1] = 1.0
    return out


def strip_constants():
    out = np.zeros((P, 2, 1 + 4 * 17), np.float32)
    for c in CFGS[0:2]:
        for j in range(c.per_group):
            out[j * c.strip + c.krows:j * c.strip + c.krows + 2, c.kind, 0] = -1.0
        for j in range(4):
            for d in range(c.hd + 1):
                out[j * 32 + d, c.kind, 1 + j * (c.hd + 1) + d] = 1.0
    return out


def expert_constants():
    out = np.zeros((P, 6, 8), np.float32)
    out[:, 0] = 8 - np.arange(8)
    out[:, 1] = CAP * np.arange(8)
    out[:, 2:] = (TOKENS + P * np.arange(NB * BLK)[None, :] + np.arange(P)[:, None]).reshape(P, 4, 8)
    return out


def adaln_two_layers(nc, a, out):
    with ExitStack() as ctx:
        def sb(name, shape, dt=F32):
            return ctx.enter_context(nc.sbuf_tensor(name, shape, dt))

        def psum(name, shape, dt=F32):
            return ctx.enter_context(nc.psum_tensor(name, shape, dt))

        def sem(name):
            return ctx.enter_context(nc.semaphore(name))

        ps_max = psum("ps_max", [P, 2, 512])
        ps_four = psum("ps_four", [P, 4, 512])
        ps_exp = ps_four[:, 0:3, :]
        ps_out = psum("ps_out", [P, 512])
        ps_work = psum("ps_work", [P, 512])
        work = (ps_work[:], ps_four[:, 3, :])

        x_all = sb("x_all", [P, NB * BLK, D])
        res_all = sb("res_all", [P, NB * BLK, D])
        res_words = res_all[:].rearrange("p a d -> p (a d)")
        squares = res_words[:, 0:7 * P].rearrange("p (n m) -> p n m", n=7)
        ident_sb = sb("ident", [P, P])
        ident = ident_sb[:]
        ident_bf = sb("ident_bf", [P, P], BF16)
        masks = sb("masks", [P, 2, P], BF16)
        upper_ones = sb("upper_ones", [P, 2, P], BF16)
        rope = sb("rope", [P, 4, S])
        select = sb("select", [P, 4, GROUPS, P], F32R)
        max_place = sb("max_place", [P, 2, GROUPS, P], F32R)
        strips = sb("strips", [P, 2, 1 + 4 * 17])
        mod_t = sb("mod_t", [P, 2, 2, NB])
        expert_c = sb("expert_c", [P, 6, 8])
        half_neg = sb("half_neg", [P, 2])
        eps = sb("eps", [P, 2])
        one = sb("one", [P, 1])
        ln_w = sb("ln_w", [P, 2])
        silu_c = sb("silu_c", [P, 2, NB])
        c_rows = res_words[0:NB, 7 * P:9 * P].rearrange("p (n m) -> p n m", n=2)
        wmod = sb("wmod", [P, 2, 6 * D])
        wq = sb("wq", [P, 3, 2, D])
        kv_cols = [c.kv * c.hd for c in CFGS]
        wk_all = sb("wk_all", [P, 2 * sum(kv_cols)])
        wv_all = sb("wv_all", [P, sum(kv_cols)])
        wk = [wk_all[:, 2 * sum(kv_cols[:i]):2 * sum(kv_cols[:i + 1])].rearrange("p (t m) -> p t m", t=2)
              for i in range(3)]
        wv = [wv_all[:, sum(kv_cols[:i]):sum(kv_cols[:i + 1])] for i in range(3)]
        wo = sb("wo", [P, 3, D])
        dirs = sb("dirs", [8, 4])
        dir_rows = res_words[0:8, 9 * P:11 * P].rearrange("p (n m) -> p n m", n=2)
        dir_mix = sb("dir_mix", [P, D])
        wr = sb("wr", [P, 2, 8])
        wgu = sb("wgu", [P, 2, E0, F0])
        wg, wu = wgu[:, 0], wgu[:, 1]
        wd = sb("wd", [P, E0, F0 // P, D])

        c_bcast = sb("c_bcast", [P, 2, P])
        mod = sb("mod", [P, RING, 4, D])
        gate_tmp = sb("gate_tmp", [P, 2, 2, D])
        stats6 = sb("stats6", [P, 2, BLK, 6])
        mean_var = sb("mean_var", [P, 2, BLK, 2])
        var_eps = sb("var_eps", [P, 2, BLK])
        rstd = sb("rstd", [P, 2, BLK])
        h_tok = sb("h_tok", [P, RING, BLK, D])
        ssq = sb("ssq", [P, 2, BLK])
        ssq_eps = sb("ssq_eps", [P, 2, BLK])
        rrms = sb("rrms", [P, 2, BLK])
        h_both = sb("h_both", [P, 2, 2, S])
        hn_tok = h_both[:, 0].rearrange("p a (k d) -> p a k d", d=D)
        h_t = h_both[:, 1]
        rope_ab = sb("rope_ab", [P, 2, 2, S])
        rope_a, rope_b = rope_ab[:, 0], rope_ab[:, 1]
        split = sb("split", [P, 2, 2, S], F32R)
        q_st = sb("q_st", [P, RING, GROUPS, S], F32R)
        k_st = sb("k_st", [P, RING, GROUPS, S], F32R)
        v_all = sb("v_all", [P, RING * BLK * 16 * 9])
        v_tok = [v_all[:, 0:RING * BLK * c.kv * (c.hd + 1)].rearrange(
            "p (r k h e) -> p r k h e", r=RING, k=BLK, h=c.kv) for c in CFGS]
        row_max = sb("row_max", [P, 2, BLK, 16])
        wait_cell = sb("wait_cell", [P, 6])
        q_masks = sb("q_masks", [P, 3, P])
        max_t = sb("max_t", [P, 2, S], F32R)
        attn_f32 = sb("attn_f32", [P, 4, 2, 512])
        probs = attn_f32[:, 0:2].rearrange("p a b c -> p (a b) c")
        o_strips = attn_f32[:, 2]
        recip = sb("recip", [P, 2, BLK * 16])
        o_both = sb("o_both", [P, 2, 2, S])
        o_tok = o_both[:, 0].rearrange("p a (k d) -> p a k d", d=D)
        o_t = o_both[:, 1]
        y_tok = sb("y_tok", [P, 2, BLK, D])

        zeros = attn_f32[:, 3, 0, :]

        ht_all = sb("ht_all", [P, TOKENS])
        gates_all = sb("gates_all", [P, NB, D])
        stage = gates_all[:].rearrange("p b d -> p (b d)")
        w_hi = q_st[:].rearrange("p r g s -> p (r g s)").rearrange("p (e i f) -> p e i f", e=E0, i=2)
        w_lo = k_st[:].rearrange("p r g s -> p (r g s)").rearrange("p (e i f) -> p e i f", e=E0, i=2)
        x_split = select[:].rearrange("p a g m -> p (a g m)").rearrange("p (s h t) -> p s h t", s=2, h=2)
        logits = sb("logits", [P, NB * BLK, 8])
        hn_rt = attn_f32[:, 3, 0, :].rearrange("p (a k d) -> p a k d", a=2, k=BLK)
        ht_rt = attn_f32[:, 3, 1, :].rearrange("p (a s) -> p a s", a=2)
        stats_rt = sb("stats_rt", [P, 2, BLK, 6])
        mean_var_rt = sb("mean_var_rt", [P, 2, BLK, 2])
        ssq_rt = sb("ssq_rt", [P, 2, BLK])
        var_eps_rt = sb("var_eps_rt", [P, 2, BLK])
        rstd_rt = sb("rstd_rt", [P, 2, BLK])
        rt_of = (mod[:].rearrange("p r a d -> p (r a d)").rearrange("p (n k e) -> p n k e", n=8, e=8),
                 wg.rearrange("p e f -> p (e f)").rearrange("p (n k e) -> p n k e", n=8, e=8))
        rt1 = sb("rt1", [P, 12, NB * BLK])
        one_hot = sb("one_hot", [P, NB * BLK, 8], BF16)
        slot_put = sb("slot_put", [P, NB * BLK], I32)
        slot_get = sb("slot_get", [P, NB * BLK], I32)
        weight_t = sb("weight_t", [P, 4, 8])
        tanh_g = h_tok[:].rearrange("p a b c -> p (a b c)").rearrange("p (s t) -> p s t", s=2)
        gated = rope_ab[:].rearrange("p a b c -> p (a b c)").rearrange("p (s t) -> p s t", s=2)
        act_t = o_both[:].rearrange("p a b c -> p (a b c)").rearrange("p (s t) -> p s t", s=2)
        acc = y_tok[:].rearrange("p a k d -> p (a k) d")
        moe_y = h_both[:].rearrange("p s a (k d) -> p s (a k) d", d=D)
        w12 = wd[:].rearrange("p e c d -> p (e c d)")
        w1 = w12[:, 0:2 * F1].rearrange("p (s f) -> p s f", s=2)
        w2 = w12[:, 2 * F1:].rearrange("p (s f d) -> p s f d", s=2, f=F1 // P)
        rows_e = tanh_g.rearrange("p s (k d) -> p s k d", d=D)
        rows_t = gated
        hid_t = wgu[:].rearrange("p a e f -> p (a e f)").rearrange("p (s f t) -> p s f t", s=2, f=F1 // P)
        y_rows = act_t.rearrange("p s (k d) -> p s k d", d=D)
        y_all = attn_f32[:].rearrange("p a b (c d) -> p (a b c) d", d=D)
        slots_dram = nc.dram_tensor("slots_dram", [2 * TOKENS, D], F32, kind="Internal").ap()
        y_dram = nc.dram_tensor("y_dram", [TOKENS, D], F32, kind="Internal").ap()

        loads = sem("loads")
        loads_late = sem("loads_late")
        x_first = sem("x_first")
        x_load = sem("x_load")
        sel_load = sem("sel_load")
        select_ready = sem("select_ready")
        zeros_ready = sem("zeros_ready")
        ones_ready = sem("ones_ready")
        rotated = sem("rotated")
        zero_store = sem("zero_store")
        pro_dve = sem("pro_dve")
        pro_pe = sem("pro_pe")
        pro_act = sem("pro_act")
        x_done = sem("x_done")
        res_done = sem("res_done")
        c_bcast_done = sem("c_bcast_done")
        mod_mm = sem("mod_mm")
        mod_out = sem("mod_out")
        mod_scale = sem("mod_scale")
        gate_a = sem("gate_a")
        gate_b = sem("gate_b")
        stats_done = sem("stats_done")
        mv_done = sem("mv_done")
        var_done = sem("var_done")
        rstd_done = sem("rstd_done")
        xhat_done = sem("xhat_done")
        h_mul = sem("h_mul")
        h_done = sem("h_done")
        ssq_done = sem("ssq_done")
        ssq_eps_done = sem("ssq_eps_done")
        rrms_done = sem("rrms_done")
        hn_done = sem("hn_done")
        ht_mm = sem("ht_mm")
        ht_out = sem("ht_out")
        q_mm = sem("q_mm")
        q_rope = sem("q_rope")
        q_sum = sem("q_sum")
        qd_mm = sem("qd_mm")
        q_hi = sem("q_hi")
        q_lo = sem("q_lo")
        k_mm = sem("k_mm")
        k_rope = sem("k_rope")
        k_sum = sem("k_sum")
        k_lo = sem("k_lo")
        v_mm = sem("v_mm")
        v_out = sem("v_out")
        sel_mm = sem("sel_mm")
        sel_out = sem("sel_out")
        window_open = sem("window_open")
        max_mm = sem("max_mm")
        max_done = sem("max_done")
        mt_mm = sem("mt_mm")
        mt_hi = sem("mt_hi")
        mt_out = sem("mt_out")
        exp_mm = sem("exp_mm")
        exp_done = sem("exp_done")
        values_mm = sem("values_mm")
        strips_out = sem("strips_out")
        combined = sem("combined")
        place_mm = sem("place_mm")
        place_done = sem("place_done")
        recip_done = sem("recip_done")
        o_done = sem("o_done")
        ot_mm = sem("ot_mm")
        ot_out = sem("ot_out")
        y_mm = sem("y_mm")
        y_out = sem("y_out")

        moe_done = sem("moe_done")
        rt_stats = sem("rt_stats")
        rt_mv = sem("rt_mv")
        rt_var = sem("rt_var")
        rt_rstd = sem("rt_rstd")
        rt_xhat = sem("rt_xhat")
        rt_mul = sem("rt_mul")
        rt_h = sem("rt_h")
        rt_kept = sem("rt_kept")
        rt_ssq = sem("rt_ssq")
        rt_ht_mm = sem("rt_ht_mm")
        rt_ht_out = sem("rt_ht_out")
        rt_logit_mm = sem("rt_logit_mm")
        rt_logit = sem("rt_logit")
        rt_chain = sem("rt_chain")
        rt_diff = sem("rt_diff")
        rt_exp = sem("rt_exp")
        rt_onehot = sem("rt_onehot")
        rt_rank_mm = sem("rt_rank_mm")
        routed = sem("routed")
        w_hi_done = sem("w_hi_done")
        w_lo_done = sem("w_lo_done")
        x_hi_done = sem("x_hi_done")
        x_lo_done = sem("x_lo_done")
        gu_mm = sem("gu_mm")
        tanh_done = sem("tanh_done")
        gated_done = sem("gated_done")
        act_done = sem("act_done")
        down_mm = sem("down_mm")
        weight_done = sem("weight_done")
        acc_done = sem("acc_done")
        moe_sum = sem("moe_sum")
        moe_clip = sem("moe_clip")
        moe_gated = sem("moe_gated")
        scattered = sem("scattered")
        rows_load = [sem("rows_load0"), sem("rows_load1")]
        w1_load = [sem("w1_load0"), sem("w1_load1")]
        w2_load = [sem("w2_load0"), sem("w2_load1")]
        xt_mm = sem("xt_mm")
        xt_out = sem("xt_out")
        up_mm = sem("up_mm")
        relu_done = sem("relu_done")
        ffn_mm = sem("ffn_mm")
        ffn_out = sem("ffn_out")
        ffn_store = [sem("ffn_store0"), sem("ffn_store1")]
        gathered = [sem("gathered%d" % n) for n in range(NB // 2)]
        y_gated = sem("y_gated")
        final_done = sem("final_done")
        out_store = sem("out_store")

        X = a["L0_attn_x"].rearrange("b (k p) d -> p (b k) d", p=P)
        OUT = out.rearrange("b (k p) d -> p (b k) d", p=P)
        place_stage = res_words[:, 11 * P:11 * P + 2 * GROUPS * P]
        first_loads = [
            (ident, a["squares"][:, 0, :]), (c_rows[:, 0, :], a["L0_c"]), (c_rows[:, 1, :], a["L1_c"]),
            (dirs[:, 0:3], a["L0_attn_head_dirs"]),
            (dirs[:, 3:4], a["L0_attn_head_scales"].rearrange("(h o) -> h o", o=1)),
            (wmod[:, 0, :], a["L0_wmod"]), (wmod[:, 1, :], a["L1_wmod"]),
            (wq[:, 0, 0, :], a["L0_attn_Wq"]), (wk[0][:, 0, :], a["L0_attn_Wk"]),
            (wv[0], a["L0_attn_Wv"]), (wo[:, 0, :], a["L0_attn_Wo"]),
            (rope[:], a["rope"]), (strips[:], a["strips"]), (squares, a["squares"]),
            (place_stage, a["max_place"].rearrange("p k g m -> p (k g m)")),
        ]
        late_loads = [
            (expert_c[:], a["experts"]), (wq[:, 1, 0, :], a["L0_ffn_Wq"]), (wk[1][:, 0, :], a["L0_ffn_Wk"]),
            (wv[1], a["L0_ffn_Wv"]), (wo[:, 1, :], a["L0_ffn_Wo"]),
            (ln_w[:, 0:1], a["L0_ffn_ln1_w"].rearrange("(h o) -> h o", o=1)),
            (ln_w[:, 1:2], a["L0_ffn_ln2_w"].rearrange("(h o) -> h o", o=1)),
            (wq[:, 2, 0, :], a["L1_attn_WqT"]), (wk[2][:, 0, :], a["L1_attn_WkT"]),
            (wv[2], a["L1_attn_WvT"]), (wo[:, 2, :], a["L1_attn_WoT"]),
            (wr[:, 0, :], a["L0_ffn_Wr"]), (wr[:, 1, :], a["L1_ffn_Wr"]),
            (wg, a["L0_ffn_Wg"].rearrange("e d f -> d e f")),
            (wu, a["L0_ffn_Wu"].rearrange("e d f -> d e f")),
            (wd[:], a["L0_ffn_Wd"].rearrange("e (c p) d -> p e c d", p=P)),
        ]

        def n_of(c, b):
            return b + c.first

        PREP = ["stat", "mod", "xhat", "sq", "hn", "ht", "q", "k", "qd", "v", "sel0", "sel1", "sel2", "sel3"]
        POST = ["combine", "ot", "y"]
        MAXIMA = ["rows", "place0", "place1"]
        ROUTE = ["rstat", "rmul", "rht", "rlog"]

        def order(c):
            return (["stat", "mod", "combine", "xhat", "ot"] + (["sq", "y", "hn", "ht"] if c.index == 1 else ["ht", "y"])
                    + (["q", "k", "qd", "v", "sel0", "sel1", "sel2", "rows", "sel3"] if c.index == 0 else
                       ["q", "k", "rstat", "v", "sel0", "rmul", "sel1", "sel2", "rht", "sel3", "rows", "rlog"])
                    + ["place0", "place1"])

        def prep_names(c):
            return [n for n in PREP if n in order(c)]

        def post_names(c):
            return [n for n in order(c) if n in POST + ROUTE]

        NO_PE = ["stat", "xhat", "sq", "hn", "rstat", "rmul"]

        def bank_of(c, name):
            return [n for n in order(c) if n not in NO_PE].index(name) % 2

        def routed_before(c, b):
            return (c.index - 1) * NB + b

        def slots(c, with_post, with_prep, with_next):
            names = order(c)
            early = 3 * c.heads // 4
            table = [([], [], []) for _ in range(c.heads)]
            if with_next:
                for h in range(c.heads):
                    table[h * early // c.heads][0].append(h)
            for j, name in enumerate(names):
                at = 2 + j * (2 * c.heads - 2) // len(names)
                if j < 3:
                    at = (1, 3, 4)[j]
                if (name in POST + ROUTE and with_post) or (name in PREP and with_prep) or (name in MAXIMA and with_next):
                    table[at // 2][1 + at % 2].append(name)
            return table

        def opening(c):
            names = prep_names(c)
            return [(name, range(j * c.heads // len(names), (j + 1) * c.heads // len(names)))
                    for j, name in enumerate(names)]

        def walk(c, b, r, post, prep, maxima, names):
            for name in names:
                if name in POST + ROUTE:
                    post(c, b - 1, (r - 1) % RING, name)
                elif name in MAXIMA:
                    maxima(c, b + 1, (r + 1) % RING, name)
                else:
                    prep(c, b + 2, (r + 2) % RING, name)

        def last_entry(b):
            return isinstance(b, int) and b == NB - 1

        def beside(c, b, h, part):
            return c.index == 2 and last_entry(b) and h == SOON_HEADS[part]

        def at_least(eng, semaphore, value):
            if not isinstance(value, int) or value > 0:
                eng.wait_ge(semaphore, value)

        def pairs_until(c, b):
            if isinstance(b, int) and b < 0:
                return PAIRS_BEFORE[c.index]
            return (b + 1) * c.pairs + PAIRS_BEFORE[c.index]

        def run(eng, c, start, segment, finish):
            start(c)
            segment(c, 0, 0)
            with eng.Fori(0, (NB - RING) // RING) as g:
                for r in range(RING):
                    segment(c, g * RING + (1 + r), (1 + r) % RING)
            for b in range(NB - RING + 1, NB):
                segment(c, b, b % RING)
            finish(c)

        def heads_until(c, b):
            if isinstance(b, int) and b < 0:
                return HEADS_BEFORE[c.index]
            return (b + 1) * c.heads + HEADS_BEFORE[c.index]

        def v_in_work(c):
            return work[bank_of(c, "v")][:, 0:S].rearrange("p (k c) -> p k c", k=BLK)[:, :, 0:c.kv * c.hd].rearrange(
                "p k (h e) -> p k h e", e=c.hd)

        def flags(b):
            if not isinstance(b, int):
                return True, True, True
            return b > 0, b + 2 < NB, b + 1 < NB

        block = ctx.enter_context(nc.Block())

        def block_of(x, i):
            return x[:, bass.ds(i, 1), :].rearrange("p o d -> p (o d)")

        SOON = (NB - 2) * BLK
        TURNS = ((0, 0, NB * BLK, NB), (1, 0, SOON, NB + NB - 2), (1, SOON, NB * BLK, 2 * NB))
        SOON_SCATTER = 18
        SOON_HEADS = {"softmax": 3, "exp": 3, "rank_mm": 7, "rank": 7}

        def sp_tail(sp):
            def load_w1(e, s):
                at_least(sp, up_mm, 4 * e - 4)
                sp.dma_start(w1[:, s, :], a["L1_ffn_W1"][bass.ds(e, 1), :, :].rearrange("o d f -> d (o f)")
                             ).then_inc(w1_load[s], 16)

            def load_w2(e, s):
                at_least(sp, ffn_mm, e - 1)
                sp.dma_start(w2[:, s], a["L1_ffn_W2"][bass.ds(e, 1), :, :].rearrange("o (c p) d -> p (o c) d", p=P)
                             ).then_inc(w2_load[s], 16)

            def load_rows(e, s):
                at_least(sp, xt_mm, e - 1)
                sp.dma_start(rows_e[:, s].rearrange("p k d -> p (k d)"),
                             slots_dram[bass.ds(e * CAP, CAP), :].rearrange("(p k) d -> p (k d)", p=P)
                             ).then_inc(rows_load[s], 16)

            def store(e, s):
                sp.wait_ge(ffn_out, e + 1)
                sp.dma_start(y_dram[bass.ds(e * CAP, CAP), :].rearrange("(p k) d -> p (k d)", p=P),
                             y_rows[:, s].rearrange("p k d -> p (k d)")).then_inc(ffn_store[s], 16)

            for e in range(2):
                load_w1(e, e)
                load_w2(e, e)
            sp.wait_ge(values_mm, heads_until(CFGS[2], NB - 1))
            sp.wait_ge(scattered, 16 * NB * BLK)
            load_rows(0, 0)
            load_rows(1, 1)
            with sp.Fori(0, E1 // 2 - 1) as g:
                for s in range(2):
                    load_rows(g * 2 + (2 + s), s)
                    load_w1(g * 2 + (2 + s), s)
                    load_w2(g * 2 + (2 + s), s)
                    store(g * 2 + s, s)
            store(E1 - 2, 0)
            store(E1 - 1, 1)

            def put(b):
                sp.wait_ge(final_done, b + 1)
                sp.dma_start(OUT[:, bass.ds(b * BLK, BLK), :], x_all[:, bass.ds(b * BLK, BLK), :]
                             ).then_inc(out_store, 16)

            with sp.Fori(0, NB) as b:
                put(b)
            sp.wait_ge(out_store, 16 * NB)

        def pool_moe(pool):
            def chunk(t, s):
                pool.wait_ge(moe_gated, t + 1)
                xs = x_all[:, bass.ds(t * 4, 4), :]
                nc.gpsimd.tensor_tensor(xs, xs, moe_y[:, s], ALU.add).then_inc(moe_done, 1)

            with pool.Fori(0, NB // 4) as g:
                for s in range(2):
                    chunk(g * 2 + s, s)

        def scatter(pool, first, last):
            for k in range(first, last):
                nc.gpsimd.indirect_dma_start(slots_dram[:], bass.IndirectOffsetOnAxis(ap=slot_put[:, k:k + 1], axis=0),
                                             res_all[:, k, :], None).then_inc(scattered, 16)

        def pool_route1(pool):
            pool.wait_ge(routed, 2)
            pool.wait_ge(rt_kept, NB)
            scatter(pool, SOON, NB * BLK)
            for s in range(2):
                pool.wait_ge(ffn_store[s], 16 * (E1 // 2))
            for k in range(NB * BLK):
                nc.gpsimd.indirect_dma_start(y_all[:, k, :], None, y_dram[:],
                                             bass.IndirectOffsetOnAxis(ap=slot_get[:, k:k + 1], axis=0)
                                             ).then_inc(gathered[k // (2 * BLK)], 16)

        def act_prologue(act):
            act.wait_ge(pro_pe, 1)
            nc.scalar.activation(rt_of[0][:, 0, 0:2 * NB // 8, :].rearrange("p a b -> p (a b)"), ps_work[:, 0:2 * NB],
                                 ACT.Exp, scale=-1.0).then_inc(pro_act, 1)

        def act_route(act, turn):
            layer, lo, hi, _ = TURNS[turn]
            act.wait_ge(rt_diff, turn + 1)
            nc.scalar.activation(rt_of[layer][:, 1, lo:hi], rt_of[layer][:, 0, lo:hi], ACT.Exp).then_inc(rt_exp, 1)

        pairs = ((ps_four[:, 0, :], ps_four[:, 1, :]), (ps_four[:, 2, :], ps_four[:, 3, :]), (ps_out[:], ps_work[:]))
        UNITS = 2 * E0
        pair_of = [u % 3 for u in range(UNITS - 1)] + [1]

        def since(u):
            return next(k for k in range(1, UNITS) if pair_of[(u - k) % UNITS] == pair_of[u])

        def act_weights(act, r):
            act.wait_ge(exp_mm, heads_until(CFGS[1], NB - RING + r))
            nc.scalar.copy(w_hi[:, 2 * r:2 * r + 2], wgu[:, :, 2 * r:2 * r + 2, :].rearrange("p i e f -> p e i f")
                           ).then_inc(w_hi_done, 1)

        def act_moe(act):
            def rows(t, s):
                nc.scalar.copy(x_split[:, s, 0, :], ht_all[:, bass.ds(t * 512, 512)]).then_inc(x_hi_done, 1)

            act.wait_ge(sel_mm, 4 * CFGS[2].first)
            act.wait_ge(rt_ht_out, NB)
            rows(0, 0)
            act_route(act, 0)

            def chunk(t, s, last=False):
                for u in range(2 * E0):
                    n = t * 2 * E0 + u
                    act.wait_ge(gu_mm, n + 1)
                    at_least(act, gated_done, n - 1)
                    nc.scalar.activation(tanh_g[:, u % 2, :], pairs[pair_of[u]][0], ACT.Tanh,
                                         scale=0.5).then_inc(tanh_done, 1)
                    if u == E0 and not last:
                        rows(t + 1, 1 - s)
            chunk(0, 0)
            with act.Fori(0, TOKENS // 1024 - 1) as g:
                chunk(g * 2 + 1, 1)
                chunk(g * 2 + 2, 0)
            chunk(TOKENS // 512 - 1, 1, last=True)

        def act_route1(act):
            act_route(act, 2)

            def copy_rows(e, s):
                act.wait_ge(xt_mm, e + 1)
                at_least(act, up_mm, 4 * e - 4)
                nc.scalar.copy(rows_t[:, s, :], ps_work[:]).then_inc(xt_out, 1)

            def expert(e, s, last=False):
                for f in range(F1 // P):
                    act.wait_ge(up_mm, 4 * e + f + 1)
                    at_least(act, ffn_mm, e - 1)
                    nc.scalar.activation(hid_t[:, s, f, :], ps_four[:, f, :], ACT.Relu
                                         ).then_inc(relu_done, 1)
                if not last:
                    copy_rows(e + 1, 1 - s)

            copy_rows(0, 0)
            for e in range(2):
                expert(e, e)
            with act.Fori(0, E1 // 2 - 2) as g:
                for s in range(2):
                    expert(g * 2 + (2 + s), s)
            expert(E1 - 2, 0)
            expert(E1 - 1, 1, last=True)

        def dve_prologue(dve):
            nc.vector.memset(dir_rows[:], 0.0).then_inc(pro_dve, 1)
            dve.wait_ge(loads, 16 * len(first_loads))
            dve.wait_ge(pro_dve, 1)
            nc.vector.tensor_tensor(dir_rows[:, 0, :].rearrange("p (h e) -> p h e", e=16)[:, :, 0:3],
                                    ident[0:8, 0:8].unsqueeze(2).to_broadcast([8, 8, 3]),
                                    dirs[:, 0:3].unsqueeze(1).to_broadcast([8, 8, 3]), ALU.mult).then_inc(pro_dve, 1)
            dve.wait_ge(pro_dve, 2)
            nc.vector.tensor_scalar(dir_rows[:, 1, :], dir_rows[:, 0, :], dirs[:, 3:4], None,
                                    ALU.mult).then_inc(pro_dve, 1)
            dve.wait_ge(pro_act, 1)
            e = rt_of[0][:, 0, 0:2 * NB // 8, :].rearrange("p a b -> p (a b)")
            nc.vector.tensor_scalar(e, e, 1.0, None, ALU.add).then_inc(pro_dve, 1)
            dve.wait_ge(pro_dve, 4)
            nc.vector.reciprocal(e, e).then_inc(pro_dve, 1)
            dve.wait_ge(pro_dve, 5)
            nc.vector.tensor_tensor(silu_c[:].rearrange("p l b -> p (l b)"), ps_work[:, 0:2 * NB], e,
                                    ALU.mult).then_inc(pro_dve, 1)
            dve.wait_ge(pro_dve, 6)
            dve.wait_ge(pro_pe, 2)
            nc.vector.scalar_tensor_tensor(dir_mix[:], ident, 0.25, ps_work[:, P:2 * P], ALU.mult,
                                           ALU.add).then_inc(pro_dve, 1)
            dve.wait_ge(pro_pe, 3)
            both = ps_work[:, 0:4 * NB].rearrange("p (l k b) -> p l k b", l=2, k=2)
            nc.vector.tensor_copy(mod_t[:, :, 0, :], both[:, :, 0, :])
            nc.vector.tensor_scalar(mod_t[:, :, 1, :], both[:, :, 1, :], 1.0, None, ALU.add).then_inc(pro_dve, 1)
            nc.vector.memset(o_strips, 0.0)
            nc.vector.tensor_copy(q_masks[:, 0, :], squares[:, 1, :])
            nc.vector.tensor_copy(q_masks[:, 1, :], squares[:, 2, :])
            nc.vector.tensor_copy(q_masks[:, 2, :], squares[:, 1, :]).then_inc(pro_dve, 1)
            dve.wait_ge(pro_dve, 9)
            nc.vector.tensor_copy(max_place[:].rearrange("p k g m -> p (k g m)"), place_stage).then_inc(pro_dve, 1)

        chain = [0]

        def link(dve, ins):
            chain[0] += 1
            ins.then_inc(rt_chain, 1)
            dve.wait_ge(rt_chain, chain[0])

        def dve_softmax(dve, turn):
            layer, lo, hi, seen = TURNS[turn]
            rt = rt_of[layer][:, :, lo:hi]
            rows = rt1[:, :, lo:hi]
            shape = [P, hi - lo, 8]

            def wide(x):
                return x.unsqueeze(2).to_broadcast(shape)

            index_down = expert_c[:, 0:1, :].to_broadcast(shape)

            def first_of(prob, best, hot):
                link(dve, nc.vector.tensor_reduce(best, prob, AX_X, ALU.max))
                link(dve, nc.vector.tensor_tensor(rt[:, 3], prob, wide(best), ALU.is_equal))
                link(dve, nc.vector.tensor_tensor(rt[:, 3], rt[:, 3], index_down, ALU.mult))
                link(dve, nc.vector.tensor_reduce(rows[:, 5, :], rt[:, 3], AX_X, ALU.max))
                link(dve, nc.vector.tensor_tensor(hot, rt[:, 3], wide(rows[:, 5, :]), ALU.is_equal))

            dve.wait_ge(rt_logit, seen)
            link(dve, nc.vector.tensor_reduce(rows[:, 0, :], logits[:, lo:hi], AX_X, ALU.max))
            nc.vector.tensor_tensor(rt[:, 0], logits[:, lo:hi], wide(rows[:, 0, :]), ALU.subtract).then_inc(rt_diff, 1)
            dve.wait_ge(rt_exp, turn + 1)
            link(dve, nc.vector.tensor_reduce(rows[:, 1, :], rt[:, 1], AX_X, ALU.add))
            link(dve, nc.vector.reciprocal(rows[:, 2, :], rows[:, 1, :]))
            link(dve, nc.vector.tensor_tensor(rt[:, 1], rt[:, 1], wide(rows[:, 2, :]), ALU.mult))
            first_of(rt[:, 1], rows[:, 3, :], rt[:, 2])
            if layer == 0:
                link(dve, nc.vector.scalar_tensor_tensor(rt[:, 4], rt[:, 2], -2.0, rt[:, 1], ALU.mult, ALU.add))
                first_of(rt[:, 4], rows[:, 4, :], rt[:, 5])
                link(dve, nc.vector.tensor_tensor(rt[:, 2], rt[:, 2], rt[:, 5], ALU.add))
                link(dve, nc.vector.tensor_tensor(rt[:, 2], rt[:, 2], rt[:, 1], ALU.mult))
                link(dve, nc.vector.tensor_reduce(rows[:, 6, :], rt[:, 2], AX_X, ALU.add))
                link(dve, nc.vector.reciprocal(rows[:, 7, :], rows[:, 6, :]))
                link(dve, nc.vector.scalar_tensor_tensor(rt[:, 2], rt[:, 2], 0.5, wide(rows[:, 7, :]), ALU.mult,
                                                         ALU.mult))
            else:
                nc.vector.tensor_copy(one_hot[:, lo:hi], rt[:, 2]).then_inc(rt_onehot, 1)

        def dve_rank(dve, turn):
            layer, lo, hi, _ = TURNS[turn]
            rt = rt_of[layer][:, :, lo:hi]
            rows = rt1[:, :, lo:hi]
            n = hi - lo
            so_far = rt_of[layer][:, 6, 0:1]
            dve.wait_ge(rt_rank_mm, turn)
            earlier = ps_max[:, 0, lo * 8:hi * 8].rearrange("p (k e) -> p k e", e=8)
            counts = ps_max[:, 1, lo * 8:hi * 8].rearrange("p (k e) -> p k e", e=8)
            link(dve, nc.vector.tensor_copy(rt[:, 3], counts))
            if lo > 0:
                link(dve, nc.vector.tensor_tensor(rt[:, 3, 0:1], rt[:, 3, 0:1], so_far, ALU.add))
            src, dst = 3, 4
            shift = 1
            while shift < n:
                nc.vector.tensor_copy(rt[:, dst, 0:shift], rt[:, src, 0:shift])
                link(dve, nc.vector.tensor_tensor(rt[:, dst, shift:], rt[:, src, shift:], rt[:, src, 0:n - shift],
                                                  ALU.add))
                src, dst = dst, src
                shift *= 2
            if lo == 0:
                link(dve, nc.vector.tensor_copy(so_far, rt[:, src, n - 1:n]))
            link(dve, nc.vector.tensor_tensor(rt[:, src], rt[:, src], counts, ALU.subtract))
            link(dve, nc.vector.tensor_tensor(rt[:, src], rt[:, src], earlier, ALU.add))
            link(dve, nc.vector.tensor_tensor(rt[:, src], rt[:, src], rt[:, 2], ALU.mult))
            nc.vector.tensor_reduce(rows[:, 6, :], rt[:, src], AX_X, ALU.add)
            link(dve, nc.vector.tensor_tensor(rt[:, 5], rt[:, 2], expert_c[:, 1:2, :].to_broadcast([P, n, 8]),
                                              ALU.mult))
            nc.vector.tensor_reduce(rows[:, 7, :], rt[:, 5], AX_X, ALU.add)
            token = expert_c[:, 2:6, :].rearrange("p a b -> p (a b)")[:, lo:hi]
            link(dve, nc.vector.tensor_scalar(rows[:, 8, :], rows[:, 6, :], float(CAP), None, ALU.is_lt))
            link(dve, nc.vector.tensor_tensor(rows[:, 7, :], rows[:, 7, :], rows[:, 6, :], ALU.add))
            link(dve, nc.vector.tensor_tensor(rows[:, 9, :], rows[:, 7, :], token, ALU.subtract))
            link(dve, nc.vector.tensor_tensor(rows[:, 9, :], rows[:, 9, :], rows[:, 8, :], ALU.mult))
            nc.vector.tensor_tensor(slot_get[:, lo:hi], rows[:, 7, :], rows[:, 8, :], ALU.mult)
            nc.vector.tensor_tensor(rows[:, 3, :], rows[:, 3, :], rows[:, 8, :], ALU.mult)
            nc.vector.tensor_tensor(slot_put[:, lo:hi], rows[:, 9, :], token, ALU.add).then_inc(routed, 1)
            dve.wait_ge(routed, turn)

        def dve_weights(dve, r):
            dve.wait_ge(w_hi_done, r + 1)
            nc.vector.tensor_tensor(w_lo[:, 2 * r:2 * r + 2],
                                    wgu[:, :, 2 * r:2 * r + 2, :].rearrange("p i e f -> p e i f"),
                                    w_hi[:, 2 * r:2 * r + 2].bitcast(F32), ALU.subtract).then_inc(w_lo_done, 1)

        def dve_moe(dve):
            def rows(t, s):
                dve.wait_ge(x_hi_done, t + 1)
                nc.vector.tensor_tensor(x_split[:, s, 1, :], ht_all[:, bass.ds(t * 512, 512)],
                                        x_split[:, s, 0, :].bitcast(F32), ALU.subtract).then_inc(x_lo_done, 1)

            rows(0, 0)
            dve_softmax(dve, 0)

            def accumulate(t, e):
                dve.wait_ge(down_mm, 2 * (t * E0 + e) + 2)
                at_least(dve, acc_done, t * E0 + e)
                if e == 0:
                    dve.wait_ge(weight_done, t + 1)
                    at_least(dve, moe_sum, t)
                for k in range(4):
                    y = ps_max[:, e % 2, k * D:(k + 1) * D]
                    if e == 0:
                        ins = nc.vector.tensor_scalar(acc[:, k, :], y, weight_t[:, k, e:e + 1], None, ALU.mult)
                    else:
                        ins = nc.vector.scalar_tensor_tensor(acc[:, k, :], y, weight_t[:, k, e:e + 1],
                                                             acc[:, k, :], ALU.mult, ALU.add)
                ins.then_inc(acc_done, 1)

            def end(t, s):
                accumulate(t, E0 - 1)
                dve.wait_ge(acc_done, (t + 1) * E0)
                at_least(dve, moe_done, t - 1)
                nc.vector.tensor_tensor(moe_y[:, s], acc[:], res_all[:, bass.ds(t * 4, 4), :], ALU.add
                                        ).then_inc(moe_sum, 1)
                dve.wait_ge(moe_sum, t + 1)
                nc.vector.tensor_scalar(moe_y[:, s], moe_y[:, s], CLIP, -CLIP, ALU.min, ALU.max
                                        ).then_inc(moe_clip, 1)
                dve.wait_ge(moe_clip, t + 1)
                for k in range(2):
                    ins = nc.vector.tensor_tensor(moe_y[:, s, 2 * k:2 * k + 2, :], moe_y[:, s, 2 * k:2 * k + 2, :],
                                                  gates_all[:, bass.ds(t * 2 + k, 1), :].to_broadcast([P, BLK, D]),
                                                  ALU.mult)
                ins.then_inc(moe_gated, 1)

            def chunk(t, s, first=False, last=False):
                def unit(u):
                    n = t * 2 * E0 + u
                    gate, up = pairs[pair_of[u]]
                    dve.wait_ge(tanh_done, n + 1)
                    nc.vector.scalar_tensor_tensor(gated[:, u % 2, :], tanh_g[:, u % 2, :], 1.0,
                                                   gate, ALU.add, ALU.mult).then_inc(gated_done, 1)
                    dve.wait_ge(gated_done, n + 1)
                    at_least(dve, down_mm, n - 1)
                    nc.vector.tensor_tensor(act_t[:, u % 2, :], gated[:, u % 2, :], up, ALU.mult).then_inc(act_done, 1)

                for e in range(E0):
                    unit(2 * e)
                    unit(2 * e + 1)
                    if e == 0:
                        if not first:
                            end(t - 1, 1 - s)
                        at_least(dve, acc_done, t * E0)
                        nc.vector.tensor_copy(weight_t[:], rt_of[0][:, 2, bass.ds(t * 4, 4), :]
                                              ).then_inc(weight_done, 1)
                    else:
                        accumulate(t, e - 1)
                    if e == E0 // 2 and not last:
                        rows(t + 1, 1 - s)
                if last:
                    end(t, s)

            chunk(0, 0, first=True)
            chunk(1, 1)
            with dve.Fori(0, TOKENS // 1024 - 2) as g:
                for s in range(2):
                    chunk(g * 2 + (2 + s), s)
            chunk(TOKENS // 512 - 2, 0)
            chunk(TOKENS // 512 - 1, 1, last=True)

        def dve_route1(dve):
            dve_softmax(dve, 2)
            dve_rank(dve, 2)

            def expert(e, s):
                dve.wait_ge(ffn_mm, e + 1)
                if not isinstance(e, int) or e >= 2:
                    dve.wait_ge(ffn_store[s], 8 * (e - s))
                nc.vector.tensor_copy(y_rows[:, s].rearrange("p k d -> p (k d)"), ps_max[:, s, :]).then_inc(ffn_out, 1)
            for e in range(2):
                expert(e, e)
            with dve.Fori(0, E1 // 2 - 1) as g:
                for s in range(2):
                    expert(g * 2 + (2 + s), s)
            for b in range(NB):
                dve.wait_ge(gathered[b // 2], 16 * 2 * BLK)
                for k in range(BLK):
                    j = b * BLK + k
                    last = nc.vector.scalar_tensor_tensor(y_all[:, j, :], y_all[:, j, :], rt1[:, 3, j:j + 1],
                                                          gates_all[:, b, :], ALU.mult, ALU.mult)
                last.then_inc(y_gated, 1)
                dve.wait_ge(y_gated, b + 1)
                xs = x_all[:, b * BLK:(b + 1) * BLK, :]
                nc.vector.tensor_tensor(xs, xs, y_all[:, b * BLK:(b + 1) * BLK, :], ALU.add).then_inc(final_done, 1)

        def pe_prologue(pe):
            pe.wait_ge(loads, 16 * len(first_loads))
            for layer in range(2):
                last = nc.tensor.transpose(ps_work[:, layer * NB:(layer + 1) * NB], c_rows[:, layer, :],
                                           ident[0:NB, 0:NB])
            last.then_inc(pro_pe, 1)
            pe.wait_ge(pro_dve, 6)
            nc.tensor.matmul(ps_work[:, P:2 * P], dir_rows[:, 0, :], dir_rows[:, 1, :], start=True, stop=True
                             ).then_inc(pro_pe, 1)
            pe.wait_ge(pro_dve, 7)
            for layer in range(2):
                for k in range(2):
                    last = nc.tensor.matmul(ps_work[:, (2 * layer + k) * NB:(2 * layer + k + 1) * NB],
                                            wmod[:, layer, k * D:(k + 1) * D], silu_c[:, layer, :],
                                            start=True, stop=True)
            last.then_inc(pro_pe, 1)
            pe.wait_ge(pro_dve, 10)
            pe.wait_ge(ones_ready, 2)

        def pe_moe(pe):
            pe.wait_ge(rt_logit, NB)
            pe.wait_ge(w_lo_done, E0 // 2)

            def chunk(t, s, first=False, last_one=False):
                pe.wait_ge(x_lo_done, t + 1)
                x_hi, x_lo = x_split[:, s, 0, :], x_split[:, s, 1, :]

                def up(u):
                    n = t * 2 * E0 + u
                    e, f = u // 2, u % 2
                    if not isinstance(t, int) or n >= since(u):
                        pe.wait_ge(act_done, n + 1 - since(u))
                    for i in range(2):
                        hi, lo = w_hi[:, e, i, f * P:(f + 1) * P], w_lo[:, e, i, f * P:(f + 1) * P]
                        for j, (w, x) in enumerate(((hi, x_hi), (hi, x_lo), (lo, x_hi))):
                            last = nc.tensor.matmul(pairs[pair_of[u]][i], w, x, start=(j == 0), stop=(j == 2))
                    last.then_inc(gu_mm, 1)

                def down(t, u):
                    n = t * UNITS + u
                    e, f = u // 2, u % 2
                    pe.wait_ge(act_done, n + 1)
                    if f == 0:
                        at_least(pe, acc_done, t * E0 + e - 1)
                    for k in range(4):
                        last = nc.tensor.matmul(ps_max[:, e % 2, k * D:(k + 1) * D], act_t[:, f, k * P:(k + 1) * P],
                                                wd[:, e, f, :], start=(f == 0 and k == 0), stop=(f == 1),
                                                skip_group_check=True)
                    last.then_inc(down_mm, 1)

                for u in range(UNITS):
                    up(u)
                    if u > 1:
                        down(t, u - 2)
                    elif not first:
                        down(t - 1, UNITS - 2 + u)
                if last_one:
                    down(t, UNITS - 2)
                    down(t, UNITS - 1)

            chunk(0, 0, first=True)
            with pe.Fori(0, TOKENS // 1024 - 1) as g:
                chunk(g * 2 + 1, 1)
                chunk(g * 2 + 2, 0)
            chunk(TOKENS // 512 - 1, 1, last_one=True)

        def pe_rank(pe, turn):
            _, lo, hi, _ = TURNS[turn]
            pe.wait_ge(rt_onehot, turn)
            pe.wait_ge(max_done, HEADS_BEFORE[2] + NB * CFGS[2].heads)
            hot = one_hot[:, lo:hi].rearrange("p k e -> p (k e)")
            nc.tensor.matmul(ps_max[:, 0, lo * 8:hi * 8], upper_ones[:, 0, :], hot, start=True, stop=True)
            nc.tensor.matmul(ps_max[:, 1, lo * 8:hi * 8], upper_ones[:, 1, :], hot, start=True, stop=True
                             ).then_inc(rt_rank_mm, 1)

        def pe_route1(pe):
            pe_rank(pe, 2)

            def turn_rows(e, s):
                pe.wait_ge(rows_load[s], 8 * (e - s) + 16)
                at_least(pe, xt_out, e)
                for k in range(4):
                    last = nc.tensor.transpose(ps_work[:, k * P:(k + 1) * P], rows_e[:, s, k, :], ident)
                last.then_inc(xt_mm, 1)

            def expert(e, s, last_one=False):
                pe.wait_ge(xt_out, e + 1)
                pe.wait_ge(w1_load[s], 8 * (e - s) + 16)
                for f in range(F1 // P):
                    at_least(pe, relu_done, 4 * e + f - 3)
                    nc.tensor.matmul(ps_four[:, f, :], w1[:, s, f * P:(f + 1) * P], rows_t[:, s, :],
                                     start=True, stop=True).then_inc(up_mm, 1)
                if not last_one:
                    turn_rows(e + 1, 1 - s)
                pe.wait_ge(relu_done, 4 * e + 4)
                pe.wait_ge(w2_load[s], 8 * (e - s) + 16)
                at_least(pe, ffn_out, e - 1)
                for k in range(4):
                    for f in range(F1 // P):
                        last = nc.tensor.matmul(ps_max[:, s, k * D:(k + 1) * D], hid_t[:, s, f, k * P:(k + 1) * P],
                                                w2[:, s, f, :], start=(f == 0), stop=(f == F1 // P - 1))
                last.then_inc(ffn_mm, 1)

            pe.wait_ge(routed, 2)
            turn_rows(0, 0)
            for e in range(2):
                expert(e, e)
            with pe.Fori(0, E1 // 2 - 2) as g:
                for s in range(2):
                    expert(g * 2 + (2 + s), s)
            expert(E1 - 2, 0)
            expert(E1 - 1, 1, last_one=True)

        @block.sync
        def _(sp):
            stage_sel = stage.rearrange("p (a b) -> p a b", a=4)
            sel_dram = a["select"].rearrange("p a b g m -> p a b (g m)")
            k = NB * BLK // 8
            for dst, src in first_loads[0:5]:
                sp.dma_start(dst, src).then_inc(loads, 16)
            sp.dma_start(x_all[:, 0:k, :], X[:, 0:k, :]).then_inc(x_first, 16)
            for dst, src in first_loads[5:]:
                sp.dma_start(dst, src).then_inc(loads, 16)
            sp.dma_start(stage_sel, sel_dram[:, 0]).then_inc(sel_load, 16)
            for n in range(1, 8):
                sp.dma_start(x_all[:, n * k:(n + 1) * k, :], X[:, n * k:(n + 1) * k, :]).then_inc(x_load, 16)
            for dst, src in late_loads:
                sp.dma_start(dst, src).then_inc(loads_late, 16)
            sp.wait_ge(zeros_ready, 1)
            for n in range(8):
                sp.dma_start(slots_dram[n * CAP:(n + 1) * CAP, :].rearrange("(p k) d -> p (k d)", p=P),
                             zeros).then_inc(zero_store, 16)
            for n in range(1, 3):
                sp.wait_ge(select_ready, n)
                if n == 2:
                    sp.wait_ge(moe_done, NB // 2)
                sp.dma_start(stage_sel, sel_dram[:, n]).then_inc(sel_load, 16)
            sp_tail(sp)

        @block.gpsimd
        def _(pool):
            def ones_column(c):
                if c.index > 0:
                    pool.wait_ge(values_mm, HEADS_BEFORE[c.index])
                v = v_all[:, 0:RING * BLK * c.kv * (c.hd + 1)].rearrange("p (n e) -> p n e", e=c.hd + 1)
                nc.gpsimd.memset(v[:, :, c.hd:c.hd + 1], 1.0).then_inc(ones_ready, 1)

            nc.gpsimd.memset(zeros, 0.0).then_inc(zeros_ready, 1)
            nc.gpsimd.memset(half_neg[:], -0.5)
            nc.gpsimd.memset(eps[:], LN_EPS)
            nc.gpsimd.memset(one[:], 1.0)
            ones_column(CFGS[0])
            nc.gpsimd.memset(max_t[:].bitcast(F32), 0.0).then_inc(ones_ready, 1)
            pool.wait_ge(loads, 16 * len(first_loads))
            nc.gpsimd.tensor_copy(ident_bf[:], squares[:, 0, :])
            nc.gpsimd.tensor_copy(masks[:], squares[:, 3:5, :])

            def rotate(c):
                for w in (wq[:, c.index], wk[c.index]):
                    half = c.hd // 2
                    src = w[:, 0, :].rearrange("p (h e) -> p h e", e=c.hd)
                    dst = w[:, 1, :].rearrange("p (h e) -> p h e", e=c.hd)
                    if c.layer == 0:
                        nc.gpsimd.tensor_copy(dst[:, :, 0:half], src[:, :, half:])
                        last = nc.gpsimd.tensor_copy(dst[:, :, half:], src[:, :, 0:half])
                    else:
                        nc.gpsimd.tensor_copy(dst[:, :, 0:half], src[:, :, 1::2])
                        last = nc.gpsimd.tensor_copy(dst[:, :, half:], src[:, :, 0::2])
                last.then_inc(rotated, 1)

            rotate(CFGS[0])
            pool.wait_ge(rotated, 1)

            def prep(c, b, r, name):
                n, r2 = n_of(c, b), r % 2
                if name == "stat":
                    pool.wait_ge(mv_done, n + 1)
                    nc.gpsimd.tensor_tensor(var_eps[:, r2, :], mean_var[:, r2, :, 1], eps[:], ALU.add
                                            ).then_inc(var_done, 1)
                    pool.wait_ge(var_done, n + 1)
                    nc.gpsimd.tensor_tensor(rstd[:, r2, :], var_eps[:, r2, :], half_neg[:],
                                            ALU.pow).then_inc(rstd_done, 1)
                if name == "mod" and c.index > 0:
                    pool.wait_ge(mod_out, n + 1)
                    scale = mod[:, r, c.index, :]
                    nc.gpsimd.tensor_tensor(scale, scale, one[:].to_broadcast([P, D]), ALU.add).then_inc(mod_scale, 1)
                if c.index == 1:
                    if name == "xhat":
                        pool.wait_ge(h_mul, n - NB + 1)
                        nc.gpsimd.tensor_tensor(h_tok[:, r], h_tok[:, r],
                                                mod[:, r, 0:1, :].to_broadcast([P, BLK, D]), ALU.add
                                                ).then_inc(h_done, 1)
                    if name == "sq":
                        pool.wait_ge(ssq_done, n - NB + 1)
                        nc.gpsimd.tensor_tensor(ssq_eps[:, r2, :], ssq[:, r2, :], eps[:], ALU.add
                                                ).then_inc(ssq_eps_done, 1)
                        pool.wait_ge(ssq_eps_done, n - NB + 1)
                        nc.gpsimd.tensor_tensor(rrms[:, r2, :], ssq_eps[:, r2, :], half_neg[:],
                                                ALU.pow).then_inc(rrms_done, 1)
                if name in ("q", "k"):
                    i = 0 if name == "q" else 1
                    m = P if name == "q" else c.kv * c.hd
                    rope_done, sum_done, lo_done = ((q_rope, q_sum, q_lo), (k_rope, k_sum, k_lo))[i]
                    pool.wait_ge(rope_done, n + 1)
                    if c.index > 0 or i == 1:
                        at_least(pool, sel_mm, 4 * n)
                    if c.index > 0 or i == 1:
                        nc.gpsimd.tensor_tensor(split[0:m, i, 0, :], rope_a[0:m, i, :], rope_b[0:m, i, :], ALU.add)
                        nc.gpsimd.tensor_tensor(rope_a[0:m, i, :], rope_a[0:m, i, :], rope_b[0:m, i, :],
                                                ALU.add).then_inc(sum_done, 1)
                        pool.wait_ge(sum_done, n + 1)
                        nc.gpsimd.tensor_tensor(split[0:m, i, 1, :], rope_a[0:m, i, :],
                                                split[0:m, i, 0, :].bitcast(F32), ALU.subtract).then_inc(lo_done, 1)
                    else:
                        nc.gpsimd.tensor_tensor(rope_a[0:m, i, :], rope_a[0:m, i, :], rope_b[0:m, i, :],
                                                ALU.add).then_inc(sum_done, 1)

            def post(c, b, r, name):
                if name == "y" and c.index != 1:
                    pool.wait_ge(y_out, n_of(c, b) + 1)
                    xs = x_all[:, bass.ds(b * BLK, BLK), :]
                    nc.gpsimd.tensor_tensor(xs, xs, y_tok[:, r % 2], ALU.add).then_inc(x_done, 1)
                if name == "rstat":
                    m, r2 = routed_before(c, b), r % 2
                    if c.index == 1:
                        pool.wait_ge(rt_ssq, b + 1)
                        nc.gpsimd.tensor_tensor(var_eps_rt[:, r2, :], ssq_rt[:, r2, :], eps[:], ALU.add
                                                ).then_inc(rt_var, 1)
                    else:
                        pool.wait_ge(rt_mv, b + 1)
                        nc.gpsimd.tensor_tensor(var_eps_rt[:, r2, :], mean_var_rt[:, r2, :, 1], var_eps_rt[:, r2, :],
                                                ALU.add).then_inc(rt_var, 1)
                    pool.wait_ge(rt_var, m + 1)
                    nc.gpsimd.tensor_tensor(rstd_rt[:, r2, :], var_eps_rt[:, r2, :], half_neg[:],
                                            ALU.pow).then_inc(rt_rstd, 1)
                if name == "rmul" and c.index == 2:
                    pool.wait_ge(rt_mul, routed_before(c, b) + 1)
                    nc.gpsimd.tensor_tensor(hn_rt[:, r % 2], hn_rt[:, r % 2],
                                            mod[:, r, 1:2, :].to_broadcast([P, BLK, D]), ALU.add).then_inc(rt_h, 1)

            def maxima(c, b, r, name):
                pass

            def start(c):
                if c.index > 0:
                    ones_column(c)
                for b in (0, 1):
                    for name in prep_names(c):
                        prep(c, b, b, name)
                if c.index == 0:
                    pool.wait_ge(loads_late, 16 * len(late_loads))
                    nc.gpsimd.tensor_copy(upper_ones[:], squares[:, 5:7, :]).then_inc(ones_ready, 1)
                    rotate(CFGS[1])
                    rotate(CFGS[2])

            def segment(c, b, r):
                for _, before, behind in slots(c, *flags(b)):
                    walk(c, b, r, post, prep, maxima, before + behind)

            def finish(c):
                if c.index == 2:
                    pool.wait_ge(routed, 1)
                    pool.wait_ge(zero_store, 16 * 8)
                    pool.wait_ge(rt_kept, NB - 2)
                    scatter(pool, 0, SOON_SCATTER)
                for name in post_names(c):
                    post(c, NB - 1, (NB - 1) % RING, name)
                if c.index == 2:
                    scatter(pool, SOON_SCATTER, SOON)

            run(pool, CFGS[0], start, segment, finish)
            run(pool, CFGS[1], start, segment, finish)
            pool_moe(pool)
            run(pool, CFGS[2], start, segment, finish)
            pool_route1(pool)

        @block.scalar
        def _(act):
            act_prologue(act)

            def load_select(c):
                at_least(act, sel_mm, 4 * c.first)
                act.wait_ge(sel_load, 16 * (c.index + 1))
                nc.scalar.copy(select[:].rearrange("p b g m -> p (b g m)"), stage).then_inc(select_ready, 1)

            def prep(c, b, r, name):
                n, r2 = n_of(c, b), r % 2
                if name == "mod":
                    act.wait_ge(mod_mm, n + 1)
                    at_least(act, y_out, n - RING + 1)
                    if c.index == 2:
                        at_least(act, rt_h, b - RING + 1)
                    nc.scalar.copy(mod[:, r, 0:c.parts, :].rearrange("p a d -> p (a d)"),
                                   work[bank_of(c, name)][:, 0:c.parts * D]).then_inc(mod_out, 1)
                if name == "sq":
                    act.wait_ge(h_done, n - NB + 1)
                    at_least(act, ht_mm, n - 1)
                    for k in range(BLK):
                        last = nc.scalar.activation(hn_tok[:, r2, k, :], h_tok[:, r, k, :], ACT.Square, scale=RSQRT_D,
                                                    accum_out=ssq[:, r2, k:k + 1])
                    last.then_inc(ssq_done, 1)
                if name == "ht":
                    act.wait_ge(ht_mm, n + 1)
                    at_least(act, v_mm, n - 1)
                    if c.index == 1:
                        nc.scalar.activation(h_t[:, r2, :], work[bank_of(c, name)][:, 0:S], ACT.Identity,
                                             scale=ln_w[:, 0:1]).then_inc(ht_out, 1)
                    else:
                        nc.scalar.activation(h_t[:, r2, :], work[bank_of(c, name)][:, 0:S], ACT.Identity,
                                             bias=mod_t[:, c.layer, 0, bass.ds(b, 1)],
                                             scale=mod_t[:, c.layer, 1, bass.ds(b, 1)]).then_inc(ht_out, 1)
                if name == "qd":
                    act.wait_ge(qd_mm, n + 1)
                    at_least(act, sel_mm, 4 * n)
                    nc.scalar.copy(split[:, 0, 0, :], work[bank_of(c, name)][:, 0:S]).then_inc(q_hi, 1)
                if name == "v":
                    act.wait_ge(v_mm, n + 1)
                    at_least(act, values_mm, heads_until(c, b - RING))
                    nc.scalar.copy(v_tok[c.index][:, r, :, :, 0:c.hd], v_in_work(c)).then_inc(v_out, 1)
                if name[:3] == "sel":
                    j = int(name[3])
                    act.wait_ge(sel_mm, 4 * n + j + 1)
                    if j % 2 == 0:
                        at_least(act, values_mm, heads_until(c, b - RING))
                    dst = (q_st, k_st)[j // 2][:, r, 2 * (j % 2):2 * (j % 2) + 2, :]
                    src = work[bank_of(c, name)].rearrange("p (g s) -> p g s", g=2)
                    if j < 2:
                        nc.scalar.copy(dst, src).then_inc(sel_out, 1)
                    else:
                        nc.scalar.activation(dst, src, ACT.Identity, bias=strips[:, c.kind, 0:1]
                                             ).then_inc(sel_out, 1)

            def post(c, b, r, name):
                n, r2 = n_of(c, b), r % 2
                if name == "ot":
                    act.wait_ge(ot_mm, n + 1)
                    at_least(act, y_mm, n)
                    nc.scalar.copy(o_t[:, r2, :], work[bank_of(c, name)][:, 0:S]).then_inc(ot_out, 1)
                if name in ROUTE:
                    m = routed_before(c, b)
                if name == "rstat" and c.index == 1:
                    act.wait_ge(res_done, b + 1)
                    for k in range(BLK):
                        last = nc.scalar.activation(hn_rt[:, r2, k, :], block_of(res_all, b * BLK + k),
                                                    ACT.Square, scale=RSQRT_D, accum_out=ssq_rt[:, r2, k:k + 1])
                    last.then_inc(rt_ssq, 1)
                if name == "rht":
                    act.wait_ge(rt_ht_mm, m + 1)
                    src = work[bank_of(c, name)][:, 0:S]
                    if c.index == 1:
                        nc.scalar.activation(ht_all[:, bass.ds(b * S, S)], src, ACT.Identity, scale=ln_w[:, 1:2])
                        nc.scalar.activation(ht_rt[:, r2, :], src, ACT.Identity, scale=ln_w[:, 1:2]
                                             ).then_inc(rt_ht_out, 1)
                    else:
                        nc.scalar.copy(ht_rt[:, r2, :], src).then_inc(rt_ht_out, 1)
                        nc.scalar.copy(res_all[:, bass.ds(b * BLK, BLK), :], hn_rt[:, r2]).then_inc(rt_kept, 1)
                if name == "rlog":
                    act.wait_ge(rt_logit_mm, m + 1)
                    nc.scalar.copy(logits[:, bass.ds(b * BLK, BLK), :],
                                   work[bank_of(c, name)][:, 0:BLK * 8].rearrange("p (k e) -> p k e", e=8)
                                   ).then_inc(rt_logit, 1)

            def maxima(c, b, r, name):
                n, r2 = n_of(c, b), r % 2
                if name != "rows":
                    return
                act.wait_ge(mt_mm, n + 1)
                at_least(act, place_mm, 2 * n - 2)
                nc.scalar.copy(max_t[0:c.heads, r2, :], work[bank_of(c, name)][0:c.heads, 0:S]).then_inc(mt_hi, 1)

            def start(c):
                load_select(c)
                if c.index == 0:
                    act.wait_ge(ones_ready, 2)
                else:
                    act.wait_ge(zero_store, 16 * 8)
                for b in (0, 1):
                    for name in prep_names(c):
                        prep(c, b, b, name)
                maxima(c, 0, 0, "rows")

            def pair_out(c, b, p):
                base = 32 * (p % 4)
                act.wait_ge(values_mm, HEADS_BEFORE[c.index] + b * c.heads + 2 * p + 2)
                if p == 0:
                    at_least(act, combined, n_of(c, b))
                nc.scalar.copy(o_strips[base:base + c.hd + 1, p // 4, :], ps_out[0:c.hd + 1, :]
                               ).then_inc(strips_out, 1)

            def segment(c, b, r):
                w = c.q_cols()
                for h, (_, before, behind) in enumerate(slots(c, *flags(b))):
                    walk(c, b, r, post, prep, maxima, before)
                    hn = HEADS_BEFORE[c.index] + b * c.heads + h
                    act.wait_ge(exp_mm, hn + 1)
                    at_least(act, values_mm, hn - 3)
                    nc.scalar.activation(probs[:, h % 4, 0:w], ps_exp[:, h % 3, 0:w], ACT.Exp, scale=c.scale
                                         ).then_inc(exp_done, 1)
                    if h == 1 and flags(b)[0]:
                        pair_out(c, b - 1, c.pairs - 1)
                    if h % 2 and h > 2:
                        pair_out(c, b, (h - 3) // 2)
                    walk(c, b, r, post, prep, maxima, behind)
                    if beside(c, b, h, "exp"):
                        act_route(act, 1)
                    if c.index == 1 and last_entry(b) and h % 4 == 1 and h // 4 < RING - 1:
                        act_weights(act, h // 4)

            def finish(c):
                pair_out(c, NB - 1, c.pairs - 1)
                for name in post_names(c):
                    post(c, NB - 1, (NB - 1) % RING, name)
                    if c.index == 1 and name == "combine":
                        act_weights(act, RING - 1)

            run(act, CFGS[0], start, segment, finish)
            run(act, CFGS[1], start, segment, finish)
            act_moe(act)
            run(act, CFGS[2], start, segment, finish)
            act_route1(act)

        @block.vector
        def _(dve):
            dve_prologue(dve)

            def prep(c, b, r, name):
                n, r2 = n_of(c, b), r % 2
                if name == "stat":
                    if c.index == 0:
                        if isinstance(b, int) and b < 2:
                            dve.wait_ge(x_first, 16)
                        else:
                            dve.wait_ge(x_load, 16 * 7)
                    elif c.index == 1:
                        dve.wait_ge(x_done, b + 1)
                    else:
                        dve.wait_ge(moe_done, NB // 2)
                    for k in range(BLK):
                        last = nc.vector.bn_stats(stats6[:, r2, k, :], block_of(x_all, b * BLK + k))
                    last.then_inc(stats_done, 1)
                    dve.wait_ge(stats_done, n + 1)
                    at_least(dve, mod_mm, n - 1)
                    nc.vector.tensor_copy(c_bcast[:, r2, :], silu_c[:, c.layer, bass.ds(b, 1)].to_broadcast([P, P])
                                          ).then_inc(c_bcast_done, 1)
                    for k in range(BLK):
                        last = nc.vector.bn_aggr(mean_var[:, r2, k, :], stats6[:, r2, k, :])
                    last.then_inc(mv_done, 1)
                if name == "mod":
                    dve.wait_ge(mod_out, n + 1)
                    for g, part in enumerate(c.gates):
                        gate = mod[:, r, part, :]
                        nc.vector.tensor_scalar(gate_tmp[:, g, 0, :], gate, 0.0, 0.5, ALU.is_ge, ALU.subtract)
                        last = nc.vector.scalar_tensor_tensor(gate_tmp[:, g, 1, :], gate, -1.0, gate, ALU.mult, ALU.max)
                    last.then_inc(gate_a, 1)
                    dve.wait_ge(gate_a, n + 1)
                    for g, part in enumerate(c.gates):
                        last = nc.vector.tensor_scalar(gate_tmp[:, g, 1, :], gate_tmp[:, g, 1, :], 0.25, 2.0,
                                                       ALU.max, ALU.mult)
                    last.then_inc(gate_b, 1)
                    dve.wait_ge(gate_b, n + 1)
                    if c.index > 0 and isinstance(b, int) and b == 0:
                        dve.wait_ge(select_ready, c.index + 1)
                    for g, part in enumerate(c.gates):
                        dst = block_of(gates_all, b) if part >= 2 else mod[:, r, part, :]
                        nc.vector.tensor_tensor(dst, gate_tmp[:, g, 0, :], gate_tmp[:, g, 1, :], ALU.mult)
                if name == "xhat":
                    dve.wait_ge(rstd_done, n + 1)
                    for k in range(BLK):
                        last = nc.vector.tensor_scalar(h_tok[:, r, k, :], block_of(x_all, b * BLK + k),
                                                       mean_var[:, r2, k, 0:1], rstd[:, r2, k:k + 1],
                                                       ALU.subtract, ALU.mult)
                    last.then_inc(xhat_done, 1)
                    if c.index == 1:
                        dve.wait_ge(xhat_done, n + 1)
                        dve.wait_ge(mod_scale, n - NB + 1)
                        nc.vector.tensor_tensor(h_tok[:, r], h_tok[:, r],
                                                mod[:, r, 1:2, :].to_broadcast([P, BLK, D]), ALU.mult
                                                ).then_inc(h_mul, 1)
                if name == "hn":
                    dve.wait_ge(rrms_done, n - NB + 1)
                    at_least(dve, ht_mm, n - 1)
                    for k in range(BLK):
                        last = nc.vector.tensor_scalar(hn_tok[:, r2, k, :], h_tok[:, r, k, :],
                                                       rrms[:, r2, k:k + 1], None, ALU.mult)
                    last.then_inc(hn_done, 1)
                if name in ("q", "k"):
                    i = 0 if name == "q" else 1
                    m = P if name == "q" else c.kv * c.hd
                    mm_done, rope_done, sum_done = ((q_mm, q_rope, q_sum), (k_mm, k_rope, k_sum))[i]
                    t = 0 if c.hd == 16 else 2
                    dve.wait_ge(mm_done, n + 1)
                    at_least(dve, qd_mm if c.index == 0 and i == 0 else (q_lo, k_lo)[i], n)
                    nc.vector.tensor_tensor(rope_a[0:m, i, :], work[bank_of(c, name)][0:m, 0:S], rope[0:m, t, :], ALU.mult)
                    nc.vector.tensor_tensor(rope_b[0:m, i, :], work[bank_of(c, name)][0:m, S:2 * S], rope[0:m, t + 1, :],
                                            ALU.mult).then_inc(rope_done, 1)
                if name == "qd":
                    dve.wait_ge(q_hi, n + 1)
                    nc.vector.tensor_tensor(split[:, 0, 1, :], work[bank_of(c, name)][:, 0:S], split[:, 0, 0, :].bitcast(F32),
                                            ALU.subtract).then_inc(q_lo, 1)

            def post(c, b, r, name):
                n, r2 = n_of(c, b), r % 2
                if name == "combine":
                    dve.wait_ge(combined, n + 1)
                    at_least(dve, ot_mm, n)
                    rows = BLK * c.heads
                    po = work[bank_of(c, name)][:, 0:rows * (c.hd + 1)].rearrange("p (h e) -> p h e", e=c.hd + 1)
                    nc.vector.reciprocal(recip[:, r2, 0:rows], po[:, :, c.hd]).then_inc(recip_done, 1)
                    dve.wait_ge(recip_done, n + 1)
                    nc.vector.tensor_tensor(o_tok[:, r2].rearrange("p k (h e) -> p (k h) e", e=c.hd),
                                            po[:, :, 0:c.hd],
                                            recip[:, r2, 0:rows].unsqueeze(2).to_broadcast([P, rows, c.hd]),
                                            ALU.mult).then_inc(o_done, 1)
                if name == "y":
                    dve.wait_ge(y_mm, n + 1)
                    y = work[bank_of(c, name)][:, 0:S].rearrange("p (k d) -> p k d", k=BLK)
                    if c.index != 1:
                        if isinstance(b, int):
                            at_least(dve, x_done, NB * (c.index == 2) + b)
                        nc.vector.tensor_tensor(y_tok[:, r2], y, mod[:, r, 0:1, :].to_broadcast([P, BLK, D]),
                                                ALU.mult).then_inc(y_out, 1)
                    else:
                        nc.vector.tensor_tensor(y_tok[:, r2], y, h_tok[:, r], ALU.add).then_inc(y_out, 1)
                        dve.wait_ge(y_out, n + 1)
                        nc.vector.tensor_scalar(res_all[:, bass.ds(b * BLK, BLK), :], y_tok[:, r2], CLIP, -CLIP,
                                                ALU.min, ALU.max).then_inc(res_done, 1)

                if name in ROUTE:
                    m = routed_before(c, b)
                if name == "rstat" and c.index == 2:
                    dve.wait_ge(x_done, NB + b + 1)
                    nc.vector.tensor_copy(var_eps_rt[:, r2, 0:1], eps[:, 0:1])
                    for k in range(BLK):
                        last = nc.vector.bn_stats(stats_rt[:, r2, k, :], block_of(x_all, b * BLK + k))
                    last.then_inc(rt_stats, 1)
                    dve.wait_ge(rt_stats, b + 1)
                    nc.vector.tensor_copy(var_eps_rt[:, r2, 1:2], eps[:, 1:2])
                    for k in range(BLK):
                        last = nc.vector.bn_aggr(mean_var_rt[:, r2, k, :], stats_rt[:, r2, k, :])
                    last.then_inc(rt_mv, 1)
                if name == "rmul":
                    dve.wait_ge(rt_rstd, m + 1)
                    if c.index == 1:
                        for k in range(BLK):
                            last = nc.vector.tensor_scalar(hn_rt[:, r2, k, :], block_of(res_all, b * BLK + k),
                                                           rstd_rt[:, r2, k:k + 1], None, ALU.mult)
                        last.then_inc(rt_mul, 1)
                    else:
                        for k in range(BLK):
                            last = nc.vector.tensor_scalar(hn_rt[:, r2, k, :], block_of(x_all, b * BLK + k),
                                                           mean_var_rt[:, r2, k, 0:1], rstd_rt[:, r2, k:k + 1],
                                                           ALU.subtract, ALU.mult)
                        last.then_inc(rt_xhat, 1)
                        dve.wait_ge(rt_xhat, b + 1)
                        dve.wait_ge(mod_scale, NB + b + 1)
                        nc.vector.tensor_tensor(hn_rt[:, r2], hn_rt[:, r2], mod[:, r, 2:3, :].to_broadcast([P, BLK, D]),
                                                ALU.mult).then_inc(rt_mul, 1)

            def head_max(c, b, r, h):
                n, r2 = n_of(c, b), r % 2
                hn = HEADS_BEFORE[c.index] + b * c.heads + h
                dve.wait_ge(max_mm, hn + 1)
                if c.causal:
                    nc.vector.tensor_copy(wait_cell[:, h % 4:h % 4 + 1], one[:])
                if h == 0:
                    at_least(dve, mt_mm, n - 1)
                    if c.causal and not isinstance(n, int):
                        nc.vector.tensor_copy(wait_cell[:, 4 + r2:5 + r2], one[:])
                if c.causal:
                    for k, (first, last) in enumerate(((0, P), (P, 3 * P))):
                        ins = nc.vector.tensor_tensor_reduce(
                            ps_max[:, h % 2, first:last], ps_max[:, h % 2, first:last],
                            q_masks[:].rearrange("p n m -> p (n m)")[:, first:last], 1.0, LEAST, ALU.add, ALU.max,
                            row_max[:, r2, k, h:h + 1])
                    ins.then_inc(max_done, 1)
                else:
                    src = ps_max[:, h % 2, 0:c.q_cols()].rearrange("p (k s) -> p k s", k=BLK)
                    nc.vector.tensor_reduce(row_max[:, r2, :, h], src, AX_X, ALU.max).then_inc(max_done, 1)

            def maxima(c, b, r, name):
                n, r2 = n_of(c, b), r % 2
                if name == "rows":
                    dve.wait_ge(mt_hi, n + 1)
                    nc.vector.tensor_tensor(max_t[32:32 + c.heads, r2, :], work[bank_of(c, name)][0:c.heads, 0:S],
                                            max_t[0:c.heads, r2, :].bitcast(F32), ALU.subtract).then_inc(mt_out, 1)
                else:
                    j = int(name[5])
                    dve.wait_ge(place_mm, 2 * n + j + 1)
                    half = q_st[:, r, 2 * j:2 * j + 2, :]
                    nc.vector.tensor_tensor(half, half.bitcast(F32), work[bank_of(c, name)].rearrange("p (g s) -> p g s", g=2),
                                            ALU.add).then_inc(place_done, 1)

            def start(c):
                if c.index == 1:
                    nc.vector.memset(q_masks[:, 1, :], 0.0).then_inc(window_open, 1)
                    dve.wait_ge(window_open, 1)
                for name in prep_names(c):
                    prep(c, 0, 0, name)
                for name, heads in opening(c):
                    prep(c, 1, 1, name)
                    for h in heads:
                        head_max(c, 0, 0, h)
                for name in MAXIMA:
                    maxima(c, 0, 0, name)

            def segment(c, b, r):
                for h, (max_heads, before, behind) in enumerate(slots(c, *flags(b))):
                    for k in max_heads:
                        head_max(c, b + 1, (r + 1) % RING, k)
                    walk(c, b, r, post, prep, maxima, before)
                    walk(c, b, r, post, prep, maxima, behind)
                    if beside(c, b, h, "softmax"):
                        dve_softmax(dve, 1)
                    if beside(c, b, h, "rank"):
                        dve_rank(dve, 1)
                    if c.index == 1 and last_entry(b) and h % 4 == 2 and h // 4 < RING - 1:
                        dve_weights(dve, h // 4)

            def finish(c):
                for name in post_names(c):
                    post(c, NB - 1, (NB - 1) % RING, name)
                    if c.index == 1 and name == "rmul":
                        dve_weights(dve, RING - 1)

            run(dve, CFGS[0], start, segment, finish)
            run(dve, CFGS[1], start, segment, finish)
            dve_moe(dve)
            run(dve, CFGS[2], start, segment, finish)
            dve_route1(dve)

        @block.tensor
        def _(pe):
            pe_prologue(pe)

            def prep(c, b, r, name, free):
                n, r2 = n_of(c, b), r % 2
                m = c.kv * c.hd
                bank = work[bank_of(c, name)]
                at_least(pe, *free)
                if name == "mod":
                    pe.wait_ge(c_bcast_done, n + 1)
                    nc.tensor.matmul(bank[:, 0:c.parts * D], c_bcast[:, r2, :],
                                     wmod[:, c.layer, c.mod:c.mod + c.parts * D],
                                     start=True, stop=True).then_inc(mod_mm, 1)
                if name == "ht":
                    if c.index == 1:
                        pe.wait_ge(hn_done, n - NB + 1)
                        src = hn_tok[:, r2]
                    else:
                        pe.wait_ge(xhat_done, n + 1)
                        src = h_tok[:, r]
                    for k in range(BLK):
                        last = nc.tensor.transpose(bank[:, k * P:(k + 1) * P], src[:, k, :], ident)
                    last.then_inc(ht_mm, 1)
                if name == "q":
                    pe.wait_ge(ht_out, n + 1)
                    for i in range(2):
                        last = nc.tensor.matmul(bank[:, i * S:(i + 1) * S], wq[:, c.index, i, :], h_t[:, r2, :],
                                                start=True, stop=True)
                    last.then_inc(q_mm, 1)
                if name == "k":
                    for i in range(2):
                        last = nc.tensor.matmul(bank[0:m, i * S:(i + 1) * S], wk[c.index][:, i, :],
                                                h_t[:, r2, :], start=True, stop=True)
                    last.then_inc(k_mm, 1)
                if name == "qd":
                    pe.wait_ge(q_sum, n + 1)
                    nc.tensor.matmul(bank[:, 0:S], dir_mix[:], rope_a[:, 0, :], start=True, stop=True
                                     ).then_inc(qd_mm, 1)
                if name == "v":
                    for k in range(BLK):
                        last = nc.tensor.matmul(bank[:, k * P:k * P + m], h_t[:, r2, k * P:(k + 1) * P],
                                                wv[c.index], start=True, stop=True)
                    last.then_inc(v_mm, 1)
                if name[:3] == "sel":
                    j = int(name[3])
                    i, rows = j // 2, (P, m)[j // 2]
                    if j % 2 == 0:
                        pe.wait_ge((q_lo, k_lo)[i], n + 1)
                    for g in range(2):
                        for part in range(2):
                            last = nc.tensor.matmul(bank[:, g * S:(g + 1) * S],
                                                    select[0:rows, 2 * i + part, 2 * (j % 2) + g, :],
                                                    split[0:rows, i, part, :], start=(part == 0), stop=(part == 1))
                    last.then_inc(sel_mm, 1)

            def post(c, b, r, name, free):
                n, r2 = n_of(c, b), r % 2
                bank = work[bank_of(c, name)]
                pe.wait_ge(*free)
                if name == "combine":
                    pe.wait_ge(strips_out, pairs_until(c, b))
                    w = 4 * (c.hd + 1)
                    columns = bank[:, 0:BLK * c.heads * (c.hd + 1)].rearrange(
                        "p (k g j i e) -> p k g i j e", k=BLK, g=c.pairs // 4, i=2, e=c.hd + 1)
                    for k in range(BLK):
                        for g in range(c.pairs // 4):
                            for i in range(2):
                                at = i * S + k * P
                                last = nc.tensor.matmul(columns[:, k, g, i], o_strips[:, g, at:at + P],
                                                        strips[:, c.kind, 1:1 + w], start=True, stop=True)
                    last.then_inc(combined, 1)
                if name == "ot":
                    pe.wait_ge(o_done, n + 1)
                    for k in range(BLK):
                        last = nc.tensor.transpose(bank[:, k * P:(k + 1) * P], o_tok[:, r2, k, :], ident)
                    last.then_inc(ot_mm, 1)
                if name == "y":
                    pe.wait_ge(ot_out, n + 1)
                    for k in range(BLK):
                        last = nc.tensor.matmul(bank[:, k * P:(k + 1) * P], o_t[:, r2, k * P:(k + 1) * P],
                                                wo[:, c.index, :], start=True, stop=True)
                    last.then_inc(y_mm, 1)
                if name == "rht":
                    if c.index == 1:
                        pe.wait_ge(rt_mul, routed_before(c, b) + 1)
                    else:
                        pe.wait_ge(rt_h, b + 1)
                    for k in range(BLK):
                        last = nc.tensor.transpose(bank[:, k * P:(k + 1) * P], hn_rt[:, r2, k, :], ident)
                    last.then_inc(rt_ht_mm, 1)
                if name == "rlog":
                    pe.wait_ge(rt_ht_out, routed_before(c, b) + 1)
                    for k in range(BLK):
                        last = nc.tensor.matmul(bank[:, k * 8:(k + 1) * 8], ht_rt[:, r2, k * P:(k + 1) * P],
                                                wr[:, c.layer, :], start=True, stop=True)
                    last.then_inc(rt_logit_mm, 1)

            def max_scores(c, b, r, h):
                n = n_of(c, b)
                hn = HEADS_BEFORE[c.index] + b * c.heads + h
                g, base = h // c.per_group, (h % c.per_group) * c.strip
                rows = slice(base, base + c.krows)
                if h == 0:
                    pe.wait_ge(sel_out, 4 * n + 4)
                at_least(pe, max_done, hn - 1)
                bank = ps_max[:, h % 2, :]
                if c.causal:
                    nc.tensor.matmul(bank[:, 0:P], q_st[rows, r, g, 0:P], k_st[rows, r, g, 0:P], start=True, stop=True)
                    nc.tensor.matmul(bank[:, P:3 * P], q_st[rows, r, g, P:S], k_st[rows, r, g, :], start=True,
                                     stop=True).then_inc(max_mm, 1)
                else:
                    for k in range(BLK):
                        last = nc.tensor.matmul(bank[:, k * S:(k + 1) * S], q_st[rows, r, g, k * P:(k + 1) * P],
                                                k_st[rows, r, g, :], start=True, stop=True)
                    last.then_inc(max_mm, 1)

            def exp_scores(c, b, r, h):
                n = n_of(c, b)
                hn = HEADS_BEFORE[c.index] + b * c.heads + h
                g, base = h // c.per_group, (h % c.per_group) * c.strip
                rows = slice(base, base + c.krows + 2)
                if h == 0:
                    pe.wait_ge(place_done, 2 * n + 2)
                if h >= 3:
                    pe.wait_ge(exp_done, hn - 2)
                elif isinstance(b, int) and b == 0:
                    at_least(pe, exp_done, HEADS_BEFORE[c.index])
                else:
                    at_least(pe, exp_done, hn + 1 - (h + c.heads - max(k for k in range(c.heads) if k % 3 == h)))
                bank = ps_exp[:, h % 3, :]
                second = slice(P, S) if c.causal else slice(0, S)
                w = second.stop - second.start
                if c.causal:
                    nc.tensor.matmul(bank[:, 0:P], ident_bf[:], masks[:, 0, :], start=True, stop=False,
                                     skip_group_check=True)
                    nc.tensor.matmul(bank[:, S:S + P], ident_bf[:], masks[:, 0, :], start=False, stop=False,
                                     skip_group_check=True)
                    if c.window:
                        nc.tensor.matmul(bank[:, P:S], ident_bf[:], masks[:, 1, :], start=False, stop=False,
                                         skip_group_check=True)
                nc.tensor.matmul(bank[:, 0:S], k_st[rows, r, g, 0:P], q_st[rows, r, g, :], start=not c.causal,
                                 stop=True, skip_group_check=True)
                last = nc.tensor.matmul(bank[:, S:S + w], k_st[rows, r, g, P:S], q_st[rows, r, g, second],
                                        start=False, stop=True, skip_group_check=True)
                last.then_inc(exp_mm, 1)

            def values(c, b, r, h):
                hn = HEADS_BEFORE[c.index] + b * c.heads + h
                pe.wait_ge(exp_done, hn + 1)
                if h % 2 == 0:
                    at_least(pe, strips_out, PAIRS_BEFORE[c.index] + b * c.pairs + h // 2)
                if h == 0:
                    pe.wait_ge(v_out, n_of(c, b) + 1)
                kv = h // (c.heads // c.kv)
                for kb in range(BLK):
                    first = P if c.causal and kb == 1 else 0
                    last = nc.tensor.matmul(ps_out[0:c.hd + 1, (h % 2) * S + first:(h % 2 + 1) * S],
                                            v_tok[c.index][:, r, kb, kv, :],
                                            probs[:, h % 4, kb * S:kb * S + S - first],
                                            start=(kb == 0), stop=(kb == 1), skip_group_check=True)
                last.then_inc(values_mm, 1)

            def maxima(c, b, r, name, free):
                n, r2 = n_of(c, b), r % 2
                bank = work[bank_of(c, name)]
                pe.wait_ge(*free)
                if name == "rows":
                    pe.wait_ge(max_done, HEADS_BEFORE[c.index] + (b + 1) * c.heads)
                    for k in range(BLK):
                        last = nc.tensor.transpose(bank[0:c.heads, k * P:(k + 1) * P],
                                                   row_max[:, r2, k, 0:c.heads], ident)
                    last.then_inc(mt_mm, 1)
                else:
                    j = int(name[5])
                    pe.wait_ge(mt_out, n + 1)
                    for g in range(2):
                        last = nc.tensor.matmul(bank[:, g * S:(g + 1) * S], max_place[:, c.kind, 2 * j + g, :],
                                                max_t[:, r2, :], start=True, stop=True)
                    last.then_inc(place_mm, 1)

            readers = {"mod": (mod_out, 1, 1), "ht": (ht_out, 1, 1), "q": (q_rope, 1, 1), "k": (k_rope, 1, 1),
                       "v": (v_out, 1, 1), "combine": (o_done, 1, 1), "ot": (ot_out, 1, 1), "y": (y_out, 1, 1),
                       "rows": (mt_out, 1, 1), "place0": (place_done, 2, 1), "place1": (place_done, 2, 2)}

            def reader_of(c, b, name):
                if name[:3] == "sel":
                    semaphore, count, which = sel_out, 4, int(name[3]) + 1
                elif name == "qd":
                    semaphore, count, which = q_lo, 1, 1
                elif name in ROUTE:
                    return {"rht": rt_ht_out, "rlog": rt_logit}[name], routed_before(c, b) + 1
                else:
                    semaphore, count, which = readers[name]
                return semaphore, count * n_of(c, b) + which

            def tracked(free):
                def step(f):
                    def g(c, b, r, name):
                        if name in NO_PE:
                            return
                        f(c, b, r, name, free[bank_of(c, name)])
                        free[bank_of(c, name)] = reader_of(c, b, name)
                    return g
                return step(post), step(prep), step(maxima)

            def start(c):
                if c.index == 2:
                    free = {bank: (act_done, TOKENS // 512 * UNITS) for bank in range(2)}
                else:
                    free = {0: (y_out, c.first), 1: (o_done, c.first)}
                post_step, prep_step, maxima_step = tracked(free)
                pe.wait_ge(rotated, c.index + 1)
                pe.wait_ge(select_ready, c.index + 1)
                if c.index > 0:
                    pe.wait_ge(loads_late, 16 * len(late_loads))
                    pe.wait_ge(ones_ready, c.index + 3)
                for name in prep_names(c):
                    prep_step(c, 0, 0, name)
                for name, heads in opening(c):
                    prep_step(c, 1, 1, name)
                    for h in heads:
                        max_scores(c, 0, 0, h)
                for name in MAXIMA:
                    maxima_step(c, 0, 0, name)

            def segment(c, b, r):
                n = n_of(c, b)
                steps = tracked({bank_of(c, "place0"): (place_done, 2 * n + 1),
                                 bank_of(c, "place1"): (place_done, 2 * n + 2)})
                for h, (max_heads, before, behind) in enumerate(slots(c, *flags(b))):
                    for k in max_heads:
                        max_scores(c, b + 1, (r + 1) % RING, k)
                    walk(c, b, r, *steps, before)
                    exp_scores(c, b, r, h)
                    if h > 1:
                        values(c, b, r, h - 2)
                    elif flags(b)[0]:
                        values(c, b - 1, (r - 1) % RING, c.heads - 2 + h)
                    walk(c, b, r, *steps, behind)
                    if beside(c, b, h, "rank_mm"):
                        pe_rank(pe, 1)

            def finish(c):
                for h in (c.heads - 2, c.heads - 1):
                    values(c, NB - 1, (NB - 1) % RING, h)
                names = [n for n in post_names(c) if n not in NO_PE]
                post_step, _, _ = tracked({bank_of(c, n): reader_of(c, NB - 2, n) for n in names})
                for name in names:
                    post_step(c, NB - 1, (NB - 1) % RING, name)

            run(pe, CFGS[0], start, segment, finish)
            run(pe, CFGS[1], start, segment, finish)
            pe_moe(pe)
            run(pe, CFGS[2], start, segment, finish)
            pe_route1(pe)


_SHAPES = {"squares": square_constants, "rope": rope_tables, "experts": expert_constants,
           "select": select_constants, "max_place": max_place_constant, "strips": strip_constants}
_INS = ["L0_attn_x", "L0_attn_Wq", "L0_attn_Wk", "L0_attn_Wv", "L0_attn_Wo", "L0_attn_head_scales",
        "L0_attn_head_dirs", "L0_ffn_ln1_w", "L0_ffn_ln2_w", "L0_ffn_Wq", "L0_ffn_Wk", "L0_ffn_Wv", "L0_ffn_Wo",
        "L0_ffn_Wr", "L0_ffn_Wg", "L0_ffn_Wu", "L0_ffn_Wd", "L0_c", "L0_wmod", "L1_ffn_Wr", "L1_ffn_W1", "L1_ffn_W2",
        "L1_c", "L1_wmod"]
_TRANSPOSED = ["L1_attn_Wq", "L1_attn_Wk", "L1_attn_Wv", "L1_attn_Wo"]


def kernel(**inputs):
    import numpy as _np
    import concourse.bacc as _bacc
    from concourse import mybir as _mybir
    from concourse.bass_utils import run_bass_kernel_spmd as _run

    nc = _bacc.Bacc("TRN2", target_bir_lowering=False, num_devices=1)
    arrays = {name: _np.ascontiguousarray(inputs[name]) for name in _INS}
    arrays.update({name + "T": _np.ascontiguousarray(_np.asarray(inputs[name]).T) for name in _TRANSPOSED})
    arrays.update({name: make() for name, make in _SHAPES.items()})
    aps = {name: nc.dram_tensor(f"in_{name}", v.shape, _mybir.dt.from_np(v.dtype), kind="ExternalInput").ap()
           for name, v in arrays.items()}
    out = nc.dram_tensor("out_x", (NB, S, D), F32, kind="ExternalOutput").ap()
    adaln_two_layers(nc, aps, out)
    r = _run(nc, [{f"in_{name}": v for name, v in arrays.items()}], core_ids=[0])
    return r.results[0]["out_x"]
```
